# Optimizing a Trainium2 kernel written in Bass

```python
import numpy as np
import jax
import jax.numpy as jnp

def _softmax(x, axis=-1):
    return jax.nn.softmax(x, axis=axis)

def _gelu(x):
    return jax.nn.gelu(x, approximate=True)

def _silu(x):
    return jax.nn.silu(x)

def _sigmoid(x):
    return jax.nn.sigmoid(x)

def _layernorm(x, axis=-1, eps=1e-05):
    m = jnp.mean(x, axis=axis, keepdims=True)
    v = jnp.var(x, axis=axis, keepdims=True)
    return (x - m) / jnp.sqrt(v + eps)

def _scatter_add(tgt, idx, src, axis=0):
    return tgt.at[idx].add(src)

def _segment_sum(src, seg, n):
    return jax.ops.segment_sum(src, seg, n)
kernel_name = 'mk_seq_postln_d1_jaxref_r8_02c4b4'

def setup_inputs(seed: int=0):
    np.random.seed(seed)
    _w = jnp.asarray

    def _L0_attn_setup():
        import jax, jax.numpy as jnp
        import numpy as np
        DIM = 128
        HEADS = 16
        DIM_HEAD = DIM // HEADS
        LATENT = DIM // 4
        SCALE = DIM_HEAD ** (-0.5)
        key = jax.random.key(seed)
        ks = jax.random.split(key, 8)
        B, S = (2, 256)
        init = lambda k, shape, fan_in: jax.random.normal(k, shape, jnp.float32) * fan_in ** (-0.5)
        return {'x': jax.random.normal(ks[0], (B, S, DIM), jnp.float32), 'Wq': init(ks[1], (DIM, DIM), DIM), 'bq': jnp.zeros((DIM,), jnp.float32), 'Wl': init(ks[2], (DIM, LATENT), DIM), 'bl': jnp.zeros((LATENT,), jnp.float32), 'Wk': init(ks[3], (LATENT, DIM), LATENT), 'bk': jnp.zeros((DIM,), jnp.float32), 'Wv': init(ks[4], (LATENT, DIM), LATENT), 'bv': jnp.zeros((DIM,), jnp.float32), 'Wo': init(ks[5], (DIM, DIM), DIM), 'bo': jnp.zeros((DIM,), jnp.float32)}
    _L0_attn_in = _L0_attn_setup()

    def _L0_ffn_setup():
        import jax, jax.numpy as jnp
        import numpy as np
        B, L, H, E, FF, C = (4, 256, 128, 8, 512, 2)
        key = jax.random.key(seed)
        ks = jax.random.split(key, 6)
        s = 0.02
        return {'x': jax.random.normal(ks[0], (B, L, H), dtype=jnp.float32), 'Wg': jax.random.normal(ks[1], (H, E), dtype=jnp.float32) * s, 'W1': jax.random.normal(ks[2], (E, H, FF), dtype=jnp.float32) * s, 'b1': jnp.zeros((E, FF), dtype=jnp.float32), 'W2': jax.random.normal(ks[3], (E, FF, H), dtype=jnp.float32) * s, 'b2': jnp.zeros((E, H), dtype=jnp.float32)}
    _L0_ffn_in = _L0_ffn_setup()
    _d = {'L0_attn_x': _L0_attn_in['x'], 'L0_attn_Wq': _L0_attn_in['Wq'], 'L0_attn_bq': _L0_attn_in['bq'], 'L0_attn_Wl': _L0_attn_in['Wl'], 'L0_attn_bl': _L0_attn_in['bl'], 'L0_attn_Wk': _L0_attn_in['Wk'], 'L0_attn_bk': _L0_attn_in['bk'], 'L0_attn_Wv': _L0_attn_in['Wv'], 'L0_attn_bv': _L0_attn_in['bv'], 'L0_attn_Wo': _L0_attn_in['Wo'], 'L0_attn_bo': _L0_attn_in['bo'], 'L0_ffn_Wg': _L0_ffn_in['Wg'], 'L0_ffn_W1': _L0_ffn_in['W1'], 'L0_ffn_b1': _L0_ffn_in['b1'], 'L0_ffn_W2': _L0_ffn_in['W2'], 'L0_ffn_b2': _L0_ffn_in['b2']}
    _x0 = _d['L0_attn_x']
    _d['L0_attn_x'] = jax.random.normal(jax.random.fold_in(jax.random.key(seed), 1), (16, 256, 128), dtype=_x0.dtype)
    del _x0
    return _d

def reference(L0_attn_x, L0_attn_Wq, L0_attn_bq, L0_attn_Wl, L0_attn_bl, L0_attn_Wk, L0_attn_bk, L0_attn_Wv, L0_attn_bv, L0_attn_Wo, L0_attn_bo, L0_ffn_Wg, L0_ffn_W1, L0_ffn_b1, L0_ffn_W2, L0_ffn_b2):

    def _L0_attn_ref(x, Wq, bq, Wl, bl, Wk, bk, Wv, bv, Wo, bo):
        import jax, jax.numpy as jnp
        import numpy as np
        DIM = 128
        HEADS = 16
        DIM_HEAD = DIM // HEADS
        LATENT = DIM // 4
        SCALE = DIM_HEAD ** (-0.5)
        B, S, D = x.shape
        H, Dh = (HEADS, DIM_HEAD)
        q = (x @ Wq + bq).reshape(B, S, H, Dh)
        latent = x @ Wl + bl
        k = (latent @ Wk + bk).reshape(B, S, H, Dh)
        v = (latent @ Wv + bv).reshape(B, S, H, Dh)
        scores = jnp.einsum('bihd,bjhd->bhij', q, k) * SCALE
        attn = jax.nn.softmax(scores, axis=-1)
        out = jnp.einsum('bhij,bjhd->bihd', attn, v).reshape(B, S, D)
        out = out @ Wo + bo
        return out

    def _L0_ffn_ref(x, Wg, W1, b1, W2, b2):
        import jax, jax.numpy as jnp
        import numpy as np
        B, L, H, E, FF, C = (4, 256, 128, 8, 512, 2)
        b, l, h = x.shape
        e = Wg.shape[1]
        n = b * l
        k = min(max(int(n * C / e), 1), n)
        xt = x.reshape(n, h)
        S = jax.nn.sigmoid(xt @ Wg).T
        G, I = jax.lax.top_k(S, k)
        ex = xt[I]
        hid = jax.nn.gelu(jnp.einsum('ekh,ehf->ekf', ex, W1) + b1[:, None, :], approximate=False)
        out = (jnp.einsum('ekf,efh->ekh', hid, W2) + b2[:, None, :]) * G[..., None]
        new_x = jnp.zeros_like(xt).at[I.reshape(-1)].add(out.reshape(-1, h))
        return new_x.reshape(b, l, h)
    x = L0_attn_x
    x = _layernorm(x + _L0_attn_ref(x, L0_attn_Wq, L0_attn_bq, L0_attn_Wl, L0_attn_bl, L0_attn_Wk, L0_attn_bk, L0_attn_Wv, L0_attn_bv, L0_attn_Wo, L0_attn_bo), axis=-1)
    x = _layernorm(x + _L0_ffn_ref(x, L0_ffn_Wg, L0_ffn_W1, L0_ffn_b1, L0_ffn_W2, L0_ffn_b2), axis=-1)
    return x

_drawn_inputs = setup_inputs


def setup_inputs(seed=0):
    import zlib

    import numpy as np

    out = dict(_drawn_inputs(seed))
    spreads = {'L0_attn_bq': (0.0, 0.436),
     'L0_attn_bl': (0.0, 0.1),
     'L0_attn_bk': (0.0, 0.8),
     'L0_attn_bv': (0.0, 0.1),
     'L0_attn_bo': (0.0, 0.1),
     'L0_ffn_b1': (0.0, 0.427),
     'L0_ffn_b2': (0.0, 0.1)}
    factors = {}
    for name, (base, spread) in spreads.items():
        noise = np.random.default_rng([zlib.crc32(name.encode()), seed]).standard_normal(out[name].shape)
        drawn = base * np.exp(spread * noise) if base else spread * noise
        out[name] = jnp.asarray(drawn.astype(out[name].dtype))
    for name, factor in factors.items():
        out[name] = (out[name] * factor).astype(out[name].dtype)
    return out
```

```python
from contextlib import ExitStack

import concourse.bass as bass
from concourse import mybir

P = 128
ALU = mybir.AluOpType
ACT = mybir.ActivationFunctionType
AX = mybir.AxisListType.X
F32 = mybir.dt.float32
F32R = mybir.dt.float32r
BF16 = mybir.dt.bfloat16
F16 = mybir.dt.float16
I32 = mybir.dt.int32
U32 = mybir.dt.uint32

BATCHES, SEQ, D = 16, 256, 128
HEADS, DH, LATENT = 16, 8, 32
EXPERTS, FF = 8, 512
TOKENS = BATCHES * SEQ
CAPACITY = TOKENS * 2 // EXPERTS
TILES = TOKENS // P
PAIRS = BATCHES // 2
NPART = TILES * EXPERTS
SCALE = DH ** -0.5
EPS = 1e-5
NR = NG = 4
TERMS = 3
GATED = D + EXPERTS
CHUNKS = CAPACITY // P
SEARCH_STEPS = 12
FBLK = FF // P
ID_BASE = TOKENS // 2

PREP_AT = {0: "xT", 2: "latent", 3: "k", 4: "q", 6: "v"}
MAX_AT = {1: "max3", 5: "max0", 9: "max1", 13: "max2"}
TAIL_AT = {7: "norm0", 8: "norm1", 10: "oT", 11: "y", 14: "xcT", 15: "logits"}


def half_jobs(prep, this, nxt, tail):
    jobs = {}
    if prep:
        jobs.update(PREP_AT)
    jobs.update({s: j for s, j in MAX_AT.items() if (this if j == "max3" else nxt)})
    if tail:
        jobs.update(TAIL_AT)
    return sorted(jobs.items())


PROLOGUE = [j for j in PREP_AT.values()] + ["max0", "max1", "max2"]
FIRST = [half_jobs(True, True, True, False), half_jobs(False, True, True, True)]
MIDDLE = [half_jobs(True, True, True, True), half_jobs(False, True, True, True)]
LAST = [half_jobs(False, True, True, True), half_jobs(False, True, False, True)]
N_FIRST, N_MIDDLE, N_LAST = (sum(len(h) for h in b) for b in (FIRST, MIDDLE, LAST))
BASE_FIRST = len(PROLOGUE)
BASE_MIDDLE = BASE_FIRST + N_FIRST
BASE_LAST = BASE_MIDDLE + (PAIRS - 2) * N_MIDDLE
BASE_END = BASE_LAST + N_LAST


class Half:

    def __init__(self, n, side, first=False, last=False):
        self.n, self.side, self.b = n, side, 2 * n + side
        self.prep = side == 0 and not last
        self.nxt = not (last and side == 1)
        self.prev = not (first and side == 0)
        self.ahead = not last
        body = FIRST if first else LAST if last else MIDDLE
        base = BASE_FIRST if first else BASE_LAST if last else BASE_MIDDLE + (n - 1) * N_MIDDLE
        local = side * len(body[0])
        self.pair_base, self.pair_jobs = base, body[0]
        self.jobs = {}
        for i, (step, job) in enumerate(body[side]):
            self.jobs[step] = (job, base + local + i)
        self.after = (side + 1) % 2
        self.after_pair = n + side

    def number(self, job):
        return next(i for j, i in self.jobs.values() if j == job)

    def number_in_side_0(self, job):
        return self.pair_base + [j for _, j in self.pair_jobs].index(job)


def passed(engine, waits):
    engine.sem_inc(waits, 1)


def run_pairs(engine, body):
    for side in range(2):
        body(Half(0, side, first=True))
    with engine.Fori(1, PAIRS - 1) as n:
        for side in range(2):
            body(Half(n, side))
    for side in range(2):
        body(Half(PAIRS - 1, side, last=True))


def post_ln_layer(nc, x, Wq, bq, Wl, bl, Wk, bk, Wv, bv, Wo, bo, Wg, W1, b1, W2, b2, out):
    with ExitStack() as ctx:
        def sb(name, shape, dt=F32):
            return ctx.enter_context(nc.sbuf_tensor(name, shape, dt))

        def psum(name, shape):
            return ctx.enter_context(nc.psum_tensor(name, shape, F32))

        def sem(name):
            return ctx.enter_context(nc.semaphore(name))

        q_split = nc.dram_tensor("q_split", [BATCHES, NR, TERMS, DH, NG, SEQ], F32, kind="Internal").ap()
        k_split = nc.dram_tensor("k_split", [BATCHES, NR, TERMS, DH, NG, SEQ], F32, kind="Internal").ap()
        x1_table = nc.dram_tensor("x1_table", [TOKENS, GATED], F32, kind="Internal").ap()
        summed = nc.dram_tensor("summed", [TOKENS, D], F32, kind="Internal").ap()
        token_list = nc.dram_tensor("token_list", [EXPERTS, CAPACITY], U32, kind="Internal").ap()

        ps_first = psum("ps_first", [P, 4, 512])
        ps_second = psum("ps_second", [P, 2, 512])
        ps_pv = psum("ps_pv", [P, 2, SEQ])
        ps_job = psum("ps_job", [P, 512])

        ident = sb("ident", [P, P])
        ones = sb("ones", [P, P])
        eps_col = sb("eps_col", [P, 1])
        wq_nat, wq = sb("wq_nat", [P, P]), sb("wq", [P, P])
        wk_nat, wk = sb("wk_nat", [LATENT, P]), sb("wk", [LATENT, P])
        wl, wv = sb("wl", [P, LATENT]), sb("wv", [LATENT, P])
        wo, wg = sb("wo", [P, P]), sb("wg", [P, EXPERTS])
        bias_rows = sb("bias_rows", [1, 4, P])
        bias_perm = sb("bias_perm", [1, 2, P])
        bl_col = sb("bl_col", [LATENT, 1])
        bq_col, bk_col = sb("bq_col", [P, 1]), sb("bk_col", [P, 1])
        b1_rows, b1_cols = sb("b1_rows", [EXPERTS * FBLK, P]), sb("b1_cols", [P, EXPERTS * FBLK])
        b2_row, b2_all = sb("b2_row", [1, EXPERTS * D]), sb("b2_all", [P, EXPERTS, D])

        rows = sb("rows", [P, TILES, GATED])
        x_pair, xT = sb("x_pair", [P, 4, D]), sb("xT", [P, 2 * SEQ])
        latT = sb("latT", [LATENT, 2 * SEQ])
        kq_full = sb("kq_full", [P, 2, 2 * SEQ])
        k_full, q_full = kq_full[:, 0], kq_full[:, 1]
        k_hi, k_lo = sb("k_hi", [P, 2 * SEQ], F32R), sb("k_lo", [P, 2 * SEQ], F32R)
        q_hi, q_lo = sb("q_hi", [P, 2 * SEQ], F32R), sb("q_lo", [P, 2 * SEQ], F32R)
        v_stage = sb("v_stage", [P, 4, D])
        v_ones = sb("v_ones", [P, 2, 2, HEADS, 32])
        q_stack = sb("q_stack", [P, 2, NR, NG, SEQ], F32R)
        k_first = sb("k_first", [P, 2, NG, SEQ], F32R)
        k_second = sb("k_second", [P, 2, NG, SEQ], F32R)
        row_max = sb("row_max", [P, NR, 2 * NG])
        shift_t = sb("shift_t", [2 * NG, NR, P], F32R)
        probs = sb("probs", [P, 8, 2 * SEQ])
        oT_raw = sb("oT_raw", [P, NR, SEQ])
        den = sb("den", [P, HEADS])
        o_nat, oT = sb("o_nat", [P, 2, D]), sb("oT", [P, SEQ])
        resid, xc = sb("resid", [P, 2, D]), sb("xc", [P, 2, D])
        stats, mean_var = sb("stats", [P, 2, 6]), sb("mean_var", [P, 2, 2])
        xcT = sb("xcT", [P, SEQ])
        xc_all = sb("xc_all", [P, TILES, D])
        var_all, rstd = sb("var_all", [P, TILES]), sb("rstd", [P, TILES])
        logits = sb("logits", [P, TILES, EXPERTS])

        weights_in, consts_set, perm_done = sem("weights_in"), sem("consts_set"), sem("perm_done")
        bias_made, bias_out = sem("bias_made"), sem("bias_out")
        x_head_in, x_rest_in, x_copied = sem("x_head_in"), sem("x_rest_in"), sem("x_copied")
        job_full, job_free = sem("job_full"), sem("job_free")
        hi_done, k_cut, q_cut = sem("hi_done"), sem("k_cut"), sem("q_cut")
        split_stored = sem("split_stored")
        q_in = [sem(f"q_in{r}") for r in range(NR)]
        k_first_in = [sem(f"k_first_in{s}") for s in range(2)]
        k_second_in = [sem(f"k_second_in{s}") for s in range(2)]
        shift_in = [sem(f"shift_in{r}") for r in range(NR)]
        first_full, first_free = sem("first_full"), sem("first_free")
        second_full, exp_done = sem("second_full"), sem("exp_done")
        v_ready, pv_done, o_copied = sem("v_ready"), sem("pv_done"), sem("o_copied")
        den_done, stats_done, mv_done = sem("den_done"), sem("stats_done"), sem("mv_done")
        pool_waits, act_waits, dve_waits = sem("pool_waits"), sem("act_waits"), sem("dve_waits")
        shift_ones, indices_set, own, own_loop = sem("shift_ones"), sem("indices_set"), sem("own"), sem("own_loop")
        var_kept, centred, xc_kept = sem("var_kept"), sem("centred"), sem("xc_kept")

        lg = sb("lg", [P, TILES, EXPERTS])
        lgT = sb("lgT", [P, 2 * P])
        abs_col, abs_row, bound = sb("abs_col", [P, 1]), sb("abs_row", [1, 1]), sb("bound", [1, 1])
        steps3, lo, thr = sb("steps3", [P, 3]), sb("lo", [P, 1]), sb("thr", [P, 3])
        one23 = sb("one23", [P, 3])
        counts = sb("counts", [P, 3])
        above, n_above = sb("above", [P, 3]), sb("n_above", [P, 1])
        lo_hi, bounds = sb("lo_hi", [P, 2, EXPERTS]), sb("bounds", [P, 2, EXPERTS])
        hi_col = sb("hi_col", [P, 1])
        part_i, col_i = sb("part_i", [P, 2], I32), sb("col_i", [P, 2, P], I32)
        part_f = sb("part_f", [P, 2])
        same_e, same_eb = sb("same_e", [P, P]), sb("same_eb", [P, P], BF16)
        before_b = sb("before_b", [P, P], BF16)
        upper_b, ones_b = sb("upper_b", [P, P], BF16), sb("ones_b", [P, P], BF16)
        gt, ge = sb("gt", [P, TILES, EXPERTS], BF16), sb("ge", [P, TILES, EXPERTS], BF16)
        tie, sel = sb("tie", [P, TILES, EXPERTS], BF16), sb("sel", [P, TILES, EXPERTS], BF16)
        gt_sum, gt_all = sb("gt_sum", [P, EXPERTS], BF16), sb("gt_all", [P, EXPERTS])
        tile_sum = sb("tile_sum", [P, 2, 2], BF16)
        rank = sb("rank", [P, TILES, EXPERTS])
        off_slot, slot = sb("off_slot", [P, NPART]), sb("slot", [P, NPART], I32)
        slot_a, slot_b = sb("slot_a", [P, NPART], I32), sb("slot_b", [P, NPART], I32)
        iota32_i, iota32 = sb("iota32_i", [P, 32], I32), sb("iota32", [P, 32])
        token_i, token_id = sb("token_i", [P, TILES], I32), sb("token_id", [P, TILES])
        hot_a = probs[:].bitcast(F16).rearrange("p a b -> p (a b)").rearrange("p (t e s) -> p t e s", t=TILES, e=EXPERTS)
        hT = sb("hT", [P, 2, FBLK, 512])
        hot_b = hT[:].bitcast(F16).rearrange("p a b c -> p (a b c)").rearrange("p (t e s) -> p t e s", t=TILES, e=EXPERTS)
        picked, index = sb("picked", [P, 2, 32], U32), sb("index", [P, EXPERTS, CHUNKS], U32)
        hits = hT[:, 0, 0:3, 0:P].bitcast(BF16)
        index_now = sb("index_now", [P, 2, CHUNKS], U32)
        w1_buf, w2_buf = sb("w1_buf", [P, 2, FF]), sb("w2_buf", [P, 2, FBLK, D])
        taken = sb("taken", [P, 2, CHUNKS, GATED])
        takenT = kq_full
        y_sum = sb("y_sum", [P, 2, 4, D])
        y_out = v_ones[:].rearrange("p s j h c -> p (s j h c)").rearrange("p (s k d) -> p s k d", s=2, k=CHUNKS)
        f_stats, f_mv = sb("f_stats", [P, TILES, 6]), sb("f_mv", [P, TILES, 2])
        f_sd, f_rstd = sb("f_sd", [P, TILES]), sb("f_rstd", [P, TILES])

        var_rooted, rstd_made, lg_made = sem("var_rooted"), sem("rstd_made"), sem("lg_made")
        pe_a, dve_a = sem("pe_a"), sem("dve_a")
        thr_made, counted, totalled, found = sem("thr_made"), sem("counted"), sem("totalled"), sem("found")
        lo_made, stepped = sem("lo_made"), sem("stepped")
        hot_a_made, hot_b_made, hot_id_made = sem("hot_a_made"), sem("hot_b_made"), sem("hot_id_made")
        rows_scaled, gates_made, table_out = sem("rows_scaled"), sem("gates_made"), sem("table_out")
        sum_out, list_out, index_in = sem("sum_out"), sem("list_out"), sem("index_in")
        w_in = [sem(f"w_in{i}") for i in range(2)]
        index_set = sem("index_set")
        taken_in = [sem(f"taken_in{i}") for i in range(4)]
        turned, turned_copied = sem("turned"), sem("turned_copied")
        up_full, gelu_done = sem("up_full"), sem("gelu_done")
        down_full, y_summed, y_made = sem("down_full"), sem("y_summed"), sem("y_made")
        added = [sem(f"added{i}") for i in range(2)]
        f_in = [sem(f"f_in{i}") for i in range(4)]
        f_statted, f_averaged, f_rooted = sem("f_statted"), sem("f_averaged"), sem("f_rooted")
        f_inverted, f_done, f_out = sem("f_inverted"), sem("f_done"), sem("f_out")

        block = ctx.enter_context(nc.Block())

        x_tiled = x.rearrange("b (s p) d -> p (b s) d", p=P)
        summed_rows = summed.rearrange("(p t) d -> p t d", p=P)
        out_rows = out.rearrange("b s d -> (b s) d").rearrange("(p t) d -> p t d", p=P)
        N_WEIGHTS = 12

        @block.sync
        def _(sp):
            loads = [(wq_nat[:], Wq), (wl[:], Wl), (wk_nat[:], Wk), (wv[:], Wv), (wo[:], Wo), (wg[:], Wg),
                     (bias_rows[:, 0], bq.unsqueeze(0)), (bias_rows[:, 1], bk.unsqueeze(0)),
                     (bias_rows[:, 2], bv.unsqueeze(0)), (bias_rows[:, 3], bo.unsqueeze(0)),
                     (bl_col[:], bl.unsqueeze(1)),
                     (b1_rows[:], b1.rearrange("e (c f) -> (e c) f", f=P))]
            assert len(loads) == N_WEIGHTS
            for dst, src in loads:
                sp.dma_start(dst, src).then_inc(weights_in, 16)

            def store_split(pair):
                for cut, parts, dram in ((k_cut, (k_hi, k_lo, k_hi), k_split), (q_cut, (q_hi, q_hi, q_lo), q_split)):
                    sp.wait_ge(cut, pair + 1)
                    for side in range(2):
                        for t, part in enumerate(parts):
                            sp.dma_start(dram[2 * pair + side, :, t].rearrange("r d g i -> r (d g) i"),
                                         part[:, side * SEQ:(side + 1) * SEQ].bitcast(F32)).then_inc(split_stored, 16)

            def load_k(batch, side, buf, done):
                for r in range(NR):
                    sp.dma_start(buf[32 * r + DH:32 * r + 32, side].rearrange("p g i -> p (g i)").bitcast(F32),
                                 k_split[batch, r].rearrange("t d g i -> (t d) (g i)")).then_inc(done[side], 16)

            def load_q(batch, side, r):
                sp.dma_start(q_stack[32 * r + DH:32 * r + 32, side, r].rearrange("p g i -> p (g i)").bitcast(F32),
                             q_split[batch, r].rearrange("t d g i -> (t d) (g i)")).then_inc(q_in[r], 16)

            def load_shift(number, side, r):
                sp.wait_ge(job_free, number + 1)
                sp.dma_start(q_stack[32 * r:32 * r + 1, side, r].rearrange("p g i -> p (g i)").bitcast(F32),
                             shift_t[:, r, :].bitcast(F32)).then_inc(shift_in[r], 16)

            STORES = 16 * 2 * 2 * TERMS
            sp.wait_ge(shift_ones, NR)
            sp.wait_ge(consts_set, 6)
            store_split(0)
            sp.wait_ge(split_stored, STORES)
            for side in range(2):
                load_k(side, side, k_first, k_first_in)
                for r in range(NR):
                    if side:
                        sp.wait_ge(q_in[r], 16)
                    load_q(side, side, r)
                load_k(side, side, k_second, k_second_in)
            for r in range(3):
                load_shift(PROLOGUE.index(f"max{r}"), 0, r)

            def half(h):
                load_shift(h.number("max3"), h.side, 3)
                if h.prep:
                    store_split(h.n + 1)
                if h.nxt:
                    load_shift(h.number("max0"), h.after, 0)
                if h.ahead:
                    if h.prep:
                        sp.wait_ge(split_stored, STORES * (h.n + 2))
                    sp.wait_ge(first_full, 8 * (h.b + 1))
                    load_k(h.b + 2, h.side, k_first, k_first_in)
                for r in range(NR):
                    if h.ahead:
                        sp.wait_ge(second_full, 16 * h.b + 4 * r + 4)
                        load_q(h.b + 2, h.side, r)
                    if r < 2 and h.nxt:
                        load_shift(h.number(f"max{r + 1}"), h.after, r + 1)
                if h.ahead:
                    load_k(h.b + 2, h.side, k_second, k_second_in)

            def load_expert(e, side):
                sp.dma_start(w1_buf[:, side], W1[e]).then_inc(w_in[side], 16)
                sp.dma_start(w2_buf[:, side], W2[e].rearrange("(c f) h -> f c h", f=P)).then_inc(w_in[side], 16)

            for side in range(2):
                load_expert(side, side)

            run_pairs(sp, half)

            sp.wait_ge(rows_scaled, TILES)
            sp.dma_start(summed.rearrange("(t p) d -> p t d", p=P), rows[:, :, 0:D]).then_inc(sum_out, 16)
            sp.wait_ge(gates_made, 1)
            sp.dma_start(x1_table.rearrange("(t p) d -> p t d", p=P), rows[:]).then_inc(table_out, 16)
            sp.wait_ge(found, 1)
            sp.dma_start(token_list.rearrange("(q e) (a b) -> (e a) q b", q=2, b=32), picked[:]).then_inc(list_out, 16)
            sp.wait_ge(list_out, 16)
            sp.dma_start(index[:], token_list.rearrange("e (p c) -> p e c", c=CHUNKS)).then_inc(index_in, 16)

            with sp.Fori(1, EXPERTS // 2) as n:
                for side in range(2):
                    sp.wait_ge(down_full, 4 * (n - 1) + 2 * (side + 1))
                    load_expert(2 * n + side, side)

            for side in range(2):
                sp.wait_ge(added[side], 16 * CHUNKS * EXPERTS // 2)
            QT = TILES // 4
            for q in range(4):
                sp.dma_start(xc_all[:, q * QT:(q + 1) * QT], summed_rows[:, q * QT:(q + 1) * QT]).then_inc(f_in[q], 16)
            for q in range(4):
                sp.wait_ge(f_done, QT * (q + 1))
                sp.dma_start(out_rows[:, q * QT:(q + 1) * QT], xc_all[:, q * QT:(q + 1) * QT]).then_inc(f_out, 16)
            sp.wait_ge(f_out, 64)

        @block.gpsimd
        def _(pool):
            g = nc.gpsimd
            g.memset(ident[:], 0.0).then_inc(hi_done, 1)
            pool.wait_ge(hi_done, 1)
            g.affine_select(out=ident[:], in_=ident[:], compare_op=ALU.not_equal, fill=1.0, base=0,
                            pattern=[[-1, P]], channel_multiplier=1).then_inc(consts_set, 1)
            g.memset(ones[:], 1.0).then_inc(consts_set, 1)
            g.memset(eps_col[:], EPS).then_inc(consts_set, 1)
            g.memset(q_stack[:].bitcast(F32), 0.0).then_inc(consts_set, 1)
            g.memset(k_first[:].bitcast(F32), 0.0).then_inc(consts_set, 1)
            g.memset(k_second[:].bitcast(F32), 0.0).then_inc(hi_done, 1)
            g.memset(v_ones[:], 0.0).then_inc(hi_done, 1)
            pool.wait_ge(hi_done, 3)
            g.memset(v_ones[:, :, :, :, DH:DH + 1], 1.0).then_inc(consts_set, 1)

            def split(pair, k_number, q_number):
                for full, hi, lo_, number, done, half_ in (
                        (k_full, k_hi, k_lo, k_number, k_cut, 0), (q_full, q_hi, q_lo, q_number, q_cut, 1)):
                    pool.wait_ge(job_free, number + 1)
                    if type(pair) is not int or pair > 0:
                        pool.wait_ge(split_stored, 16 * 2 * 2 * TERMS * pair)
                        passed(pool, pool_waits)
                    g.tensor_copy(hi[:], full).then_inc(hi_done, 1)
                    pool.wait_ge(hi_done, 3 + 2 * pair + half_ + 1)
                    g.tensor_tensor(lo_[:], full, hi[:].bitcast(F32), ALU.subtract).then_inc(done, 1)

            def copy_v(batch, side):
                passed(pool, pool_waits)
                src = v_stage[:, 2 * side:2 * side + 2].rearrange("p j (h d) -> p j h d", h=HEADS)
                g.tensor_copy(v_ones[:, side, :, :, 0:DH], src).then_inc(v_ready, 1)

            def copy_x(pair):
                g.tensor_copy(x_pair[:], rows[:, bass.ds(4 * pair, 4), 0:D]).then_inc(x_copied, 1)

            def centre(batch):
                pool.wait_ge(mv_done, 2 * batch + 2)
                if not (type(batch) is int and batch == 0):
                    pool.wait_ge(xc_kept, batch)
                passed(pool, pool_waits)
                for i in range(2):
                    g.tensor_scalar(xc[:, i], resid[:, i], mean_var[:, i, 0:1], None, ALU.subtract).then_inc(centred, 1)
                pool.wait_ge(centred, 2 * batch + 2)
                passed(pool, pool_waits)
                g.tensor_copy(xc_all[:, bass.ds(2 * batch, 2)], xc[:]).then_inc(xc_kept, 1)

            g.iota(part_i[:], pattern=[[0, 2]], base=0, channel_multiplier=1).then_inc(indices_set, 1)
            g.iota(col_i[:, 0], pattern=[[0, 16], [1, EXPERTS]], base=0, channel_multiplier=0).then_inc(indices_set, 1)
            g.iota(col_i[:, 1], pattern=[[1, 16], [0, EXPERTS]], base=0, channel_multiplier=0).then_inc(indices_set, 1)
            g.iota(iota32_i[:], pattern=[[1, 32]], base=0, channel_multiplier=0).then_inc(indices_set, 1)
            g.iota(token_i[:], pattern=[[P, TILES]], base=-ID_BASE, channel_multiplier=1).then_inc(indices_set, 1)
            for j in range(3):
                g.memset(one23[:, j:j + 1], j + 1.0).then_inc(indices_set, 1)
            g.memset(ones_b[:], 1.0).then_inc(indices_set, 1)
            pool.wait_ge(indices_set, 9)
            g.affine_select(out=upper_b[:], in_=ones_b[:], compare_op=ALU.is_gt, fill=0.0, base=0,
                            pattern=[[1, P]], channel_multiplier=-1).then_inc(indices_set, 1)

            pool.wait_ge(x_head_in, 32)
            copy_x(0)
            split(0, PROLOGUE.index("k"), PROLOGUE.index("q"))
            pool.wait_ge(job_free, PROLOGUE.index("v") + 1)
            copy_v(0, 0)
            pool.wait_ge(x_rest_in, 16)

            def half(h):
                if h.side == 0:
                    if h.prep:
                        copy_x(h.n + 1)
                    if h.prev:
                        pool.wait_ge(pv_done, 4 * h.b)
                    copy_v(h.b + 1, 1)
                    if h.prep:
                        split(h.n + 1, h.number("k"), h.number("q"))
                elif h.ahead:
                    pool.wait_ge(pv_done, 4 * h.b)
                    pool.wait_ge(job_free, h.number_in_side_0("v") + 1)
                    copy_v(h.b + 1, 0)
                if h.prev:
                    centre(h.b - 1)

            run_pairs(pool, half)
            centre(BATCHES - 1)

            for q in range(4):
                ts = slice(q * TILES // 4, (q + 1) * TILES // 4)
                pool.wait_ge(hot_b_made, q + 1)
                ids = token_id[:, ts].unsqueeze(2).unsqueeze(3).to_broadcast([P, TILES // 4, EXPERTS, 32])
                g.tensor_tensor(hot_b[:, ts], hot_b[:, ts], ids, ALU.mult).then_inc(hot_id_made, 1)


            pool.wait_ge(index_in, 16)
            pool.wait_ge(table_out, 16)
            pool.wait_ge(sum_out, 16)

            def gather(n, side, again):
                e = 2 * n + side
                g.tensor_copy(index_now[:, side], index[:, bass.ds(e, 1)].rearrange("p o c -> p (o c)")).then_inc(index_set, 1)
                pool.wait_ge(index_set, e + 1)
                if again:
                    pool.wait_ge(y_made, 8 * (e - 2) + 8)
                passed(pool, pool_waits)
                for c in range(CHUNKS):
                    g.indirect_dma_start(taken[:, side, c], None, x1_table,
                                         bass.IndirectOffsetOnAxis(ap=index_now[:, side, c:c + 1], axis=0)
                                         ).then_inc(taken_in[2 * side + c // 4], 16)

            def scatter(n, side, first=False):
                e = 2 * n + side
                if not first:
                    before = 16 * CHUNKS * (n if side == 0 else n + 1)
                    pool.wait_ge(added[1 - side], before)
                for c in range(CHUNKS):
                    pool.wait_ge(y_made, 8 * e + c + 1)
                    passed(pool, pool_waits)
                    g.indirect_dma_start(summed, bass.IndirectOffsetOnAxis(ap=index_now[:, side, c:c + 1], axis=0),
                                         y_out[:, side, c], None, compute_op=ALU.add).then_inc(added[side], 16)

            gather(0, 0, False)
            gather(0, 1, False)
            with pool.Fori(1, EXPERTS // 2) as n:
                for side in range(2):
                    scatter(n - 1, side)
                    pool.wait_ge(added[side], 16 * CHUNKS * n)
                    gather(n, side, True)
            for side in range(2):
                scatter(EXPERTS // 2 - 1, side)

        @block.scalar
        def _(act):
            s = nc.scalar
            act.dma_start(rows[:, 0:4, 0:D], x_tiled[:, 0:4]).then_inc(x_head_in, 16)
            act.dma_start(rows[:, 4:TILES, 0:D], x_tiled[:, 4:TILES]).then_inc(x_rest_in, 16)
            act.dma_start(b2_row[:], b2.rearrange("e h -> (e h)").unsqueeze(0)).then_inc(x_head_in, 16)

            def evacuate(job, number):
                if job not in ("xT", "latent", "k", "q", "v", "oT", "xcT"):
                    return
                act.wait_ge(job_full, number + 1)
                if job == "xT":
                    ins = s.copy(xT[:], ps_job[:])
                elif job == "latent":
                    ins = s.activation(latT[:], ps_job[0:LATENT], ACT.Identity, bias=bl_col[:, 0:1])
                elif job == "k":
                    ins = s.activation(k_full, ps_job[:], ACT.Identity, bias=bk_col[:, 0:1])
                elif job == "q":
                    ins = s.activation(q_full, ps_job[:], ACT.Identity, bias=bq_col[:, 0:1])
                elif job == "v":
                    ins = s.copy(v_stage[:].rearrange("p a b -> p (a b)"), ps_job[:])
                elif job == "oT":
                    ins = s.copy(oT[:], ps_job[:, 0:SEQ])
                else:
                    ins = s.copy(xcT[:], ps_job[:, 0:SEQ])
                ins.then_inc(job_free, 1)

            act.wait_ge(weights_in, 16 * N_WEIGHTS)
            act.wait_ge(bias_out, 1)
            for i, job in enumerate(PROLOGUE):
                evacuate(job, i)

            def half(h):
                for k in range(HEADS):
                    r, gg = divmod(k, NG)
                    head = 16 * h.b + k
                    act.wait_ge(second_full, head + 1)
                    if gg == 0 and (h.prev or r >= 2):
                        act.wait_ge(pv_done, 4 * h.b + r - 1)
                    s.activation(probs[:, 4 * (r % 2) + gg], ps_second[:, k % 2], ACT.Exp,
                                 scale=SCALE).then_inc(exp_done, 1)
                    if k in h.jobs:
                        job, number = h.jobs[k]
                        if job in ("k", "q"):
                            act.wait_ge(k_cut if job == "k" else q_cut, h.n + 1)
                        if job == "v":
                            act.wait_ge(v_ready, h.b + 2)
                        evacuate(job, number)
                    if k == 11:
                        act.wait_ge(pv_done, 4 * h.b + 2)
                        if h.prev:
                            act.wait_ge(job_full, h.number("norm1") + 1)
                        s.copy(oT_raw[:, 0:2].rearrange("p r i -> p (r i)"),
                               ps_pv[:].rearrange("p r i -> p (r i)")).then_inc(o_copied, 1)

            run_pairs(act, half)
            evacuate("oT", BASE_END + 2)
            evacuate("xcT", BASE_END + 4)

            act.wait_ge(var_kept, BATCHES)
            s.activation(rstd[:], var_all[:], ACT.Sqrt, bias=eps_col[:, 0:1]).then_inc(var_rooted, 1)
            act.wait_ge(rstd_made, 1)
            act.wait_ge(xc_kept, BATCHES)
            with act.Fori(0, TILES) as t:
                s.activation(rows[:, bass.ds(t, 1), 0:D].rearrange("p o d -> p (o d)"),
                             xc_all[:, bass.ds(t, 1)].rearrange("p o d -> p (o d)"),
                             ACT.Copy, scale=rstd[:, bass.ds(t, 1)]).then_inc(rows_scaled, 1)
            act.wait_ge(lg_made, 1)
            s.activation(rows[:, :, D:GATED], lg[:], ACT.Sigmoid).then_inc(gates_made, 1)

            def gelu(n, blk):
                for f in range(FBLK):
                    act.wait_ge(up_full, 16 * n + 4 * blk + f + 1)
                    if f == 0 and not (type(n) is int and blk < 2):
                        act.wait_ge(down_full, 4 * n + blk - 1)
                    passed(act, act_waits)
                    s.activation(hT[:, blk % 2, f], ps_first[:, f], ACT.Gelu,
                                 bias=b1_cols[:, bass.ds(FBLK * (2 * n + blk // 2) + f, 1)]).then_inc(gelu_done, 1)

            for blk in range(4):
                gelu(0, blk)
            with act.Fori(1, EXPERTS // 2) as n:
                for blk in range(4):
                    gelu(n, blk)

            QT = TILES // 4
            for q in range(4):
                act.wait_ge(f_averaged, QT * (q + 1))
                s.activation(f_sd[:, q * QT:(q + 1) * QT].unsqueeze(2), f_mv[:, q * QT:(q + 1) * QT, 1:2], ACT.Sqrt,
                             bias=eps_col[:, 0:1]).then_inc(f_rooted, 1)

        @block.tensor
        def _(pe):
            t_ = nc.tensor
            pe.wait_ge(weights_in, 16 * N_WEIGHTS)
            pe.wait_ge(consts_set, 2)
            pe.wait_ge(perm_done, 4)
            pe.wait_ge(x_head_in, 32)
            for i in range(2):
                t_.matmul(ps_pv[:, 0, i:i + 1], bias_perm[:, i], ones[0:1, 0:1], start=True, stop=True)
            t_.transpose(ps_pv[:, 0, 32:32 + EXPERTS * FBLK], b1_rows[:], ident[0:EXPERTS * FBLK, 0:EXPERTS * FBLK])
            for i in range(2):
                mm = t_.matmul(ps_second[:, i], ones[0:1, :], b2_row[:, i * 512:(i + 1) * 512], start=True, stop=True)
            mm.then_inc(bias_made, 1)

            def run_job(job, number, batch, tail_batch=None):
                if not (type(number) is int and number == 0):
                    pe.wait_ge(job_free, number)
                if job == "xT":
                    pe.wait_ge(x_copied, batch + 1)
                    for c in range(4):
                        mm = t_.transpose(ps_job[:, c * P:(c + 1) * P], x_pair[:, c], ident[:])
                elif job == "latent":
                    mm = t_.matmul(ps_job[0:LATENT, :], wl[:], xT[:], start=True, stop=True)
                elif job == "k":
                    mm = t_.matmul(ps_job[:], wk[:], latT[:], start=True, stop=True)
                elif job == "q":
                    mm = t_.matmul(ps_job[:], wq[:], xT[:], start=True, stop=True)
                elif job == "v":
                    for c in range(4):
                        o = ps_job[:, c * D:(c + 1) * D]
                        t_.matmul(o, ones[0:1, :], bias_rows[:, 2], start=True, stop=False)
                        mm = t_.matmul(o, latT[:, c * P:(c + 1) * P], wv[:], start=False, stop=True)
                elif job.startswith("max"):
                    r = int(job[3])
                    pe.wait_ge(first_free, 8 * batch + 2 * (r + 1))
                    mm = t_.transpose(ps_job[0:2 * NG, 0:P], row_max[:, r], ident[:])
                elif job.startswith("norm"):
                    i = int(job[4])
                    pe.wait_ge(o_copied, 2 * tail_batch + 2)
                    for r in range(NR):
                        mm = t_.transpose(ps_job[:, r * P:(r + 1) * P], oT_raw[:, r, i * P:(i + 1) * P], ident[:])
                elif job == "oT":
                    for i in range(2):
                        mm = t_.transpose(ps_job[:, i * P:(i + 1) * P], o_nat[:, i], ident[:])
                elif job == "y":
                    for i in range(2):
                        o = ps_job[:, i * D:(i + 1) * D]
                        t_.matmul(o, ones[0:1, :], bias_rows[:, 3], start=True, stop=False)
                        mm = t_.matmul(o, oT[:, i * P:(i + 1) * P], wo[:], start=False, stop=True)
                elif job == "xcT":
                    pe.wait_ge(centred, 2 * tail_batch + 2)
                    for i in range(2):
                        mm = t_.transpose(ps_job[:, i * P:(i + 1) * P], xc[:, i], ident[:])
                else:
                    for i in range(2):
                        mm = t_.matmul(ps_job[:, i * EXPERTS:(i + 1) * EXPERTS], xcT[:, i * P:(i + 1) * P], wg[:],
                                       start=True, stop=True)
                mm.then_inc(job_full, 1)

            def first_pass(batch, side, pair, k, fresh):
                r, gg = divmod(k, NG)
                if k == 0:
                    pe.wait_ge(k_first_in[side], 64 * (pair + 1))
                if gg == 0:
                    pe.wait_ge(q_in[r], 16 * (batch + 1))
                tile = 8 * batch + k // 2
                if k % 2 == 0 and not (fresh and k < 4):
                    pe.wait_ge(first_free, tile - 1)
                for i in range(2):
                    o = ps_first[:, 2 * (k // 2 % 2) + k % 2, i * SEQ:(i + 1) * SEQ]
                    mm = t_.matmul(o, q_stack[:, side, r, gg, i * P:(i + 1) * P], k_first[:, side, gg],
                                   start=True, stop=True)
                if k % 2:
                    mm.then_inc(first_full, 1)

            def pv(batch, side, r):
                for j in range(2):
                    for gg in range(NG):
                        mm = t_.matmul(ps_pv[32 * gg:32 * gg + 32, r % 2], v_ones[:, side, j, NR * r + gg],
                                       probs[:, 4 * (r % 2) + gg, j * SEQ:(j + 1) * SEQ],
                                       start=(j == 0), stop=(j == 1), tile_position=(0, 32 * gg))
                mm.then_inc(pv_done, 1)

            for i, job in enumerate(PROLOGUE[:5]):
                run_job(job, i, 0)
            pe.wait_ge(bias_out, 1)
            for k in range(HEADS):
                first_pass(0, 0, 0, k, True)
                if k in MAX_AT and MAX_AT[k] != "max3":
                    run_job(MAX_AT[k], PROLOGUE.index(MAX_AT[k]), 0)

            def half(h):
                for k in range(HEADS):
                    r, gg = divmod(k, NG)
                    if h.nxt:
                        first_pass(h.b + 1, h.after, h.after_pair, k, False)
                    if k == 0:
                        pe.wait_ge(k_second_in[h.side], 64 * (h.n + 1))
                    if gg == 0:
                        pe.wait_ge(shift_in[r], 16 * (h.b + 1))
                    if h.prev or k >= 2:
                        pe.wait_ge(exp_done, 16 * h.b + k - 1)
                    for j in range(2):
                        mm = t_.matmul(ps_second[:, k % 2, j * SEQ:(j + 1) * SEQ],
                                       k_second[:, h.side, gg, j * P:(j + 1) * P],
                                       q_stack[:, h.side, r, gg], start=True, stop=True)
                    mm.then_inc(second_full, 1)
                    if k % 4 == 2 and (k > 2 or h.prev):
                        if k > 2:
                            rr = k // 4 - 1
                            pe.wait_ge(exp_done, 16 * h.b + 4 * (rr + 1))
                            if rr == 0:
                                pe.wait_ge(v_ready, h.b + 1)
                                if h.prev:
                                    pe.wait_ge(o_copied, 2 * h.b)
                            if rr == 2:
                                pe.wait_ge(o_copied, 2 * h.b + 1)
                            pv(h.b, h.side, rr)
                        else:
                            pe.wait_ge(exp_done, 16 * h.b)
                            pv(h.b - 1, 1 - h.side, 3)
                    if k in h.jobs:
                        job, number = h.jobs[k]
                        if job == "xT":
                            run_job(job, number, h.n + 1)
                        elif job == "max3":
                            run_job(job, number, h.b)
                        else:
                            run_job(job, number, h.b + 1, h.b - 1)

            run_pairs(pe, half)
            pe.wait_ge(exp_done, 16 * BATCHES)
            pv(BATCHES - 1, 1, 3)
            for i, job in enumerate(TAIL_AT.values()):
                run_job(job, BASE_END + i, None, BATCHES - 1)

            dv = [0]

            def dve_step(n=1):
                dv[0] += n
                pe.wait_ge(dve_a, dv[0])

            dve_step()
            for i in range(2):
                mm = t_.transpose(ps_job[:, i * P:(i + 1) * P], lg[:, 16 * i:16 * i + 16].rearrange("p t e -> p (t e)"), ident[:])
            mm.then_inc(pe_a, 1)
            dve_step()
            t_.transpose(ps_pv[0:1, 0, 0:P], abs_col[:], ident[:]).then_inc(pe_a, 1)
            dve_step()
            t_.matmul(ps_job[:, 0:1], ones[0:1, :], bound[:], start=True, stop=True).then_inc(pe_a, 1)
            with pe.Fori(0, SEARCH_STEPS) as n:
                pe.wait_ge(counted, 3 * n + 3)
                t_.matmul(ps_pv[:, 0, 0:3], same_e[:], counts[:], start=True, stop=True).then_inc(totalled, 1)
            dve_step()
            t_.matmul(ps_job[:, 0:2 * EXPERTS], ones[:], lo_hi[:].rearrange("p a e -> p (a e)"), start=True,
                      stop=True).then_inc(pe_a, 1)
            dve_step()
            t_.matmul(ps_pv[:, 0, 0:EXPERTS], ones_b[:], gt_sum[:], start=True, stop=True).then_inc(pe_a, 1)

            def prefix(mask, which):
                flat = mask[:].rearrange("p t e -> p (t e)")
                for i in range(2):
                    mm = t_.matmul(ps_pv[:, 1, i:i + 1], flat[:, i * P:(i + 1) * P], ones_b[:, 0:1], start=True, stop=True)
                mm.then_inc(pe_a, 1)
                dve_step()
                t_.matmul(ps_job[:, 0:NPART], upper_b[:], flat, start=True, stop=False, skip_group_check=True)
                first = tile_sum[:, which, 0:1].to_broadcast([P, P])
                second = tile_sum[:, which, 1:2].to_broadcast([P, P])
                t_.matmul(ps_job[:, 0:P], first, before_b[:], start=False, stop=False, skip_group_check=True)
                t_.matmul(ps_job[:, P:2 * P], first, same_eb[:], start=False, stop=False, skip_group_check=True)
                t_.matmul(ps_job[:, P:2 * P], second, before_b[:], start=False, stop=True,
                          skip_group_check=True).then_inc(pe_a, 1)

            dve_step()
            prefix(tie, 0)
            dve_step()
            prefix(sel, 1)
            for t in range(TILES):
                if t % (TILES // 4) == 0:
                    pe.wait_ge(hot_a_made, t // (TILES // 4) + 1)
                    pe.wait_ge(hot_id_made, t // (TILES // 4) + 1)
                for q in range(2):
                    mm = t_.matmul(ps_second[:, q, 0:P], hot_a[:, t, 4 * q:4 * q + 4].rearrange("p e s -> p (e s)"),
                                   hot_b[:, t, 4 * q:4 * q + 4].rearrange("p e s -> p (e s)"),
                                   start=(t == 0), stop=(t == TILES - 1))
            mm.then_inc(pe_a, 1)

            def turn(n, blk):
                side, hb = divmod(blk, 2)
                pe.wait_ge(taken_in[blk], 64 * (n + 1))
                if not (type(n) is int and n == 0 and blk == 0):
                    pe.wait_ge(turned_copied, 4 * n + blk)
                for c in range(4):
                    mm = t_.transpose(ps_job[:, c * P:(c + 1) * P], taken[:, side, 4 * hb + c, 0:D], ident[:])
                mm.then_inc(turned, 1)

            def up(n, blk):
                side = blk // 2
                if blk % 2 == 0:
                    pe.wait_ge(w_in[side], 32 * (n + 1))
                pe.wait_ge(turned_copied, 4 * n + blk + 1)
                for f in range(FBLK):
                    if not (type(n) is int and n == 0 and blk == 0):
                        pe.wait_ge(gelu_done, 16 * n + 4 * blk + f - 3)
                    t_.matmul(ps_first[:, f], w1_buf[:, side, f * P:(f + 1) * P], takenT[:, blk % 2],
                              start=True, stop=True).then_inc(up_full, 1)

            def down(n, blk, early):
                side = blk // 2
                pe.wait_ge(gelu_done, 16 * n + 4 * blk + 4)
                if not early:
                    pe.wait_ge(y_summed, 4 * n + blk - 1)
                for c in range(4):
                    for f in range(FBLK):
                        mm = t_.matmul(ps_second[:, blk % 2, c * P:(c + 1) * P], hT[:, blk % 2, f, c * P:(c + 1) * P],
                                       w2_buf[:, side, f], start=(f == 0), stop=(f == FBLK - 1))
                mm.then_inc(down_full, 1)

            pe.wait_ge(found, 1)
            for blk in range(4):
                turn(0, blk)
                if blk:
                    down(0, blk - 1, blk < 3)
                up(0, blk)
            with pe.Fori(1, EXPERTS // 2) as n:
                for blk in range(4):
                    turn(n, blk)
                    if blk:
                        down(n, blk - 1, False)
                    else:
                        down(n - 1, 3, False)
                    up(n, blk)
            down(EXPERTS // 2 - 1, 3, False)

        @block.vector
        def _(dve):
            v = nc.vector
            dve.wait_ge(weights_in, 16 * N_WEIGHTS)
            for nat, perm in ((wq_nat[:], wq[:]), (wk_nat[:], wk[:]), (bias_rows[:, 0], bias_perm[:, 0]),
                              (bias_rows[:, 1], bias_perm[:, 1])):
                v.tensor_copy(perm.rearrange("p (r d g) -> p r d g", r=NR, g=NG),
                              nat.rearrange("p (r g d) -> p r d g", r=NR, g=NG)).then_inc(perm_done, 1)
            dve.wait_ge(hi_done, 2)
            for r in range(NR):
                v.memset(k_second[32 * r:32 * r + 1].bitcast(F32), 1.0).then_inc(shift_ones, 1)
            dve.wait_ge(bias_made, 1)
            v.tensor_copy(bq_col[:], ps_pv[:, 0, 0:1])
            v.tensor_copy(bk_col[:], ps_pv[:, 0, 1:2])
            v.tensor_copy(b1_cols[:], ps_pv[:, 0, 32:32 + EXPERTS * FBLK])
            v.tensor_copy(b2_all[:].rearrange("p e d -> p (e d)"),
                          ps_second[:].rearrange("p a b -> p (a b)")).then_inc(bias_out, 1)

            def take_maxima(batch, k):
                r, half_ = k // 4, k // 2 % 2
                tile = 8 * batch + k // 2
                dve.wait_ge(first_full, tile + 1)
                v.tensor_reduce(row_max[:, r, 4 * half_:4 * half_ + 4],
                                ps_first[:, 2 * half_:2 * half_ + 2].rearrange("p a (i j) -> p (a i) j", i=2),
                                AX, ALU.max).then_inc(first_free, 1)

            def evacuate(job, number, batch, tail):
                if job in ("xT", "latent", "k", "q", "v", "oT", "xcT"):
                    return
                dve.wait_ge(job_full, number + 1)
                if job.startswith("max"):
                    r = int(job[3])
                    if not (type(batch) is int and batch == 0):
                        dve.wait_ge(shift_in[r], 16 * batch)
                    ins = v.tensor_scalar(shift_t[:, r], ps_job[0:2 * NG, 0:P], -1.0, None, ALU.mult)
                elif job.startswith("norm"):
                    i = int(job[4])
                    heads = ps_job[:].rearrange("p (h c) -> p h c", c=32)
                    v.reciprocal(den[:].unsqueeze(2), heads[:, :, DH:DH + 1]).then_inc(den_done, 1)
                    dve.wait_ge(den_done, 2 * tail + i + 1)
                    ins = v.tensor_tensor(o_nat[:, i].rearrange("p (h d) -> p h d", d=DH), heads[:, :, 0:DH],
                                          den[:].unsqueeze(2).to_broadcast([P, HEADS, DH]), ALU.mult)
                elif job == "y":
                    if not (type(tail) is int and tail == 0):
                        dve.wait_ge(centred, 2 * tail)
                    ins = v.tensor_tensor(resid[:], ps_job[:, 0:2 * D].rearrange("p (i d) -> p i d", i=2),
                                          rows[:, bass.ds(2 * tail, 2), 0:D], ALU.add)
                else:
                    ins = v.tensor_copy(logits[:, bass.ds(2 * tail, 2)],
                                        ps_job[:, 0:2 * EXPERTS].rearrange("p (i e) -> p i e", i=2))
                ins.then_inc(job_free, 1)
                if job == "y":
                    dve.wait_ge(job_free, number + 1)
                    for i in range(2):
                        v.bn_stats(stats[:, i], resid[:, i]).then_inc(stats_done, 1)
                    dve.wait_ge(stats_done, 2 * tail + 2)
                    passed(dve, dve_waits)
                    for i in range(2):
                        v.bn_aggr(mean_var[:, i], stats[:, i]).then_inc(mv_done, 1)
                    dve.wait_ge(mv_done, 2 * tail + 2)
                    v.tensor_copy(var_all[:, bass.ds(2 * tail, 2)].unsqueeze(2), mean_var[:, :, 1:2]).then_inc(var_kept, 1)

            for k in range(HEADS):
                if k % 2:
                    take_maxima(0, k)
                if k in MAX_AT and MAX_AT[k] != "max3":
                    evacuate(MAX_AT[k], PROLOGUE.index(MAX_AT[k]), 0, 0)
            dve.wait_ge(x_head_in, 32)
            dve.wait_ge(x_rest_in, 16)

            def half(h):
                for k in range(HEADS):
                    if h.nxt and k % 2:
                        take_maxima(h.b + 1, k)
                    if k == 3 and h.prev:
                        dve.wait_ge(pv_done, 4 * h.b)
                        v.tensor_copy(oT_raw[:, 2:4], ps_pv[:]).then_inc(o_copied, 1)
                    if k in h.jobs:
                        job, number = h.jobs[k]
                        evacuate(job, number, h.b if job == "max3" else h.b + 1, h.b - 1)

            run_pairs(dve, half)
            dve.wait_ge(pv_done, 4 * BATCHES)
            v.tensor_copy(oT_raw[:, 2:4], ps_pv[:]).then_inc(o_copied, 1)
            for i, job in enumerate(TAIL_AT.values()):
                evacuate(job, BASE_END + i, None, BATCHES - 1)

            made, chained = [0], [0]

            def for_pe(ins):
                made[0] += 1
                ins.then_inc(dve_a, 1)
                dve.wait_ge(dve_a, made[0])

            def link(ins):
                chained[0] += 1
                ins.then_inc(own, 1)
                dve.wait_ge(own, chained[0])

            read = [0]

            def from_pe():
                read[0] += 1
                dve.wait_ge(pe_a, read[0])

            dve.wait_ge(indices_set, 10)
            v.tensor_copy(iota32[:], iota32_i[:])
            v.tensor_copy(token_id[:], token_i[:])
            link(v.tensor_scalar(part_i[:, 0:1], part_i[:, 0:1], EXPERTS - 1, None, ALU.bitwise_and))
            link(v.tensor_scalar(part_i[:, 1:2], part_i[:, 1:2], 3, None, ALU.arith_shift_right))
            link(v.tensor_copy(part_f[:], part_i[:]))
            link(v.tensor_scalar(same_e[:], col_i[:, 0], part_f[:, 0:1], None, ALU.is_equal))
            link(v.tensor_copy(same_eb[:], same_e[:]))
            link(v.scalar_tensor_tensor(out=before_b[:], in0=col_i[:, 1], scalar=part_f[:, 1:2], in1=same_e[:],
                                        op0=ALU.is_gt, op1=ALU.mult))

            dve.wait_ge(var_rooted, 1)
            v.reciprocal(rstd[:], rstd[:]).then_inc(rstd_made, 1)
            dve.wait_ge(rstd_made, 1)
            v.tensor_tensor(lg[:], logits[:], rstd[:].unsqueeze(2).to_broadcast([P, TILES, EXPERTS]),
                            ALU.mult).then_inc(lg_made, 1)
            dve.wait_ge(lg_made, 1)
            for_pe(v.memset(abs_row[:], 0.0))
            from_pe()
            link(v.tensor_copy(lgT[:], ps_job[:, 0:2 * P]))
            for_pe(v.tensor_reduce(abs_col[:], lgT[:], AX, ALU.max, apply_absolute_value=True))
            from_pe()
            link(v.tensor_reduce(abs_row[:], ps_pv[0:1, 0, 0:P], AX, ALU.max))
            link(v.tensor_scalar(bound[:].bitcast(I32), abs_row[:].bitcast(I32), 0x7F800000, None, ALU.bitwise_and))
            for_pe(v.tensor_scalar(bound[:], bound[:], 2.0, 1e-30, ALU.mult, ALU.max))
            from_pe()
            link(v.tensor_scalar(lo[:], ps_job[:, 0:1], -1.0, None, ALU.mult))
            link(v.tensor_scalar(steps3[:], one23[:], lo[:, 0:1], -0.5, ALU.mult, ALU.mult))
            with dve.Fori(0, SEARCH_STEPS) as n:
                v.tensor_scalar(thr[:], steps3[:], lo[:, 0:1], None, ALU.add).then_inc(thr_made, 1)
                dve.wait_ge(thr_made, n + 1)
                for j in range(3):
                    v.tensor_scalar(hits[:, j], lgT[:], thr[:, j:j + 1], None, ALU.is_ge, ALU.add,
                                    accum_out=counts[:, j:j + 1]).then_inc(counted, 1)
                dve.wait_ge(totalled, n + 1)
                v.tensor_scalar(above[:], ps_pv[:, 0, 0:3], CAPACITY - 0.5, None, ALU.is_ge, ALU.add,
                                accum_out=n_above[:]).then_inc(own_loop, 1)
                dve.wait_ge(own_loop, n + 1)
                v.scalar_tensor_tensor(out=lo[:], in0=n_above[:], scalar=steps3[:, 0:1], in1=lo[:],
                                       op0=ALU.mult, op1=ALU.add).then_inc(lo_made, 1)
                dve.wait_ge(lo_made, n + 1)
                v.tensor_scalar(steps3[:], steps3[:], 0.25, None, ALU.mult).then_inc(stepped, 1)
                dve.wait_ge(stepped, n + 1)

            link(v.scalar_tensor_tensor(out=hi_col[:], in0=steps3[:, 0:1], scalar=4.0, in1=lo[:],
                                        op0=ALU.mult, op1=ALU.add))
            link(v.tensor_scalar(lo_hi[:, 0], ident[:, 0:EXPERTS], lo[:, 0:1], None, ALU.mult))
            for_pe(v.tensor_scalar(lo_hi[:, 1], ident[:, 0:EXPERTS], hi_col[:, 0:1], None, ALU.mult))
            from_pe()
            link(v.tensor_copy(bounds[:].rearrange("p a e -> p (a e)"), ps_job[:, 0:2 * EXPERTS]))
            wide = [P, TILES, EXPERTS]
            link(v.tensor_tensor(gt[:], lg[:], bounds[:, 1].unsqueeze(1).to_broadcast(wide), ALU.is_ge))
            with nc.allow_low_precision("counts up to 32 are exact in bfloat16"):
                for_pe(v.tensor_reduce(gt_sum[:], gt[:].rearrange("p t e -> p e t"), AX, ALU.add))
            link(v.tensor_tensor(ge[:], lg[:], bounds[:, 0].unsqueeze(1).to_broadcast(wide), ALU.is_ge))
            from_pe()
            link(v.tensor_copy(gt_all[:], ps_pv[:, 0, 0:EXPERTS]))
            for_pe(v.tensor_tensor(tie[:], ge[:], gt[:], ALU.subtract))
            from_pe()
            for_pe(v.tensor_copy(tile_sum[:, 0], ps_pv[:, 1, 0:2]))
            from_pe()
            ranks = ps_job[:, 0:NPART].rearrange("p (t e) -> p t e", e=EXPERTS)
            link(v.tensor_tensor(rank[:], ranks, gt_all[:].unsqueeze(1).to_broadcast(wide), ALU.add))
            link(v.scalar_tensor_tensor(out=ge[:], in0=rank[:], scalar=CAPACITY - 0.5, in1=tie[:],
                                        op0=ALU.is_lt, op1=ALU.mult))
            for_pe(v.tensor_tensor(sel[:], gt[:], ge[:], ALU.add))
            link(v.tensor_scalar(off_slot[:], sel[:].rearrange("p t e -> p (t e)"), float(TOKENS), -float(TOKENS),
                                 ALU.mult, ALU.add))
            from_pe()
            for_pe(v.tensor_copy(tile_sum[:, 1], ps_pv[:, 1, 0:2]))
            from_pe()
            link(v.tensor_tensor(slot[:], ps_job[:, 0:NPART], off_slot[:], ALU.add))
            link(v.tensor_scalar(slot_a[:], slot[:], 5, None, ALU.arith_shift_right))
            link(v.tensor_scalar(slot_b[:], slot[:], 31, None, ALU.bitwise_and))
            for q in range(4):
                ts = slice(q * TILES // 4, (q + 1) * TILES // 4)
                cols = slice(q * NPART // 4, (q + 1) * NPART // 4)
                shape = [P, NPART // 4, 32]
                for hot, part, done in ((hot_a, slot_a, hot_a_made), (hot_b, slot_b, hot_b_made)):
                    v.tensor_tensor(hot[:, ts].rearrange("p t e s -> p (t e) s"), iota32[:].unsqueeze(1).to_broadcast(shape),
                                    part[:, cols].unsqueeze(2).to_broadcast(shape), ALU.is_equal).then_inc(done, 1)
            from_pe()
            for e in range(4):
                ins = v.tensor_scalar(picked[32 * e:32 * e + 32], ps_second[32 * e:32 * e + 32, :, 32 * e:32 * e + 32],
                                      float(ID_BASE), None, ALU.add)
            ins.then_inc(found, 1)

            def copy_turned(n, blk):
                dve.wait_ge(turned, 4 * n + blk + 1)
                v.tensor_copy(takenT[:, blk % 2], ps_job[:]).then_inc(turned_copied, 1)

            def gate(n, blk):
                side, hb = divmod(blk, 2)
                e = 2 * n + side
                dve.wait_ge(down_full, 4 * n + blk + 1)
                b2_rows = b2_all[:, bass.ds(e, 1)].to_broadcast([P, 4, D])
                v.tensor_tensor(y_sum[:, blk % 2], ps_second[:, blk % 2].rearrange("p (c d) -> p c d", c=4), b2_rows,
                                ALU.add).then_inc(y_summed, 1)
                dve.wait_ge(y_summed, 4 * n + blk + 1)
                if hb == 0 and not (type(n) is int and n == 0):
                    dve.wait_ge(added[side], 16 * CHUNKS * n)
                for c in range(4):
                    ch = 4 * hb + c
                    v.tensor_scalar(y_out[:, side, ch], y_sum[:, blk % 2, c], taken[:, side, ch, bass.ds(D + e, 1)],
                                    None, ALU.mult).then_inc(y_made, 1)

            for blk in range(4):
                copy_turned(0, blk)
                if blk:
                    gate(0, blk - 1)
            with dve.Fori(1, EXPERTS // 2) as n:
                for blk in range(4):
                    copy_turned(n, blk)
                    if blk:
                        gate(n, blk - 1)
                    else:
                        gate(n - 1, 3)
            gate(EXPERTS // 2 - 1, 3)

            QT = TILES // 4
            for q in range(4):
                dve.wait_ge(f_in[q], 16)
                with dve.Fori(QT * q, QT * (q + 1)) as t:
                    row = xc_all[:, bass.ds(t, 1)].rearrange("p o d -> p (o d)")
                    v.bn_stats(f_stats[:, bass.ds(t, 1)].rearrange("p o s -> p (o s)"), row).then_inc(f_statted, 1)
                dve.wait_ge(f_statted, QT * (q + 1))
                for t in range(QT * q, QT * (q + 1)):
                    v.bn_aggr(f_mv[:, t], f_stats[:, t]).then_inc(f_averaged, 1)
            for q in range(4):
                dve.wait_ge(f_rooted, q + 1)
                v.reciprocal(f_rstd[:, QT * q:QT * (q + 1)], f_sd[:, QT * q:QT * (q + 1)]).then_inc(f_inverted, 1)
                dve.wait_ge(f_inverted, q + 1)
                with dve.Fori(QT * q, QT * (q + 1)) as t:
                    row = xc_all[:, bass.ds(t, 1)].rearrange("p o d -> p (o d)")
                    v.tensor_scalar(row, row, f_mv[:, bass.ds(t, 1), 0:1].rearrange("p o s -> p (o s)"),
                                    f_rstd[:, bass.ds(t, 1)], ALU.subtract, ALU.mult).then_inc(f_done, 1)


_INS = ['L0_attn_x', 'L0_attn_Wq', 'L0_attn_bq', 'L0_attn_Wl', 'L0_attn_bl', 'L0_attn_Wk', 'L0_attn_bk',
        'L0_attn_Wv', 'L0_attn_bv', 'L0_attn_Wo', 'L0_attn_bo', 'L0_ffn_Wg', 'L0_ffn_W1', 'L0_ffn_b1',
        'L0_ffn_W2', 'L0_ffn_b2']


def kernel(**inputs):
    import numpy as _np
    import concourse.bacc as _bacc
    from concourse import mybir as _mybir
    from concourse.bass_utils import run_bass_kernel_spmd as _run

    nc = _bacc.Bacc("TRN2", target_bir_lowering=False, num_devices=1)
    arrays, args = {}, []
    for name in _INS:
        a = _np.ascontiguousarray(inputs[name])
        arrays[f"in_{name}"] = a
        args.append(nc.dram_tensor(f"in_{name}", a.shape, _mybir.dt.from_np(a.dtype), kind="ExternalInput").ap())
    out = nc.dram_tensor("out", (BATCHES, SEQ, D), F32, kind="ExternalOutput").ap()
    post_ln_layer(nc, *args, out)
    return _run(nc, [arrays], core_ids=[0]).results[0]["out"]
```

```python
from contextlib import ExitStack

import concourse.bass as bass
from concourse import mybir

P = 128
ALU = mybir.AluOpType
ACT = mybir.ActivationFunctionType
AX = mybir.AxisListType.X
F32 = mybir.dt.float32
F32R = mybir.dt.float32r
BF16 = mybir.dt.bfloat16
F16 = mybir.dt.float16
I32 = mybir.dt.int32
U32 = mybir.dt.uint32

BATCHES, SEQ, D = 16, 256, 128
HEADS, DH, LATENT = 16, 8, 32
EXPERTS, FF = 8, 512
TOKENS = BATCHES * SEQ
CAPACITY = TOKENS * 2 // EXPERTS
TILES = TOKENS // P
PAIRS = BATCHES // 2
NPART = TILES * EXPERTS
SCALE = DH ** -0.5
EPS = 1e-5
NR = NG = 4
TERMS = 3
GATED = D + EXPERTS
CHUNKS = CAPACITY // P
SEARCH_STEPS = 12
FBLK = FF // P
ID_BASE = TOKENS // 2

PREP_AT = {0: "xT", 1: "q", 2: "latent", 4: "k", 12: "v"}
MAX_AT = {3: "max3", 7: "max0", 9: "max1", 13: "max2"}
TAIL_AT = {5: "norm0", 6: "norm1", 8: "oT", 10: "y", 14: "xcT", 15: "logits"}
BANK = {"xT": 0, "latent": 0, "q": 1, "k": 0, "v": 1, "max3": 1, "max0": 1, "max1": 1, "max2": 0,
        "norm0": 1, "norm1": 0, "oT": 0, "y": 0, "xcT": 1, "logits": 0}
READS = {"latent": "xT", "q": "xT", "k": "latent", "v": "latent", "oT": "norm0", "y": "oT", "logits": "xcT"}
FIRST_BANK = [k % 3 for k in range(HEADS - 1)] + [1]
FIRST_AGO = [next(a for a in range(1, 5) if FIRST_BANK[(k - a) % HEADS] == FIRST_BANK[k]) for k in range(HEADS)]


def half_jobs(prep, this, nxt, tail):
    jobs = {}
    if prep:
        jobs.update(PREP_AT)
    jobs.update({s: j for s, j in MAX_AT.items() if (this if j == "max3" else nxt)})
    if tail:
        jobs.update(TAIL_AT)
    return sorted(jobs.items())


def uses(jobs):
    return [sum(BANK[j] == bank for j in jobs) for bank in range(2)]


PROLOGUE = list(PREP_AT.values()) + ["max0", "max1", "max2"]
FIRST = [half_jobs(True, True, True, False), half_jobs(False, True, True, True)]
MIDDLE = [half_jobs(True, True, True, True), half_jobs(False, True, True, True)]
LAST = [half_jobs(False, True, True, True), half_jobs(False, True, False, True)]
N_FIRST, N_MIDDLE, N_LAST = (uses([j for h in body for _, j in h]) for body in (FIRST, MIDDLE, LAST))
BASE_FIRST = uses(PROLOGUE)
BASE_MIDDLE = [b + n for b, n in zip(BASE_FIRST, N_FIRST)]
BASE_LAST = [b + (PAIRS - 2) * n for b, n in zip(BASE_MIDDLE, N_MIDDLE)]
BASE_END = [b + n for b, n in zip(BASE_LAST, N_LAST)]


def numbers(jobs, base):
    base, out = list(base), {}
    for job in jobs:
        out[job] = base[BANK[job]]
        base[BANK[job]] = base[BANK[job]] + 1
    return out


class Half:

    def __init__(self, n, side, first=False, last=False):
        self.n, self.side, self.b = n, side, 2 * n + side
        self.prep = side == 0 and not last
        self.nxt = not (last and side == 1)
        self.prev = not (first and side == 0)
        self.ahead = not last
        body = FIRST if first else LAST if last else MIDDLE
        base = BASE_FIRST if first else BASE_LAST if last else [
            b + (n - 1) * k for b, k in zip(BASE_MIDDLE, N_MIDDLE)]
        before = uses([j for _, j in body[0]]) if side else [0, 0]
        self.side_0 = numbers([j for _, j in body[0]], base)
        self.uses = numbers([j for _, j in body[side]], [b + k for b, k in zip(base, before)])
        self.jobs = dict(body[side])
        self.after = (side + 1) % 2
        self.after_pair = n + side


def passed(engine, waits):
    engine.sem_inc(waits, 1)


def run_pairs(engine, body, last_pairs=1):
    for side in range(2):
        body(Half(0, side, first=True))
    with engine.Fori(1, PAIRS - last_pairs) as n:
        for side in range(2):
            body(Half(n, side))
    for n in range(PAIRS - last_pairs, PAIRS):
        for side in range(2):
            body(Half(n, side, last=(n == PAIRS - 1)))


def post_ln_layer(nc, x, Wq, bq, Wl, bl, Wk, bk, Wv, bv, Wo, bo, Wg, W1, b1, W2, b2, out):
    with ExitStack() as ctx:
        def sb(name, shape, dt=F32):
            return ctx.enter_context(nc.sbuf_tensor(name, shape, dt))

        def psum(name, shape):
            return ctx.enter_context(nc.psum_tensor(name, shape, F32))

        def sem(name):
            return ctx.enter_context(nc.semaphore(name))

        q_split = nc.dram_tensor("q_split", [PAIRS, NR, TERMS, DH, NG, 2, SEQ], F32, kind="Internal").ap()
        k_split = nc.dram_tensor("k_split", [PAIRS, NR, TERMS, DH, NG, 2, SEQ], F32, kind="Internal").ap()
        x1_table = nc.dram_tensor("x1_table", [TOKENS, GATED], F32, kind="Internal").ap()
        summed = nc.dram_tensor("summed", [TOKENS, D], F32, kind="Internal").ap()
        token_list = nc.dram_tensor("token_list", [EXPERTS, CAPACITY], U32, kind="Internal").ap()

        banks = psum("banks", [P, 8, 512])
        ps_first, ps_job = banks[:, 0:3], banks[:, 3:5]
        ps_second = banks[:, 5:7]
        ps_pv = banks[:, 7].rearrange("p (r i) -> p r i", r=2)
        ps_up, ps_turn = banks[:, 0:4], banks[:, 4]
        ps_a = ps_job[:, 0]

        ident = sb("ident", [P, P])
        ones = sb("ones", [P, P])
        eps_col = sb("eps_col", [P, 1])
        wq_nat, wq = sb("wq_nat", [P, P]), sb("wq", [P, P])
        wk_nat, wk = sb("wk_nat", [LATENT, P]), sb("wk", [LATENT, P])
        wl, wv = sb("wl", [P, LATENT]), sb("wv", [LATENT + 1, P])
        wo, wg = sb("wo", [P, P]), sb("wg", [P, EXPERTS])
        bias_rows = sb("bias_rows", [1, 2, P])
        bo_all = sb("bo_all", [P, P])
        bias_perm = sb("bias_perm", [1, 2, P])
        bl_col = sb("bl_col", [LATENT, 1])
        bq_col, bk_col = sb("bq_col", [P, 1]), sb("bk_col", [P, 1])
        b1_rows, b1_cols = sb("b1_rows", [EXPERTS * FBLK, P]), sb("b1_cols", [P, EXPERTS * FBLK])
        b2_all = sb("b2_all", [P, EXPERTS, D])
        shift_rows = sb("shift_rows", [P, 1])

        rows = sb("rows", [P, TILES, GATED])
        x_pair, xT = sb("x_pair", [P, 4, D]), sb("xT", [P, 2 * SEQ])
        latT = sb("latT", [LATENT + 1, 2 * SEQ])
        kq_full = sb("kq_full", [P, 2, 2 * SEQ])
        k_full, q_full = kq_full[:, 0], kq_full[:, 1]
        k_hi, k_lo = sb("k_hi", [P, 2 * SEQ], F32R), sb("k_lo", [P, 2 * SEQ], F32R)
        q_hi, q_lo = sb("q_hi", [P, 2 * SEQ], F32R), sb("q_lo", [P, 2 * SEQ], F32R)
        v_stage = sb("v_stage", [P, 4, D])
        v_ones = sb("v_ones", [P, 2, 2, HEADS, 32])
        q_stack = sb("q_stack", [P, 2, NR, NG, SEQ], F32R)
        k_first = sb("k_first", [P, 2, NG, SEQ], F32R)
        k_second = sb("k_second", [P, 2, NG, SEQ], F32R)
        row_max = sb("row_max", [P, NR, 2 * NG])
        shift_t = sb("shift_t", [2 * NG, NR, P], F32R)
        probs = sb("probs", [P, 8, 2 * SEQ])
        oT_raw = sb("oT_raw", [P, NR, SEQ])
        den = sb("den", [P, 2, HEADS])
        o_nat, oT = sb("o_nat", [P, 2, D]), sb("oT", [P, SEQ])
        resid, xc = sb("resid", [P, 2, D]), sb("xc", [P, 2, D])
        stats, mean_var = sb("stats", [P, 2, 6]), sb("mean_var", [P, 2, 2])
        xcT = sb("xcT", [P, SEQ])
        xc_all = sb("xc_all", [P, TILES, D])
        var_all, rstd = sb("var_all", [P, TILES]), sb("rstd", [P, TILES])
        logits = sb("logits", [P, TILES, EXPERTS])

        weights_in, consts_set, perm_done = sem("weights_in"), sem("consts_set"), sem("perm_done")
        bias_made, bias_out = sem("bias_made"), sem("bias_out")
        rows_in, x_pair_in = sem("rows_in"), sem("x_pair_in")
        job_full, job_free = [sem(f"job_full{i}") for i in range(2)], [sem(f"job_free{i}") for i in range(2)]
        rows_biased, latent_one, k_kept = sem("rows_biased"), sem("latent_one"), sem("k_kept")
        hi_done, k_cut, q_cut = sem("hi_done"), sem("k_cut"), sem("q_cut")
        split_stored = sem("split_stored")
        q_in = [sem(f"q_in{r}") for r in range(NR)]
        k_first_in = [sem(f"k_first_in{s}") for s in range(2)]
        shift_in = [sem(f"shift_in{r}") for r in range(NR)]
        first_full, first_free = sem("first_full"), sem("first_free")
        second_full, exp_done = sem("second_full"), sem("exp_done")
        v_ready, pv_done, o_copied = sem("v_ready"), sem("pv_done"), sem("o_copied")
        den_done, stats_done, mv_done = sem("den_done"), sem("stats_done"), sem("mv_done")
        pool_waits, act_waits, dve_waits = sem("pool_waits"), sem("act_waits"), sem("dve_waits")
        shift_ones, indices_set, own, own_loop = sem("shift_ones"), sem("indices_set"), sem("own"), sem("own_loop")
        var_kept, centred, xc_kept = sem("var_kept"), sem("centred"), sem("xc_kept")

        lg = sb("lg", [P, TILES, EXPERTS])
        lgT = sb("lgT", [P, 2 * P])
        abs_col, abs_row, bound = sb("abs_col", [P, 1]), sb("abs_row", [1, 1]), sb("bound", [1, 1])
        bound_col = sb("bound_col", [P, 1])
        quarters, widths = sb("quarters", [P, SEARCH_STEPS + 1, 4]), sb("widths", [P, SEARCH_STEPS + 1, 4])
        thr, next_thr = sb("thr", [P, 4]), sb("next_thr", [P, 4])
        counts = sb("counts", [P, 3])
        above, n_above = sb("above", [P, 3]), sb("n_above", [P, 1])
        lo_hi, bounds = sb("lo_hi", [P, 2, EXPERTS]), sb("bounds", [P, 2, EXPERTS])
        hi_col = sb("hi_col", [P, 1])
        part_i, col_i = sb("part_i", [P, 2], I32), sb("col_i", [P, 2, P], I32)
        part_f = sb("part_f", [P, 2])
        same_e, same_eb = sb("same_e", [P, P]), sb("same_eb", [P, P], BF16)
        before_b = sb("before_b", [P, P], BF16)
        upper_b, ones_b = sb("upper_b", [P, P], BF16), sb("ones_b", [P, P], BF16)
        gt, ge = sb("gt", [P, TILES, EXPERTS], BF16), sb("ge", [P, TILES, EXPERTS], BF16)
        tie, sel = sb("tie", [P, TILES, EXPERTS], BF16), sb("sel", [P, TILES, EXPERTS], BF16)
        gt_sum, gt_all = sb("gt_sum", [P, EXPERTS], BF16), sb("gt_all", [P, EXPERTS])
        tile_sum = sb("tile_sum", [P, 2, 2], BF16)
        rank = sb("rank", [P, TILES, EXPERTS])
        off_slot, slot = sb("off_slot", [P, NPART]), sb("slot", [P, NPART], I32)
        slot_a, slot_b = sb("slot_a", [P, NPART], I32), sb("slot_b", [P, NPART], I32)
        iota32_i, iota32 = sb("iota32_i", [P, 32], I32), sb("iota32", [P, 32])
        token_i, token_id = sb("token_i", [P, TILES], I32), sb("token_id", [P, TILES])
        hot_a = probs[:].bitcast(F16).rearrange("p a b -> p (a b)").rearrange("p (t e s) -> p t e s", t=TILES, e=EXPERTS)
        hT = sb("hT", [P, 2, FBLK, 512])
        hot_b = hT[:].bitcast(F16).rearrange("p a b c -> p (a b c)").rearrange("p (t e s) -> p t e s", t=TILES, e=EXPERTS)
        picked, index = sb("picked", [P, 2, 32], U32), sb("index", [P, EXPERTS, CHUNKS], U32)
        hits = hT[:, 0, 0:3, 0:P].bitcast(BF16)
        from_index, to_index = sb("from_index", [P, 2, CHUNKS], U32), sb("to_index", [P, 2, CHUNKS], U32)
        w1_buf, w2_buf = sb("w1_buf", [P, 2, FF]), sb("w2_buf", [P, 2, FBLK, D])
        taken = sb("taken", [P, 2, CHUNKS, GATED])
        takenT = kq_full
        y_sum = sb("y_sum", [P, 2, 4, D])
        y_out = v_ones[:].rearrange("p s j h c -> p (s j h c)").rearrange("p (s k d) -> p s k d", s=2, k=CHUNKS)
        f_stats, f_mv = sb("f_stats", [P, TILES, 6]), sb("f_mv", [P, TILES, 2])
        f_sd, f_rstd = sb("f_sd", [P, TILES]), sb("f_rstd", [P, TILES])

        var_rooted, rstd_made, lg_made = sem("var_rooted"), sem("rstd_made"), sem("lg_made")
        pe_a, dve_a = sem("pe_a"), sem("dve_a")
        thr_made, counted, totalled, found = sem("thr_made"), sem("counted"), sem("totalled"), sem("found")
        hot_a_made, hot_b_made, hot_id_made = sem("hot_a_made"), sem("hot_b_made"), sem("hot_id_made")
        rows_scaled, gates_made, table_out = sem("rows_scaled"), sem("gates_made"), sem("table_out")
        sum_out, list_out, index_in = sem("sum_out"), sem("list_out"), sem("index_in")
        w_in = [sem(f"w_in{i}") for i in range(2)]
        from_set, to_set = sem("from_set"), sem("to_set")
        taken_in = [sem(f"taken_in{i}") for i in range(4)]
        turned, turned_copied = sem("turned"), sem("turned_copied")
        up_full, gelu_done = sem("up_full"), sem("gelu_done")
        down_full, y_summed, y_made = sem("down_full"), sem("y_summed"), sem("y_made")
        added = [sem(f"added{i}") for i in range(2)]
        f_in = [sem(f"f_in{i}") for i in range(4)]
        f_statted, f_averaged, f_rooted = sem("f_statted"), sem("f_averaged"), sem("f_rooted")
        f_inverted, f_done, f_out = sem("f_inverted"), sem("f_done"), sem("f_out")

        block = ctx.enter_context(nc.Block())

        def last_free(engine, job, uses_of):
            number = uses_of[job]
            if not (type(number) is int and number == 0):
                engine.wait_ge(job_free[BANK[job]], number)

        def made(engine, job, uses_of):
            engine.wait_ge(job_full[BANK[job]], uses_of[job] + 1)

        def copied_out(engine, job, uses_of):
            engine.wait_ge(job_free[BANK[job]], uses_of[job] + 1)

        x_tiled = x.rearrange("b (s p) d -> p (b s) d", p=P)
        summed_rows = summed.rearrange("(p t) d -> p t d", p=P)
        out_rows = out.rearrange("b s d -> (b s) d").rearrange("(p t) d -> p t d", p=P)
        N_WEIGHTS = 13
        QT = TILES // 4

        @block.sync
        def _(sp):
            sp.dma_start(x_pair[:], x_tiled[:, 0:4]).then_inc(x_pair_in, 16)
            loads = [(wq_nat[:], Wq), (wl[:], Wl), (wk_nat[:], Wk),
                     (wv[0:LATENT], Wv), (wo[:], Wo), (wg[:], Wg),
                     (bias_rows[:, 0], bq.unsqueeze(0)), (bias_rows[:, 1], bk.unsqueeze(0)),
                     (wv[LATENT:LATENT + 1], bv.unsqueeze(0)),
                     (bo_all[:], bo.unsqueeze(0).to_broadcast([P, D])),
                     (b2_all[:], b2.rearrange("e h -> (e h)").unsqueeze(0).to_broadcast([P, EXPERTS * D])),
                     (bl_col[:], bl.unsqueeze(1)),
                     (b1_rows[:], b1.rearrange("e (c f) -> (e c) f", f=P))]
            assert len(loads) == N_WEIGHTS
            for dst, src in loads:
                sp.dma_start(dst, src).then_inc(weights_in, 16)

            def store_split(pair):
                for cut, parts, dram in ((q_cut, (q_hi, q_hi, q_lo), q_split), (k_cut, (k_hi, k_lo, k_hi), k_split)):
                    sp.wait_ge(cut, pair + 1)
                    for t, part in enumerate(parts):
                        sp.dma_start(dram[pair, :, t].rearrange("r d g s i -> r (d g s i)"),
                                     part[:].bitcast(F32)).then_inc(split_stored, 16)

            def load_k(pair, side):
                for r in range(NR):
                    sp.dma_start(k_first[32 * r + DH:32 * r + 32, side].rearrange("p g i -> p (g i)").bitcast(F32),
                                 k_split[pair, r, :, :, :, side].rearrange("t d g i -> (t d) g i")
                                 ).then_inc(k_first_in[side], 16)

            def load_x(pair):
                sp.dma_start(x_pair[:], x_tiled[:, bass.ds(4 * pair, 4)]).then_inc(x_pair_in, 16)

            def load_q(pair, side, r):
                sp.dma_start(q_stack[32 * r + DH:32 * r + 32, side, r].rearrange("p g i -> p (g i)").bitcast(F32),
                             q_split[pair, r, :, :, :, side].rearrange("t d g i -> (t d) g i")).then_inc(q_in[r], 16)

            def load_shift(job, uses_of, side):
                r = int(job[3])
                copied_out(sp, job, uses_of)
                sp.dma_start(q_stack[32 * r:32 * r + 1, side, r].rearrange("p g i -> p (g i)").bitcast(F32),
                             shift_t[:, r, :].bitcast(F32)).then_inc(shift_in[r], 16)

            STORES = 16 * 2 * TERMS
            sp.wait_ge(consts_set, 6)
            store_split(0)
            in_prologue = numbers(PROLOGUE, [0, 0])
            copied_out(sp, "xT", in_prologue)
            load_x(1)
            sp.wait_ge(split_stored, STORES)
            for side in range(2):
                load_k(0, side)
                for r in range(NR):
                    if side:
                        sp.wait_ge(q_in[r], 16)
                    load_q(0, side, r)
            for r in range(3):
                load_shift(f"max{r}", in_prologue, 0)

            def half(h):
                load_shift("max3", h.uses, h.side)
                if h.prep:
                    store_split(h.n + 1)
                if h.nxt:
                    load_shift("max0", h.uses, h.after)
                if h.side and (type(h.n) is not int or h.n < PAIRS - 2):
                    copied_out(sp, "xT", h.side_0)
                    load_x(h.n + 2)
                if h.ahead:
                    if h.prep:
                        sp.wait_ge(split_stored, STORES * (h.n + 2))
                    sp.wait_ge(first_full, 16 * (h.b + 1))
                    sp.wait_ge(k_kept, h.b + 1)
                    load_k(h.n + 1, h.side)
                for r in range(NR):
                    if h.ahead:
                        sp.wait_ge(second_full, 16 * h.b + 4 * r + 4)
                        load_q(h.n + 1, h.side, r)
                    if r < 2 and h.nxt:
                        load_shift(f"max{r + 1}", h.uses, h.after)

            def load_expert(e, side):
                sp.dma_start(w1_buf[:, side], W1[e]).then_inc(w_in[side], 16)
                sp.dma_start(w2_buf[:, side], W2[e].rearrange("(c f) h -> f c h", f=P)).then_inc(w_in[side], 16)

            for side in range(2):
                load_expert(side, side)

            run_pairs(sp, half, last_pairs=2)

            sp.wait_ge(rows_scaled, TILES)
            sp.dma_start(summed.rearrange("(t p) d -> p t d", p=P), rows[:, :, 0:D]).then_inc(sum_out, 16)
            sp.wait_ge(gates_made, 1)
            sp.dma_start(x1_table.rearrange("(t p) d -> p t d", p=P), rows[:]).then_inc(table_out, 16)
            sp.wait_ge(found, 1)
            sp.dma_start(token_list.rearrange("(q e) (a b) -> (e a) q b", q=2, b=32), picked[:]).then_inc(list_out, 16)
            sp.wait_ge(list_out, 16)
            sp.dma_start(index[:], token_list.rearrange("e (p c) -> p e c", c=CHUNKS)).then_inc(index_in, 16)

            with sp.Fori(1, EXPERTS // 2) as n:
                for side in range(2):
                    sp.wait_ge(down_full, 4 * (n - 1) + 2 * (side + 1))
                    load_expert(2 * n + side, side)

            for side in range(2):
                sp.wait_ge(added[side], 16 * CHUNKS * EXPERTS // 2)
            for q in range(4):
                sp.dma_start(xc_all[:, q * QT:(q + 1) * QT], summed_rows[:, q * QT:(q + 1) * QT]).then_inc(f_in[q], 16)
            for q in range(4):
                sp.wait_ge(f_done, QT * (q + 1))
                sp.dma_start(out_rows[:, q * QT:(q + 1) * QT], xc_all[:, q * QT:(q + 1) * QT]).then_inc(f_out, 16)
            sp.wait_ge(f_out, 64)

        @block.gpsimd
        def _(pool):
            g = nc.gpsimd
            g.memset(ident[:], 0.0).then_inc(hi_done, 1)
            pool.wait_ge(hi_done, 1)
            g.affine_select(out=ident[:], in_=ident[:], compare_op=ALU.not_equal, fill=1.0, base=0,
                            pattern=[[-1, P]], channel_multiplier=1).then_inc(consts_set, 1)
            g.memset(ones[:], 1.0).then_inc(consts_set, 1)
            g.memset(eps_col[:], EPS).then_inc(consts_set, 1)
            g.memset(q_stack[:].bitcast(F32), 0.0).then_inc(consts_set, 1)
            g.memset(k_first[:].bitcast(F32), 0.0).then_inc(consts_set, 1)
            g.memset(v_ones[:], 0.0).then_inc(hi_done, 1)
            pool.wait_ge(hi_done, 2)
            g.memset(v_ones[:, :, :, :, DH:DH + 1], 1.0).then_inc(consts_set, 1)

            def split(uses_of):
                for job, full, hi, lo_, done in (("q", q_full, q_hi, q_lo, q_cut), ("k", k_full, k_hi, k_lo, k_cut)):
                    copied_out(pool, job, uses_of)
                    passed(pool, pool_waits)
                    g.tensor_tensor(lo_[:], full, hi[:].bitcast(F32), ALU.subtract).then_inc(done, 1)

            def copy_v(batch, side):
                passed(pool, pool_waits)
                src = v_stage[:, 2 * side:2 * side + 2].rearrange("p j (h d) -> p j h d", h=HEADS)
                g.tensor_copy(v_ones[:, side, :, :, 0:DH], src).then_inc(v_ready, 1)

            def keep_centred(batch):
                pool.wait_ge(centred, 2 * batch + 2)
                passed(pool, pool_waits)
                g.tensor_copy(xc_all[:, bass.ds(2 * batch, 2)], xc[:]).then_inc(xc_kept, 1)

            g.iota(part_i[:], pattern=[[0, 2]], base=0, channel_multiplier=1).then_inc(indices_set, 1)
            g.iota(col_i[:, 0], pattern=[[0, 16], [1, EXPERTS]], base=0, channel_multiplier=0).then_inc(indices_set, 1)
            g.iota(col_i[:, 1], pattern=[[1, 16], [0, EXPERTS]], base=0, channel_multiplier=0).then_inc(indices_set, 1)
            g.iota(iota32_i[:], pattern=[[1, 32]], base=0, channel_multiplier=0).then_inc(indices_set, 1)
            g.iota(token_i[:], pattern=[[P, TILES]], base=-ID_BASE, channel_multiplier=1).then_inc(indices_set, 1)
            g.memset(ones_b[:], 1.0).then_inc(indices_set, 1)
            pool.wait_ge(indices_set, 6)
            g.affine_select(out=upper_b[:], in_=ones_b[:], compare_op=ALU.is_gt, fill=0.0, base=0,
                            pattern=[[1, P]], channel_multiplier=-1).then_inc(indices_set, 1)

            in_prologue = numbers(PROLOGUE, [0, 0])
            split(in_prologue)
            copied_out(pool, "v", in_prologue)
            copy_v(0, 0)
            pool.wait_ge(weights_in, 16 * N_WEIGHTS)
            pool.wait_ge(rows_in, 16)
            g.tensor_tensor(rows[:, :, 0:D], rows[:, :, 0:D], bo_all[:].unsqueeze(1).to_broadcast([P, TILES, D]),
                            ALU.add).then_inc(rows_biased, 1)

            def half(h):
                if h.side == 0:
                    if h.prev:
                        pool.wait_ge(pv_done, 4 * h.b)
                    copy_v(h.b + 1, 1)
                    if h.prep:
                        split(h.uses)
                elif h.ahead:
                    pool.wait_ge(pv_done, 4 * h.b)
                    copied_out(pool, "v", h.side_0)
                    copy_v(h.b + 1, 0)
                if h.prev:
                    keep_centred(h.b - 1)

            run_pairs(pool, half)
            keep_centred(BATCHES - 1)

            for q in range(4):
                ts = slice(q * TILES // 4, (q + 1) * TILES // 4)
                pool.wait_ge(hot_b_made, q + 1)
                ids = token_id[:, ts].unsqueeze(2).unsqueeze(3).to_broadcast([P, TILES // 4, EXPERTS, 32])
                g.tensor_tensor(hot_b[:, ts], hot_b[:, ts], ids, ALU.mult).then_inc(hot_id_made, 1)


            pool.wait_ge(index_in, 16)
            pool.wait_ge(table_out, 16)
            pool.wait_ge(sum_out, 16)

            def gather(n, side, again):
                e = 2 * n + side
                if again:
                    pool.wait_ge(y_made, 8 * (e - 2) + 8)
                    passed(pool, pool_waits)
                g.tensor_copy(from_index[:, side], index[:, bass.ds(e, 1)].rearrange("p o c -> p (o c)")).then_inc(from_set, 1)
                pool.wait_ge(from_set, e + 1)
                passed(pool, pool_waits)
                for c in range(CHUNKS):
                    g.indirect_dma_start(taken[:, side, c], None, x1_table,
                                         bass.IndirectOffsetOnAxis(ap=from_index[:, side, c:c + 1], axis=0)
                                         ).then_inc(taken_in[2 * side + c // 4], 16)

            def scatter(n, side, first=False):
                e = 2 * n + side
                if not (type(n) is int and n == 0):
                    pool.wait_ge(added[side], 16 * CHUNKS * n)
                    passed(pool, pool_waits)
                g.tensor_copy(to_index[:, side], index[:, bass.ds(e, 1)].rearrange("p o c -> p (o c)")).then_inc(to_set, 1)
                pool.wait_ge(to_set, e + 1)
                if not first:
                    before = 16 * CHUNKS * (n if side == 0 else n + 1)
                    pool.wait_ge(added[1 - side], before)
                for c in range(CHUNKS):
                    pool.wait_ge(y_made, 8 * e + c + 1)
                    passed(pool, pool_waits)
                    g.indirect_dma_start(summed, bass.IndirectOffsetOnAxis(ap=to_index[:, side, c:c + 1], axis=0),
                                         y_out[:, side, c], None, compute_op=ALU.add).then_inc(added[side], 16)

            gather(0, 0, False)
            gather(0, 1, False)
            for side in range(2):
                scatter(0, side, first=(side == 0))
                gather(1, side, True)
            with pool.Fori(2, EXPERTS // 2) as n:
                for side in range(2):
                    scatter(n - 1, side)
                    gather(n, side, True)
            for side in range(2):
                scatter(EXPERTS // 2 - 1, side)

        @block.scalar
        def _(act):
            s = nc.scalar
            act.dma_start(rows[:, :, 0:D], x_tiled).then_inc(rows_in, 16)

            def evacuate(job, uses_of):
                if job not in ("xT", "latent", "k", "q", "v", "oT", "xcT"):
                    return
                made(act, job, uses_of)
                bank = ps_job[:, BANK[job]]
                if job == "xT":
                    ins = s.copy(xT[:], bank)
                elif job == "latent":
                    ins = s.activation(latT[0:LATENT], bank[0:LATENT], ACT.Identity, bias=bl_col[:, 0:1])
                elif job in ("k", "q"):
                    full, hi, col = (k_full, k_hi, bk_col) if job == "k" else (q_full, q_hi, bq_col)
                    s.activation(hi[:], bank, ACT.Identity, bias=col[:, 0:1])
                    ins = s.activation(full, bank, ACT.Identity, bias=col[:, 0:1])
                elif job == "v":
                    ins = s.copy(v_stage[:].rearrange("p a b -> p (a b)"), bank)
                elif job == "oT":
                    ins = s.copy(oT[:], bank[:, 0:SEQ])
                else:
                    ins = s.copy(xcT[:], bank[:, 0:SEQ])
                ins.then_inc(job_free[BANK[job]], 1)

            def keep_k(pair, side):
                act.wait_ge(k_first_in[side], 64 * (pair + 1))
                s.activation(k_second[:, side], k_first[:, side], ACT.Identity,
                             bias=shift_rows[:, 0:1]).then_inc(k_kept, 1)

            act.wait_ge(weights_in, 16 * N_WEIGHTS)
            act.wait_ge(bias_out, 1)
            act.wait_ge(shift_ones, 1 + NR)
            in_prologue = numbers(PROLOGUE, [0, 0])
            for job in PROLOGUE:
                evacuate(job, in_prologue)
            keep_k(0, 0)

            def half(h):
                for k in range(HEADS):
                    r, gg = divmod(k, NG)
                    head = 16 * h.b + k
                    if k in h.jobs:
                        job = h.jobs[k]
                        if job in ("k", "q"):
                            act.wait_ge(k_cut if job == "k" else q_cut, h.n + 1)
                            act.wait_ge(split_stored, 16 * 2 * TERMS * (h.n + 1))
                        if job == "v":
                            act.wait_ge(v_ready, h.b + 2)
                        evacuate(job, h.uses)
                    act.wait_ge(second_full, head + 1)
                    if gg == 0 and (h.prev or r >= 2):
                        act.wait_ge(pv_done, 4 * h.b + r - 1)
                    s.activation(probs[:, 4 * (r % 2) + gg], ps_second[:, k % 2], ACT.Exp,
                                 scale=SCALE).then_inc(exp_done, 1)
                    if k == 5 and h.nxt:
                        keep_k(h.after_pair, h.after)
                    if k == 11:
                        act.wait_ge(pv_done, 4 * h.b + 2)
                        if h.prev:
                            made(act, "norm1", h.uses)
                        s.copy(oT_raw[:, 0:2].rearrange("p r i -> p (r i)"),
                               ps_pv.rearrange("p r i -> p (r i)")).then_inc(o_copied, 1)

            run_pairs(act, half)
            at_end = numbers(TAIL_AT.values(), BASE_END)
            evacuate("oT", at_end)
            evacuate("xcT", at_end)

            act.wait_ge(var_kept, BATCHES)
            s.activation(rstd[:], var_all[:], ACT.Sqrt, bias=eps_col[:, 0:1]).then_inc(var_rooted, 1)
            act.wait_ge(rstd_made, 1)
            act.wait_ge(xc_kept, BATCHES)
            with act.Fori(0, TILES) as t:
                s.activation(rows[:, bass.ds(t, 1), 0:D].rearrange("p o d -> p (o d)"),
                             xc_all[:, bass.ds(t, 1)].rearrange("p o d -> p (o d)"),
                             ACT.Copy, scale=rstd[:, bass.ds(t, 1)]).then_inc(rows_scaled, 1)
            act.wait_ge(lg_made, 1)
            s.activation(rows[:, :, D:GATED], lg[:], ACT.Sigmoid).then_inc(gates_made, 1)

            def gelu(n, blk):
                for f in range(FBLK):
                    act.wait_ge(up_full, 16 * n + 4 * blk + f + 1)
                    if f == 0 and not (type(n) is int and blk < 2):
                        act.wait_ge(down_full, 4 * n + blk - 1)
                    passed(act, act_waits)
                    s.activation(hT[:, blk % 2, f], ps_up[:, f], ACT.Gelu,
                                 bias=b1_cols[:, bass.ds(FBLK * (2 * n + blk // 2) + f, 1)]).then_inc(gelu_done, 1)

            for blk in range(4):
                gelu(0, blk)
            with act.Fori(1, EXPERTS // 2) as n:
                for blk in range(4):
                    gelu(n, blk)

            for q in range(4):
                act.wait_ge(f_averaged, QT * (q + 1))
                s.activation(f_sd[:, q * QT:(q + 1) * QT].unsqueeze(2), f_mv[:, q * QT:(q + 1) * QT, 1:2], ACT.Sqrt,
                             bias=eps_col[:, 0:1]).then_inc(f_rooted, 1)

        @block.tensor
        def _(pe):
            t_ = nc.tensor
            pe.wait_ge(weights_in, 16 * N_WEIGHTS)
            pe.wait_ge(consts_set, 2)
            pe.wait_ge(perm_done, 4)
            pe.wait_ge(latent_one, 1)
            for i in range(2):
                t_.matmul(ps_pv[:, 0, i:i + 1], bias_perm[:, i], ones[0:1, 0:1], start=True, stop=True)
            t_.transpose(ps_pv[:, 0, 32:32 + EXPERTS * FBLK], b1_rows[:],
                         ident[0:EXPERTS * FBLK, 0:EXPERTS * FBLK]).then_inc(bias_made, 1)

            def run_job(job, uses_of, batch, tail_batch=None):
                last_free(pe, job, uses_of)
                if job in READS:
                    copied_out(pe, READS[job], uses_of)
                if job == "oT":
                    copied_out(pe, "norm1", uses_of)
                bank = ps_job[:, BANK[job]]
                if job == "xT":
                    pe.wait_ge(x_pair_in, 16 * (batch + 1))
                    for c in range(4):
                        mm = t_.transpose(bank[:, c * P:(c + 1) * P], x_pair[:, c], ident[:])
                elif job == "latent":
                    mm = t_.matmul(bank[0:LATENT, :], wl[:], xT[:], start=True, stop=True)
                elif job == "k":
                    mm = t_.matmul(bank, wk[:], latT[0:LATENT], start=True, stop=True)
                elif job == "q":
                    mm = t_.matmul(bank, wq[:], xT[:], start=True, stop=True)
                elif job == "v":
                    for c in range(4):
                        o = bank[:, c * D:(c + 1) * D]
                        mm = t_.matmul(o, latT[:, c * P:(c + 1) * P], wv[:], start=True, stop=True)
                elif job.startswith("max"):
                    r = int(job[3])
                    pe.wait_ge(first_free, 16 * batch + 4 * (r + 1))
                    mm = t_.transpose(bank[0:2 * NG, 0:P], row_max[:, r], ident[:])
                elif job.startswith("norm"):
                    i = int(job[4])
                    pe.wait_ge(o_copied, 2 * tail_batch + 2)
                    for r in range(NR):
                        mm = t_.transpose(bank[:, r * P:(r + 1) * P], oT_raw[:, r, i * P:(i + 1) * P], ident[:])
                elif job == "oT":
                    for i in range(2):
                        mm = t_.transpose(bank[:, i * P:(i + 1) * P], o_nat[:, i], ident[:])
                elif job == "y":
                    for i in range(2):
                        o = bank[:, i * D:(i + 1) * D]
                        mm = t_.matmul(o, oT[:, i * P:(i + 1) * P], wo[:], start=True, stop=True)
                elif job == "xcT":
                    pe.wait_ge(centred, 2 * tail_batch + 2)
                    for i in range(2):
                        mm = t_.transpose(bank[:, i * P:(i + 1) * P], xc[:, i], ident[:])
                else:
                    for i in range(2):
                        mm = t_.matmul(bank[:, i * EXPERTS:(i + 1) * EXPERTS], xcT[:, i * P:(i + 1) * P], wg[:],
                                       start=True, stop=True)
                mm.then_inc(job_full[BANK[job]], 1)

            def first_pass(batch, side, pair, k, fresh):
                r, gg = divmod(k, NG)
                if k == 0:
                    pe.wait_ge(k_first_in[side], 64 * (pair + 1))
                if gg == 0:
                    pe.wait_ge(q_in[r], 16 * (batch + 1))
                if not (fresh and k < 3):
                    pe.wait_ge(first_free, 16 * batch + k - FIRST_AGO[k] + 1)
                for i in range(2):
                    o = ps_first[:, FIRST_BANK[k], i * SEQ:(i + 1) * SEQ]
                    mm = t_.matmul(o, q_stack[:, side, r, gg, i * P:(i + 1) * P], k_first[:, side, gg],
                                   start=True, stop=True)
                mm.then_inc(first_full, 1)

            def pv(batch, side, r):
                for j in range(2):
                    for gg in range(NG):
                        mm = t_.matmul(ps_pv[32 * gg:32 * gg + 32, r % 2], v_ones[:, side, j, NR * r + gg],
                                       probs[:, 4 * (r % 2) + gg, j * SEQ:(j + 1) * SEQ],
                                       start=(j == 0), stop=(j == 1), tile_position=(0, 32 * gg))
                mm.then_inc(pv_done, 1)

            in_prologue = numbers(PROLOGUE, [0, 0])
            for job in PREP_AT.values():
                run_job(job, in_prologue, 0)
            pe.wait_ge(bias_out, 1)
            for k in range(HEADS):
                if k in MAX_AT and MAX_AT[k] != "max3":
                    run_job(MAX_AT[k], in_prologue, 0)
                first_pass(0, 0, 0, k, True)

            def half(h):
                for k in range(HEADS):
                    r, gg = divmod(k, NG)
                    if k in h.jobs:
                        job = h.jobs[k]
                        if job == "xT":
                            run_job(job, h.uses, h.n + 1)
                        elif job == "max3":
                            run_job(job, h.uses, h.b)
                        else:
                            run_job(job, h.uses, h.b + 1, h.b - 1)
                    if h.nxt:
                        first_pass(h.b + 1, h.after, h.after_pair, k, False)
                    if k == 0:
                        pe.wait_ge(k_kept, h.b + 1)
                    if gg == 0:
                        pe.wait_ge(shift_in[r], 16 * (h.b + 1))
                    if h.prev or k >= 2:
                        pe.wait_ge(exp_done, 16 * h.b + k - 1)
                    for j in range(2):
                        mm = t_.matmul(ps_second[:, k % 2, j * SEQ:(j + 1) * SEQ],
                                       k_second[:, h.side, gg, j * P:(j + 1) * P],
                                       q_stack[:, h.side, r, gg], start=True, stop=True)
                    mm.then_inc(second_full, 1)
                    if k == 2 and h.prev:
                        pe.wait_ge(exp_done, 16 * h.b)
                        pv(h.b - 1, 1 - h.side, 3)
                    if k in (6, 10, 14):
                        group = k // 4 - 1
                        pe.wait_ge(exp_done, 16 * h.b + 4 * (group + 1))
                        if group == 0:
                            pe.wait_ge(v_ready, h.b + 1)
                            if h.prev:
                                pe.wait_ge(o_copied, 2 * h.b)
                        if group == 2:
                            pe.wait_ge(o_copied, 2 * h.b + 1)
                        pv(h.b, h.side, group)

            run_pairs(pe, half)
            pe.wait_ge(exp_done, 16 * BATCHES)
            pv(BATCHES - 1, 1, 3)
            at_end = numbers(TAIL_AT.values(), BASE_END)
            for job in TAIL_AT.values():
                run_job(job, at_end, None, BATCHES - 1)

            dv = [0]

            def dve_step(n=1):
                dv[0] += n
                pe.wait_ge(dve_a, dv[0])

            dve_step()
            for i in range(2):
                mm = t_.transpose(ps_a[:, i * P:(i + 1) * P], lg[:, 16 * i:16 * i + 16].rearrange("p t e -> p (t e)"), ident[:])
            mm.then_inc(pe_a, 1)
            dve_step()
            t_.transpose(ps_pv[0:1, 0, 0:P], abs_col[:], ident[:]).then_inc(pe_a, 1)
            dve_step()
            t_.matmul(ps_a[:, 0:1], ones[0:1, :], bound[:], start=True, stop=True).then_inc(pe_a, 1)
            for n in range(SEARCH_STEPS):
                pe.wait_ge(counted, 3 * n + 3)
                t_.matmul(ps_pv[:, 0, 0:3], same_e[:], counts[:], start=True, stop=True).then_inc(totalled, 1)
            dve_step()
            t_.matmul(ps_a[:, 0:2 * EXPERTS], ones[:], lo_hi[:].rearrange("p a e -> p (a e)"), start=True,
                      stop=True).then_inc(pe_a, 1)
            dve_step()
            t_.matmul(ps_pv[:, 0, 0:EXPERTS], ones_b[:], gt_sum[:], start=True, stop=True).then_inc(pe_a, 1)

            def prefix(mask, which):
                flat = mask[:].rearrange("p t e -> p (t e)")
                for i in range(2):
                    mm = t_.matmul(ps_pv[:, 1, i:i + 1], flat[:, i * P:(i + 1) * P], ones_b[:, 0:1], start=True, stop=True)
                mm.then_inc(pe_a, 1)
                dve_step()
                t_.matmul(ps_a[:, 0:NPART], upper_b[:], flat, start=True, stop=False, skip_group_check=True)
                first = tile_sum[:, which, 0:1].to_broadcast([P, P])
                second = tile_sum[:, which, 1:2].to_broadcast([P, P])
                t_.matmul(ps_a[:, 0:P], first, before_b[:], start=False, stop=False, skip_group_check=True)
                t_.matmul(ps_a[:, P:2 * P], first, same_eb[:], start=False, stop=False, skip_group_check=True)
                t_.matmul(ps_a[:, P:2 * P], second, before_b[:], start=False, stop=True,
                          skip_group_check=True).then_inc(pe_a, 1)

            dve_step()
            prefix(tie, 0)
            dve_step()
            prefix(sel, 1)
            for t in range(TILES):
                if t % (TILES // 4) == 0:
                    pe.wait_ge(hot_a_made, t // (TILES // 4) + 1)
                    pe.wait_ge(hot_id_made, t // (TILES // 4) + 1)
                for q in range(2):
                    mm = t_.matmul(ps_second[:, q, 0:P], hot_a[:, t, 4 * q:4 * q + 4].rearrange("p e s -> p (e s)"),
                                   hot_b[:, t, 4 * q:4 * q + 4].rearrange("p e s -> p (e s)"),
                                   start=(t == 0), stop=(t == TILES - 1))
            mm.then_inc(pe_a, 1)

            def turn(n, blk):
                side, hb = divmod(blk, 2)
                pe.wait_ge(taken_in[blk], 64 * (n + 1))
                if not (type(n) is int and n == 0 and blk == 0):
                    pe.wait_ge(turned_copied, 4 * n + blk)
                for c in range(4):
                    mm = t_.transpose(ps_turn[:, c * P:(c + 1) * P], taken[:, side, 4 * hb + c, 0:D], ident[:])
                mm.then_inc(turned, 1)

            def up(n, blk):
                side = blk // 2
                if blk % 2 == 0:
                    pe.wait_ge(w_in[side], 32 * (n + 1))
                pe.wait_ge(turned_copied, 4 * n + blk + 1)
                for f in range(FBLK):
                    if not (type(n) is int and n == 0 and blk == 0):
                        pe.wait_ge(gelu_done, 16 * n + 4 * blk + f - 3)
                    t_.matmul(ps_up[:, f], w1_buf[:, side, f * P:(f + 1) * P], takenT[:, blk % 2],
                              start=True, stop=True).then_inc(up_full, 1)

            def down(n, blk, early):
                side = blk // 2
                pe.wait_ge(gelu_done, 16 * n + 4 * blk + 4)
                if not early:
                    pe.wait_ge(y_summed, 4 * n + blk - 1)
                for c in range(4):
                    for f in range(FBLK):
                        mm = t_.matmul(ps_second[:, blk % 2, c * P:(c + 1) * P], hT[:, blk % 2, f, c * P:(c + 1) * P],
                                       w2_buf[:, side, f], start=(f == 0), stop=(f == FBLK - 1))
                mm.then_inc(down_full, 1)

            pe.wait_ge(found, 1)
            for blk in range(4):
                turn(0, blk)
                if blk:
                    down(0, blk - 1, blk < 3)
                up(0, blk)
            with pe.Fori(1, EXPERTS // 2) as n:
                for blk in range(4):
                    turn(n, blk)
                    if blk:
                        down(n, blk - 1, False)
                    else:
                        down(n - 1, 3, False)
                    up(n, blk)
            down(EXPERTS // 2 - 1, 3, False)

        @block.vector
        def _(dve):
            v = nc.vector
            v.memset(latT[LATENT:LATENT + 1], 1.0).then_inc(latent_one, 1)
            v.memset(shift_rows[:], 0.0).then_inc(shift_ones, 1)
            dve.wait_ge(shift_ones, 1)
            dve.wait_ge(weights_in, 16 * N_WEIGHTS)
            for nat, perm in ((wq_nat[:], wq[:]), (wk_nat[:], wk[:]), (bias_rows[:, 0], bias_perm[:, 0]),
                              (bias_rows[:, 1], bias_perm[:, 1])):
                v.tensor_copy(perm.rearrange("p (r d g) -> p r d g", r=NR, g=NG),
                              nat.rearrange("p (r g d) -> p r d g", r=NR, g=NG)).then_inc(perm_done, 1)
            for r in range(NR):
                v.memset(shift_rows[32 * r:32 * r + 1], 1.0).then_inc(shift_ones, 1)
            dve.wait_ge(bias_made, 1)
            v.tensor_copy(bq_col[:], ps_pv[:, 0, 0:1])
            v.tensor_copy(bk_col[:], ps_pv[:, 0, 1:2])
            v.tensor_copy(b1_cols[:], ps_pv[:, 0, 32:32 + EXPERTS * FBLK]).then_inc(bias_out, 1)

            def take_maxima(batch, k):
                r, gg = divmod(k, NG)
                dve.wait_ge(first_full, 16 * batch + k + 1)
                v.tensor_reduce(row_max[:, r, 2 * gg:2 * gg + 2],
                                ps_first[:, FIRST_BANK[k]].rearrange("p (i j) -> p i j", i=2),
                                AX, ALU.max).then_inc(first_free, 1)

            def evacuate(job, uses_of, batch, tail):
                if job in ("xT", "latent", "k", "q", "v", "oT", "xcT"):
                    return
                made(dve, job, uses_of)
                bank = ps_job[:, BANK[job]]
                if job.startswith("max"):
                    r = int(job[3])
                    if not (type(batch) is int and batch == 0):
                        dve.wait_ge(shift_in[r], 16 * batch)
                    ins = v.tensor_scalar(shift_t[:, r], bank[0:2 * NG, 0:P], -1.0, None, ALU.mult)
                elif job.startswith("norm"):
                    i = int(job[4])
                    heads = bank.rearrange("p (h c) -> p h c", c=32)
                    v.reciprocal(den[:, i].unsqueeze(2), heads[:, :, DH:DH + 1]).then_inc(den_done, 1)
                    dve.wait_ge(den_done, 2 * tail + i + 1)
                    ins = v.tensor_tensor(o_nat[:, i].rearrange("p (h d) -> p h d", d=DH), heads[:, :, 0:DH],
                                          den[:, i].unsqueeze(2).to_broadcast([P, HEADS, DH]), ALU.mult)
                elif job == "y":
                    if not (type(tail) is int and tail == 0):
                        dve.wait_ge(centred, 2 * tail)
                    else:
                        dve.wait_ge(rows_biased, 1)
                    ins = v.tensor_tensor(resid[:], bank[:, 0:2 * D].rearrange("p (i d) -> p i d", i=2),
                                          rows[:, bass.ds(2 * tail, 2), 0:D], ALU.add)
                else:
                    ins = v.tensor_copy(logits[:, bass.ds(2 * tail, 2)],
                                        bank[:, 0:2 * EXPERTS].rearrange("p (i e) -> p i e", i=2))
                ins.then_inc(job_free[BANK[job]], 1)

            def finish(stage, uses_of, tail):
                if stage == 0:
                    copied_out(dve, "y", uses_of)
                    for i in range(2):
                        v.bn_stats(stats[:, i], resid[:, i]).then_inc(stats_done, 1)
                elif stage == 1:
                    dve.wait_ge(stats_done, 2 * tail + 2)
                    passed(dve, dve_waits)
                    for i in range(2):
                        v.bn_aggr(mean_var[:, i], stats[:, i]).then_inc(mv_done, 1)
                else:
                    dve.wait_ge(mv_done, 2 * tail + 2)
                    if not (type(tail) is int and tail == 0):
                        dve.wait_ge(xc_kept, tail)
                    for i in range(2):
                        v.tensor_scalar(xc[:, i], resid[:, i], mean_var[:, i, 0:1], None,
                                        ALU.subtract).then_inc(centred, 1)
                    v.tensor_copy(var_all[:, bass.ds(2 * tail, 2)].unsqueeze(2), mean_var[:, :, 1:2]).then_inc(var_kept, 1)

            sent, chained = [0], [0]

            def for_pe(ins):
                sent[0] += 1
                ins.then_inc(dve_a, 1)
                dve.wait_ge(dve_a, sent[0])

            def link(ins):
                chained[0] += 1
                ins.then_inc(own, 1)
                dve.wait_ge(own, chained[0])

            for n in range(SEARCH_STEPS + 1):
                for j in range(4):
                    v.memset(quarters[:, n, j:j + 1], 0.5 * j * 0.25 ** n)
            dve.wait_ge(indices_set, 7)
            v.tensor_copy(iota32[:], iota32_i[:])
            v.tensor_copy(token_id[:], token_i[:])
            link(v.tensor_scalar(part_i[:, 0:1], part_i[:, 0:1], EXPERTS - 1, None, ALU.bitwise_and))
            link(v.tensor_scalar(part_i[:, 1:2], part_i[:, 1:2], 3, None, ALU.arith_shift_right))
            link(v.tensor_copy(part_f[:], part_i[:]))
            link(v.tensor_scalar(same_e[:], col_i[:, 0], part_f[:, 0:1], None, ALU.is_equal))
            link(v.tensor_copy(same_eb[:], same_e[:]))
            link(v.scalar_tensor_tensor(out=before_b[:], in0=col_i[:, 1], scalar=part_f[:, 1:2], in1=same_e[:],
                                        op0=ALU.is_gt, op1=ALU.mult))

            in_prologue = numbers(PROLOGUE, [0, 0])
            for k in range(HEADS):
                if k in MAX_AT and MAX_AT[k] != "max3":
                    evacuate(MAX_AT[k], in_prologue, 0, 0)
                take_maxima(0, k)

            def half(h):
                for k in range(HEADS):
                    if k in h.jobs:
                        job = h.jobs[k]
                        evacuate(job, h.uses, h.b if job == "max3" else h.b + 1, h.b - 1)
                    if h.nxt:
                        take_maxima(h.b + 1, k)
                    if k in (10, 11, 12) and h.prev:
                        finish(k - 10, h.uses, h.b - 1)
                    if k == 3 and h.prev:
                        dve.wait_ge(pv_done, 4 * h.b)
                        v.tensor_copy(oT_raw[:, 2:4], ps_pv).then_inc(o_copied, 1)

            run_pairs(dve, half)
            dve.wait_ge(pv_done, 4 * BATCHES)
            v.tensor_copy(oT_raw[:, 2:4], ps_pv).then_inc(o_copied, 1)
            at_end = numbers(TAIL_AT.values(), BASE_END)
            for job in TAIL_AT.values():
                evacuate(job, at_end, None, BATCHES - 1)
                if job == "y":
                    for stage in range(3):
                        finish(stage, at_end, BATCHES - 1)

            read = [0]

            def from_pe():
                read[0] += 1
                dve.wait_ge(pe_a, read[0])

            dve.wait_ge(var_rooted, 1)
            v.reciprocal(rstd[:], rstd[:]).then_inc(rstd_made, 1)
            dve.wait_ge(rstd_made, 1)
            v.tensor_tensor(lg[:], logits[:], rstd[:].unsqueeze(2).to_broadcast([P, TILES, EXPERTS]),
                            ALU.mult).then_inc(lg_made, 1)
            dve.wait_ge(lg_made, 1)
            for_pe(v.memset(abs_row[:], 0.0))
            from_pe()
            link(v.tensor_copy(lgT[:], ps_a[:, 0:2 * P]))
            for_pe(v.tensor_reduce(abs_col[:], lgT[:], AX, ALU.max, apply_absolute_value=True))
            from_pe()
            link(v.tensor_reduce(abs_row[:], ps_pv[0:1, 0, 0:P], AX, ALU.max))
            link(v.tensor_scalar(bound[:].bitcast(I32), abs_row[:].bitcast(I32), 0x7F800000, None, ALU.bitwise_and))
            for_pe(v.tensor_scalar(bound[:], bound[:], 2.0, 1e-30, ALU.mult, ALU.max))
            from_pe()
            link(v.tensor_copy(bound_col[:], ps_a[:, 0:1]))
            link(v.tensor_scalar(widths[:], quarters[:], bound_col[:, 0:1], None, ALU.mult))
            link(v.tensor_scalar(thr[:], widths[:, 0], bound_col[:, 0:1], None, ALU.subtract))
            for n in range(SEARCH_STEPS):
                for j in range(3):
                    v.tensor_scalar(hits[:, j], lgT[:], thr[:, j + 1:j + 2], None, ALU.is_ge, ALU.add,
                                    accum_out=counts[:, j:j + 1]).then_inc(counted, 1)
                v.tensor_scalar(next_thr[:], widths[:, n + 1], thr[:, 0:1], None, ALU.add).then_inc(thr_made, 1)
                dve.wait_ge(totalled, n + 1)
                link(v.tensor_scalar(above[:], ps_pv[:, 0, 0:3], CAPACITY - 0.5, None, ALU.is_ge, ALU.add,
                                     accum_out=n_above[:]))
                link(v.scalar_tensor_tensor(out=thr[:], in0=widths[:, n, 1:2].to_broadcast([P, 4]), scalar=n_above[:, 0:1],
                                            in1=next_thr[:], op0=ALU.mult, op1=ALU.add))

            link(v.scalar_tensor_tensor(out=hi_col[:], in0=widths[:, SEARCH_STEPS, 1:2], scalar=4.0, in1=thr[:, 0:1],
                                        op0=ALU.mult, op1=ALU.add))
            link(v.tensor_scalar(lo_hi[:, 0], ident[:, 0:EXPERTS], thr[:, 0:1], None, ALU.mult))
            for_pe(v.tensor_scalar(lo_hi[:, 1], ident[:, 0:EXPERTS], hi_col[:, 0:1], None, ALU.mult))
            from_pe()
            link(v.tensor_copy(bounds[:].rearrange("p a e -> p (a e)"), ps_a[:, 0:2 * EXPERTS]))
            wide = [P, TILES, EXPERTS]
            link(v.tensor_tensor(gt[:], lg[:], bounds[:, 1].unsqueeze(1).to_broadcast(wide), ALU.is_ge))
            with nc.allow_low_precision("counts up to 32 are exact in bfloat16"):
                for_pe(v.tensor_reduce(gt_sum[:], gt[:].rearrange("p t e -> p e t"), AX, ALU.add))
            link(v.tensor_tensor(ge[:], lg[:], bounds[:, 0].unsqueeze(1).to_broadcast(wide), ALU.is_ge))
            from_pe()
            link(v.tensor_copy(gt_all[:], ps_pv[:, 0, 0:EXPERTS]))
            for_pe(v.tensor_tensor(tie[:], ge[:], gt[:], ALU.subtract))
            from_pe()
            for_pe(v.tensor_copy(tile_sum[:, 0], ps_pv[:, 1, 0:2]))
            from_pe()
            ranks = ps_a[:, 0:NPART].rearrange("p (t e) -> p t e", e=EXPERTS)
            link(v.tensor_tensor(rank[:], ranks, gt_all[:].unsqueeze(1).to_broadcast(wide), ALU.add))
            link(v.scalar_tensor_tensor(out=ge[:], in0=rank[:], scalar=CAPACITY - 0.5, in1=tie[:],
                                        op0=ALU.is_lt, op1=ALU.mult))
            for_pe(v.tensor_tensor(sel[:], gt[:], ge[:], ALU.add))
            link(v.tensor_scalar(off_slot[:], sel[:].rearrange("p t e -> p (t e)"), float(TOKENS), -float(TOKENS),
                                 ALU.mult, ALU.add))
            from_pe()
            for_pe(v.tensor_copy(tile_sum[:, 1], ps_pv[:, 1, 0:2]))
            from_pe()
            link(v.tensor_tensor(slot[:], ps_a[:, 0:NPART], off_slot[:], ALU.add))
            link(v.tensor_scalar(slot_a[:], slot[:], 5, None, ALU.arith_shift_right))
            link(v.tensor_scalar(slot_b[:], slot[:], 31, None, ALU.bitwise_and))
            for q in range(4):
                ts = slice(q * TILES // 4, (q + 1) * TILES // 4)
                cols = slice(q * NPART // 4, (q + 1) * NPART // 4)
                shape = [P, NPART // 4, 32]
                for hot, part, done in ((hot_a, slot_a, hot_a_made), (hot_b, slot_b, hot_b_made)):
                    v.tensor_tensor(hot[:, ts].rearrange("p t e s -> p (t e) s"), iota32[:].unsqueeze(1).to_broadcast(shape),
                                    part[:, cols].unsqueeze(2).to_broadcast(shape), ALU.is_equal).then_inc(done, 1)
            from_pe()
            for e in range(4):
                ins = v.tensor_scalar(picked[32 * e:32 * e + 32], ps_second[32 * e:32 * e + 32, :, 32 * e:32 * e + 32],
                                      float(ID_BASE), None, ALU.add)
            ins.then_inc(found, 1)

            def normalise(q):
                part = slice(QT * q, QT * (q + 1))
                dve.wait_ge(f_rooted, q + 1)
                v.reciprocal(f_rstd[:, part], f_sd[:, part]).then_inc(f_inverted, 1)
                dve.wait_ge(f_inverted, q + 1)
                for t in range(QT * q, QT * (q + 1)):
                    v.tensor_scalar(xc_all[:, t], xc_all[:, t], f_mv[:, t, 0:1], f_rstd[:, t:t + 1], ALU.subtract,
                                    ALU.mult).then_inc(f_done, 1)

            def copy_turned(n, blk):
                dve.wait_ge(turned, 4 * n + blk + 1)
                v.tensor_copy(takenT[:, blk % 2], ps_turn).then_inc(turned_copied, 1)

            def gate(n, blk):
                side, hb = divmod(blk, 2)
                e = 2 * n + side
                dve.wait_ge(down_full, 4 * n + blk + 1)
                b2_rows = b2_all[:, bass.ds(e, 1)].to_broadcast([P, 4, D])
                v.tensor_tensor(y_sum[:, blk % 2], ps_second[:, blk % 2].rearrange("p (c d) -> p c d", c=4), b2_rows,
                                ALU.add).then_inc(y_summed, 1)
                dve.wait_ge(y_summed, 4 * n + blk + 1)
                if hb == 0 and not (type(n) is int and n == 0):
                    dve.wait_ge(added[side], 16 * CHUNKS * n)
                for c in range(4):
                    ch = 4 * hb + c
                    v.tensor_scalar(y_out[:, side, ch], y_sum[:, blk % 2, c], taken[:, side, ch, bass.ds(D + e, 1)],
                                    None, ALU.mult).then_inc(y_made, 1)

            for blk in range(4):
                copy_turned(0, blk)
                if blk:
                    gate(0, blk - 1)
            with dve.Fori(1, EXPERTS // 2) as n:
                for blk in range(4):
                    copy_turned(n, blk)
                    if blk:
                        gate(n, blk - 1)
                    else:
                        gate(n - 1, 3)
            gate(EXPERTS // 2 - 1, 3)

            for q in range(4):
                dve.wait_ge(f_in[q], 16)
                for t in range(QT * q, QT * (q + 1)):
                    v.bn_stats(f_stats[:, t], xc_all[:, t]).then_inc(f_statted, 1)
                dve.wait_ge(f_statted, QT * (q + 1))
                for t in range(QT * q, QT * (q + 1)):
                    v.bn_aggr(f_mv[:, t], f_stats[:, t]).then_inc(f_averaged, 1)
                if q:
                    normalise(q - 1)
            normalise(3)


_INS = ['L0_attn_x', 'L0_attn_Wq', 'L0_attn_bq', 'L0_attn_Wl', 'L0_attn_bl', 'L0_attn_Wk', 'L0_attn_bk',
        'L0_attn_Wv', 'L0_attn_bv', 'L0_attn_Wo', 'L0_attn_bo', 'L0_ffn_Wg', 'L0_ffn_W1', 'L0_ffn_b1',
        'L0_ffn_W2', 'L0_ffn_b2']


def kernel(**inputs):
    import numpy as _np
    import concourse.bacc as _bacc
    from concourse import mybir as _mybir
    from concourse.bass_utils import run_bass_kernel_spmd as _run

    nc = _bacc.Bacc("TRN2", target_bir_lowering=False, num_devices=1)
    arrays, args = {}, []
    for name in _INS:
        a = _np.ascontiguousarray(inputs[name])
        arrays[f"in_{name}"] = a
        args.append(nc.dram_tensor(f"in_{name}", a.shape, _mybir.dt.from_np(a.dtype), kind="ExternalInput").ap())
    out = nc.dram_tensor("out", (BATCHES, SEQ, D), F32, kind="ExternalOutput").ap()
    post_ln_layer(nc, *args, out)
    return _run(nc, [arrays], core_ids=[0]).results[0]["out"]
```

```python
from contextlib import ExitStack

import concourse.bass as bass
from concourse import mybir

P = 128
ALU = mybir.AluOpType
ACT = mybir.ActivationFunctionType
AX = mybir.AxisListType.X
F32 = mybir.dt.float32
F32R = mybir.dt.float32r
BF16 = mybir.dt.bfloat16
F16 = mybir.dt.float16
I32 = mybir.dt.int32
U32 = mybir.dt.uint32

BATCHES, SEQ, D = 16, 256, 128
HEADS, DH, LATENT = 16, 8, 32
EXPERTS, FF = 8, 512
TOKENS = BATCHES * SEQ
CAPACITY = TOKENS * 2 // EXPERTS
TILES = TOKENS // P
PAIRS = BATCHES // 2
NPART = TILES * EXPERTS
SCALE = DH ** -0.5
EPS = 1e-5
NR = NG = 4
TERMS = 3
GATED = D + EXPERTS
CHUNKS = CAPACITY // P
SEARCH_STEPS = 12
FBLK = FF // P
GROUPS = [(0, 2), (2, 6)]
HOT_TILES = [16, 4]
HOT_PARTS = [TILES // tiles for tiles in HOT_TILES]
EARLY_TURN = (1, 6)
BLOCKS = [[(0, 2)], [(2, 4), (6, 2)]]
TURN_CHUNK = 3
ID_BASE = TOKENS // 2

PREP_AT = {0: "latent", 4: "q", 2: "k", 12: "v"}
TURN_AT = {12: "xT"}
MAX_AT = {1: "max3", 8: "max0", 11: "max1", 13: "max2"}
TAIL_AT = {5: "norm", 7: "oT", 9: "y", 14: "xcT", 15: "logits"}
BANK = {"first_xT": 0, "latent": 0, "q": 1, "k": 0, "max3": 1, "norm": 0, "max0": 0, "oT": 1, "y": 1, "max1": 0,
        "v": 1, "xT": 1, "max2": 0, "xcT": 1, "logits": 0}
READS = {"k": "latent", "v": "latent", "oT": "norm", "y": "oT", "logits": "xcT"}
OFFSET, SLOT = [0, DH + 1, 2 * (DH + 1), 0], [0, 0, 0, 1]
FIRST_BANK = [k % 3 for k in range(HEADS - 1)] + [1]
FIRST_AGO = [next(a for a in range(1, 5) if FIRST_BANK[(k - a) % HEADS] == FIRST_BANK[k]) for k in range(HEADS)]


def half_jobs(prep, turn, nxt, tail):
    jobs = {}
    if prep:
        jobs.update(PREP_AT)
    if turn:
        jobs.update(TURN_AT)
    jobs.update({s: j for s, j in MAX_AT.items() if nxt or j == "max3"})
    if tail:
        jobs.update(TAIL_AT)
    return sorted(jobs.items())


def uses(jobs):
    return [sum(BANK[j] == bank for j in jobs) for bank in range(2)]


PROLOGUE = ["first_xT", "latent", "q", "k", "v", "xT", "max0", "max1", "max2"]
FIRST = [half_jobs(True, False, True, False), half_jobs(False, True, True, True)]
MIDDLE = [half_jobs(True, False, True, True), half_jobs(False, True, True, True)]
LAST_BUT_ONE = [half_jobs(True, False, True, True), half_jobs(False, False, True, True)]
LAST = [half_jobs(False, False, True, True), half_jobs(False, False, False, True)]
N_FIRST, N_MIDDLE, N_LAST_BUT_ONE, N_LAST = (
    uses([j for h in body for _, j in h]) for body in (FIRST, MIDDLE, LAST_BUT_ONE, LAST))
BASE_FIRST = uses(PROLOGUE)
BASE_MIDDLE = [b + n for b, n in zip(BASE_FIRST, N_FIRST)]
BASE_LAST_BUT_ONE = [b + (PAIRS - 3) * n for b, n in zip(BASE_MIDDLE, N_MIDDLE)]
BASE_LAST = [b + n for b, n in zip(BASE_LAST_BUT_ONE, N_LAST_BUT_ONE)]
BASE_END = [b + n for b, n in zip(BASE_LAST, N_LAST)]


def numbers(jobs, base):
    base, out = list(base), {}
    for job in jobs:
        out[job] = base[BANK[job]]
        base[BANK[job]] = base[BANK[job]] + 1
    return out


def bank_1_uses_after_xT(jobs):
    jobs = list(jobs)
    return sum(BANK[j] == 1 for j in jobs[jobs.index("xT") + 1:])


class Half:

    def __init__(self, n, side):
        first, last_but_one, last = (type(n) is int and n == k for k in (0, PAIRS - 2, PAIRS - 1))
        self.n, self.side, self.b = n, side, 2 * n + side
        self.prep = side == 0 and not last
        self.nxt = not (last and side == 1)
        self.prev = not (first and side == 0)
        self.ahead = not last
        self.turn = side == 0 and not (last_but_one or last)
        body = FIRST if first else LAST_BUT_ONE if last_but_one else LAST if last else MIDDLE
        base = BASE_FIRST if first else BASE_LAST_BUT_ONE if last_but_one else BASE_LAST if last else [
            b + (n - 1) * k for b, k in zip(BASE_MIDDLE, N_MIDDLE)]
        self.turned_before = base[1] - bank_1_uses_after_xT(PROLOGUE if first else [j for _, j in MIDDLE[1]])
        before = uses([j for _, j in body[0]]) if side else [0, 0]
        self.side_0 = numbers([j for _, j in body[0]], base)
        self.uses = numbers([j for _, j in body[side]], [b + k for b, k in zip(base, before)])
        self.jobs = dict(body[side])
        self.after = (side + 1) % 2
        self.after_pair = n + side


class Count:

    def __init__(self):
        self.value = 0

    def next(self):
        self.value += 1
        return self.value


def passed(engine, waits):
    engine.sem_inc(waits, 1)


def run_pairs(engine, body):
    for side in range(2):
        body(Half(0, side))
    with engine.Fori(1, PAIRS - 2) as n:
        for side in range(2):
            body(Half(n, side))
    for n in (PAIRS - 2, PAIRS - 1):
        for side in range(2):
            body(Half(n, side))


def post_ln_layer(nc, x, Wq, bq, Wl, bl, Wk, bk, Wv, bv, Wo, bo, Wg, W1, b1, W2, b2, out):
    with ExitStack() as ctx:
        def sb(name, shape, dt=F32):
            return ctx.enter_context(nc.sbuf_tensor(name, shape, dt))

        def psum(name, shape):
            return ctx.enter_context(nc.psum_tensor(name, shape, F32))

        def sem(name):
            return ctx.enter_context(nc.semaphore(name))

        q_split = nc.dram_tensor("q_split", [PAIRS, NR, TERMS, DH, NG, 2, SEQ], F32, kind="Internal").ap()
        k_split = nc.dram_tensor("k_split", [PAIRS, NR, TERMS, DH, NG, 2, SEQ], F32, kind="Internal").ap()
        x1_table = nc.dram_tensor("x1_table", [TOKENS, GATED], F32, kind="Internal").ap()
        summed = nc.dram_tensor("summed", [TOKENS, D], F32, kind="Internal").ap()

        banks = psum("banks", [P, 8, 512])
        ps_first, ps_job = banks[:, 0:3], banks[:, 3:5]
        ps_second = banks[:, 5:7]
        ps_pv = banks[:, 7].rearrange("p (r i) -> p r i", r=2)
        ps_up, ps_turn = banks[:, 0:4], banks[:, 4]
        ps_a = ps_job[:, 0]

        ident = sb("ident", [P, P])
        ones = sb("ones", [P, P])
        eps_col, warm = sb("eps_col", [P, 1]), sb("warm", [P, 1])
        wq_nat, wq = sb("wq_nat", [P, P]), sb("wq", [P, P])
        wk_nat, wk = sb("wk_nat", [LATENT, P]), sb("wk", [LATENT, P])
        wl, wv = sb("wl", [P, LATENT]), sb("wv", [LATENT + 1, P])
        wo, wg = sb("wo", [P, P]), sb("wg", [P, EXPERTS])
        bias_rows = sb("bias_rows", [1, 2, P])
        bo_all = sb("bo_all", [P, P])
        bias_perm = sb("bias_perm", [1, 2, P])
        bl_col = sb("bl_col", [LATENT, 1])
        bq_col, bk_col = sb("bq_col", [P, 1]), sb("bk_col", [P, 1])
        b1_rows, b1_cols = sb("b1_rows", [EXPERTS * FBLK, P]), sb("b1_cols", [P, EXPERTS * FBLK])
        b2_all = sb("b2_all", [P, EXPERTS, D])
        shift_rows = sb("shift_rows", [P, 1])

        rows = sb("rows", [P, TILES, GATED])
        x_pair, xT = sb("x_pair", [P, 4, D]), sb("xT", [P, 2 * SEQ])
        latT = sb("latT", [LATENT + 1, 2 * SEQ])
        kq_full = sb("kq_full", [P, 2, 2 * SEQ])
        k_full, q_full = kq_full[:, 0], kq_full[:, 1]
        k_hi, k_lo = sb("k_hi", [P, 2 * SEQ], F32R), sb("k_lo", [P, 2 * SEQ], F32R)
        q_hi, q_lo = sb("q_hi", [P, 2 * SEQ], F32R), sb("q_lo", [P, 2 * SEQ], F32R)
        v_stage = sb("v_stage", [P, 4, D])
        v_ones = sb("v_ones", [P, 2, 2, HEADS, 32])
        q_stack = sb("q_stack", [P, 2, NR, NG, SEQ], F32R)
        k_first = sb("k_first", [P, 2, NG, SEQ], F32R)
        k_second = sb("k_second", [P, 2, NG, SEQ], F32R)
        row_max = sb("row_max", [P, NR, 2 * NG])
        shift_t = sb("shift_t", [2 * NG, NR, P], F32R)
        probs = sb("probs", [P, 8, 2 * SEQ])
        oT_raw = sb("oT_raw", [P, 2, SEQ])
        den = sb("den", [P, 2, HEADS])
        o_nat, oT = sb("o_nat", [P, 2, D]), sb("oT", [P, SEQ])
        resid, xc = sb("resid", [P, 2, D]), sb("xc", [P, 2, D])
        stats, mean_var = sb("stats", [P, 2, 6]), sb("mean_var", [P, 2, 2])
        xcT = sb("xcT", [P, SEQ])
        xc_all = sb("xc_all", [P, TILES, D])
        var_all, rstd = sb("var_all", [P, TILES]), sb("rstd", [P, TILES])
        logits = sb("logits", [P, TILES, EXPERTS])

        late_in = sem("late_in")
        weights_in, consts_set, perm_done = sem("weights_in"), sem("consts_set"), sem("perm_done")
        bias_made, bias_out, warmed = sem("bias_made"), sem("bias_out"), sem("warmed")
        rows_in, x_pair_in = sem("rows_in"), sem("x_pair_in")
        job_full, job_free = [sem(f"job_full{i}") for i in range(2)], [sem(f"job_free{i}") for i in range(2)]
        b1_out = sem("b1_out")
        rows_biased, latent_one, k_kept = sem("rows_biased"), sem("latent_one"), sem("k_kept")
        hi_done, k_cut, q_cut = sem("hi_done"), sem("k_cut"), sem("q_cut")
        k_stored, q_stored = sem("k_stored"), sem("q_stored")
        q_in = [sem(f"q_in{r}") for r in range(NR)]
        k_first_in = [sem(f"k_first_in{s}") for s in range(2)]
        shift_in = [sem(f"shift_in{r}") for r in range(NR)]
        first_full, first_free = sem("first_full"), sem("first_free")
        second_full, exp_done = sem("second_full"), sem("exp_done")
        v_ready, pv_done, o_copied = sem("v_ready"), sem("pv_done"), sem("o_copied")
        o_scaled = sem("o_scaled")
        den_done, stats_done, mv_done = sem("den_done"), sem("stats_done"), sem("mv_done")
        pool_waits, act_waits, dve_waits = sem("pool_waits"), sem("act_waits"), sem("dve_waits")
        shift_ones, indices_set, linked_step = sem("shift_ones"), sem("indices_set"), sem("linked_step")
        var_kept, centred, xc_kept = sem("var_kept"), sem("centred"), sem("xc_kept")

        lg = sb("lg", [P, TILES, EXPERTS])
        lgT = sb("lgT", [P, 2 * P])
        abs_col, abs_row, bound = sb("abs_col", [P, 1]), sb("abs_row", [1, 1]), sb("bound", [1, 1])
        bound_col = sb("bound_col", [P, 1])
        quarters, widths = sb("quarters", [P, SEARCH_STEPS + 1, 4]), sb("widths", [P, SEARCH_STEPS + 1, 4])
        thr, next_thr = sb("thr", [P, 4]), sb("next_thr", [P, 4])
        counts = sb("counts", [P, 3], BF16)
        above, n_above = sb("above", [P, 3]), sb("n_above", [P, 1])
        lo_hi, bounds = sb("lo_hi", [P, 2, EXPERTS]), sb("bounds", [P, 2, EXPERTS])
        hi_col = sb("hi_col", [P, 1])
        part_i, col_i = sb("part_i", [P, 2], I32), sb("col_i", [P, 2, P], I32)
        part_f = sb("part_f", [P, 2])
        same_e, same_eb = sb("same_e", [P, P]), sb("same_eb", [P, P], BF16)
        before_b = sb("before_b", [P, P], BF16)
        upper_b, ones_b = sb("upper_b", [P, P], BF16), sb("ones_b", [P, P], BF16)
        gt, ge = sb("gt", [P, TILES, EXPERTS], BF16), sb("ge", [P, TILES, EXPERTS], BF16)
        tie, sel = sb("tie", [P, TILES, EXPERTS], BF16), sb("sel", [P, TILES, EXPERTS], BF16)
        gt_sum, gt_all = sb("gt_sum", [P, EXPERTS], BF16), sb("gt_all", [P, EXPERTS])
        tile_sum = sb("tile_sum", [P, 2, 2], BF16)
        rank = sb("rank", [P, TILES, EXPERTS])
        off_slot, slot = sb("off_slot", [P, NPART]), sb("slot", [P, NPART], I32)
        slot_a, slot_b = ([sb(f"{name}{g}", [P, TILES, n], I32) for g, (_, n) in enumerate(GROUPS)]
                          for name in ("slot_a", "slot_b"))
        iota32_i, iota32 = sb("iota32_i", [P, 32], I32), sb("iota32", [P, 32])
        token_i, token_id = sb("token_i", [P, TILES], I32), sb("token_id", [P, TILES])

        def by_group(flat):
            return [flat[:, TILES * 32 * first:TILES * 32 * (first + n)].rearrange("p (t e s) -> p t e s", t=TILES, e=n)
                    for first, n in GROUPS]

        hot_a = by_group(probs[:].bitcast(F16).rearrange("p a b -> p (a b)"))
        hT = sb("hT", [P, 2, FBLK, 512])
        hot_b = by_group(hT[:].bitcast(F16).rearrange("p a b c -> p (a b c)"))
        picked, index = sb("picked", [P, 3, 32]), sb("index", [P, EXPERTS + 2, CHUNKS], U32)
        hits = hT[:, 0, 0:3, 0:P].bitcast(BF16)
        from_index, to_index = sb("from_index", [P, 2, CHUNKS], U32), sb("to_index", [P, 2, CHUNKS], U32)
        w1_buf, w2_buf = sb("w1_buf", [P, 2, FF]), sb("w2_buf", [P, 2, FBLK, D])
        taken = sb("taken", [P, 2, CHUNKS, GATED])
        gates = sb("gates", [P, 2, CHUNKS])
        taken_hi, taken_lo = (k_hi, q_hi), (k_lo, q_lo)
        w1_hi, w1_lo = (k_first[:, i].rearrange("p g j -> p (g j)").rearrange("p (s f) -> p s f", s=2)
                        for i in range(2))
        y_sum = sb("y_sum", [P, 2, 4, D])
        y_out = v_ones[:].rearrange("p s j h c -> p (s j h c)").rearrange("p (s k d) -> p s k d", s=2, k=CHUNKS)
        f_stats, f_mv = sb("f_stats", [P, TILES, 6]), sb("f_mv", [P, TILES, 2])
        f_sd, f_rstd, f_bias = sb("f_sd", [P, TILES]), sb("f_rstd", [P, TILES]), sb("f_bias", [P, TILES])

        var_rooted, rstd_made, lg_made = sem("var_rooted"), sem("rstd_made"), sem("lg_made")
        tensor_step, vector_step = sem("tensor_step"), sem("vector_step")
        counted, totalled, found = sem("counted"), sem("totalled"), sem("found")
        hot_a_made, hot_b_made = sem("hot_a_made"), sem("hot_b_made")
        hot_id_made = [sem(f"hot_id_made{q}") for q in range(2)]
        rows_scaled, gates_made, table_out = sem("rows_scaled"), sem("gates_made"), sem("table_out")
        sum_out = sem("sum_out")
        w1_in, w2_in = ([sem(f"{name}{i}") for i in range(2)] for name in ("w1_in", "w2_in"))
        w1_hi_made, w1_cut, taken_hi_made = sem("w1_hi_made"), sem("w1_cut"), sem("taken_hi_made")
        from_set, to_set, gates_kept = sem("from_set"), sem("to_set"), sem("gates_kept")
        taken_in = [sem(f"taken_in{i}") for i in range(4)]
        turned, turned_copied = sem("turned"), sem("turned_copied")
        up_full, gelu_done = sem("up_full"), sem("gelu_done")
        down_full, y_summed, y_made = sem("down_full"), sem("y_summed"), sem("y_made")
        added = [sem(f"added{i}") for i in range(2)]
        f_in = [sem(f"f_in{i}") for i in range(4)]
        f_statted, f_averaged, f_rooted = sem("f_statted"), sem("f_averaged"), sem("f_rooted")
        f_inverted, f_biased, f_out = sem("f_inverted"), sem("f_biased"), sem("f_out")
        f_done, f_done_too = sem("f_done"), sem("f_done_too")

        block = ctx.enter_context(nc.Block())

        def product_of(first, n):
            at = {0: ps_second[:, 0, 0:64], 2: ps_second[:, 1, 0:128], 6: ps_second[:, 0, 64:128]}[first]
            return at[0:32 * n]

        def last_free(engine, job, uses_of):
            number = uses_of[job]
            if not (type(number) is int and number == 0):
                engine.wait_ge(job_free[BANK[job]], number)

        def made(engine, job, uses_of):
            engine.wait_ge(job_full[BANK[job]], uses_of[job] + 1)

        def copied_out(engine, job, uses_of):
            engine.wait_ge(job_free[BANK[job]], uses_of[job] + 1)

        x_tiled = x.rearrange("b (s p) d -> p (b s) d", p=P)
        summed_rows = summed.rearrange("(p t) d -> p t d", p=P)
        out_rows = out.rearrange("b s d -> (b s) d").rearrange("(p t) d -> p t d", p=P)
        N_WEIGHTS, N_LATE = 8, 5
        BY_DVE = 2
        QT = TILES // 4

        @block.sync
        def _(sp):
            sp.dma_start(x_pair[:], x_tiled[:, 0:4]).then_inc(x_pair_in, 16)
            loads = [(wq_nat[:], Wq), (wl[:], Wl), (bias_rows[:, 0], bq.unsqueeze(0)), (bias_rows[:, 1], bk.unsqueeze(0)),
                     (bl_col[:], bl.unsqueeze(1)), (wk_nat[:], Wk), (wv[0:LATENT], Wv),
                     (wv[LATENT:LATENT + 1], bv.unsqueeze(0))]
            assert len(loads) == N_WEIGHTS
            for dst, src in loads:
                sp.dma_start(dst, src).then_inc(weights_in, 16)
            late_loads = [(bo_all[:], bo.unsqueeze(0).to_broadcast([P, D])),
                          (b2_all[:], b2.rearrange("e h -> (e h)").unsqueeze(0).to_broadcast([P, EXPERTS * D])),
                          (wo[:], Wo), (wg[:], Wg), (b1_rows[:], b1.rearrange("e (c f) -> (e c) f", f=P))]
            assert len(late_loads) == N_LATE
            for dst, src in late_loads:
                sp.dma_start(dst, src).then_inc(late_in, 16)

            def store_split(pair, uses_of):
                for job, cut, stored, hi, lo_, dram, hi_terms in (
                        ("k", k_cut, k_stored, k_hi, k_lo, k_split, (0, 2)),
                        ("q", q_cut, q_stored, q_hi, q_lo, q_split, (0, 1))):
                    copied_out(sp, job, uses_of)
                    for t in hi_terms:
                        sp.dma_start(dram[pair, :, t].rearrange("r d g s i -> r (d g s i)"),
                                     hi[:].bitcast(F32)).then_inc(stored, 16)
                    sp.wait_ge(cut, pair + 1)
                    sp.dma_start(dram[pair, :, 3 - sum(hi_terms)].rearrange("r d g s i -> r (d g s i)"),
                                 lo_[:].bitcast(F32)).then_inc(stored, 16)

            def load_k(pair, side):
                for r in range(NR):
                    sp.dma_start(k_first[32 * r + DH:32 * r + 32, side].rearrange("p g i -> p (g i)").bitcast(F32),
                                 k_split[pair, r, :, :, :, side].rearrange("t d g i -> (t d) g i")
                                 ).then_inc(k_first_in[side], 16)

            def load_x(pair):
                sp.dma_start(x_pair[:], x_tiled[:, bass.ds(4 * pair, 4)]).then_inc(x_pair_in, 16)

            def load_q(pair, side, r):
                sp.dma_start(q_stack[32 * r + DH:32 * r + 32, side, r].rearrange("p g i -> p (g i)").bitcast(F32),
                             q_split[pair, r, :, :, :, side].rearrange("t d g i -> (t d) g i")).then_inc(q_in[r], 16)

            def load_shift(job, uses_of, side):
                r = int(job[3])
                copied_out(sp, job, uses_of)
                sp.dma_start(q_stack[32 * r:32 * r + 1, side, r].rearrange("p g i -> p (g i)").bitcast(F32),
                             shift_t[:, r, :].bitcast(F32)).then_inc(shift_in[r], 16)

            STORES = 16 * TERMS
            sp.wait_ge(consts_set, 6)
            in_prologue = numbers(PROLOGUE, [0, 0])
            store_split(0, in_prologue)
            sp.wait_ge(k_stored, STORES)
            for side in range(2):
                load_k(0, side)
                if side == 0:
                    copied_out(sp, "first_xT", in_prologue)
                    load_x(1)
                    sp.wait_ge(q_stored, STORES)
                for r in range(NR):
                    if side:
                        sp.wait_ge(q_in[r], 16)
                    load_q(0, side, r)
            for r in range(3):
                load_shift(f"max{r}", in_prologue, 0)

            def half(h):
                if h.prep:
                    store_split(h.n + 1, h.uses)
                load_shift("max3", h.uses, h.side)
                if h.ahead:
                    if h.prep:
                        sp.wait_ge(k_stored, STORES * (h.n + 2))
                    sp.wait_ge(first_full, 16 * (h.b + 1))
                    sp.wait_ge(k_kept, h.b + 1)
                    load_k(h.n + 1, h.side)
                if h.turn:
                    load_x(h.n + 2)
                if h.prep:
                    sp.wait_ge(q_stored, STORES * (h.n + 2))
                for r in range(NR):
                    if h.ahead:
                        sp.wait_ge(second_full, 16 * h.b + 4 * r + 4)
                        load_q(h.n + 1, h.side, r)
                    if r < 3 and h.nxt:
                        load_shift(f"max{r}", h.uses, h.after)

            def load_w1(e, side):
                sp.dma_start(w1_buf[:, side], W1[e]).then_inc(w1_in[side], 16)

            def load_w2(e, side):
                sp.dma_start(w2_buf[:, side], W2[e].rearrange("(c f) h -> f c h", f=P)).then_inc(w2_in[side], 16)

            for side in range(2):
                load_w1(side, side)
                load_w2(side, side)

            run_pairs(sp, half)

            sp.wait_ge(rows_scaled, TILES)
            sp.dma_start(summed.rearrange("(t p) d -> p t d", p=P), rows[:, :, 0:D]).then_inc(sum_out, 16)
            sp.wait_ge(gates_made, 1)
            sp.dma_start(x1_table.rearrange("(t p) d -> p t d", p=P), rows[:]).then_inc(table_out, 16)
            with sp.Fori(1, EXPERTS // 2) as n:
                for side in range(2):
                    sp.wait_ge(w1_cut, 2 * n + side - 1)
                    load_w1(2 * n + side, side)
                    sp.wait_ge(down_full, 4 * (n - 1) + 2 * (side + 1))
                    load_w2(2 * n + side, side)

            for side in range(2):
                sp.wait_ge(added[side], 16 * CHUNKS * EXPERTS // 2)
            for q in range(4):
                sp.dma_start(xc_all[:, q * QT:(q + 1) * QT], summed_rows[:, q * QT:(q + 1) * QT]).then_inc(f_in[q], 16)
            for q in range(4):
                sp.wait_ge(f_done, (QT - BY_DVE) * (q + 1))
                sp.wait_ge(f_done_too, BY_DVE * (q + 1))
                sp.dma_start(out_rows[:, q * QT:(q + 1) * QT], xc_all[:, q * QT:(q + 1) * QT]).then_inc(f_out, 16)
            sp.wait_ge(f_out, 64)

        @block.gpsimd
        def _(pool):
            g = nc.gpsimd
            g.memset(ident[:], 0.0).then_inc(hi_done, 1)
            pool.wait_ge(hi_done, 1)
            g.affine_select(out=ident[:], in_=ident[:], compare_op=ALU.not_equal, fill=1.0, base=0,
                            pattern=[[-1, P]], channel_multiplier=1).then_inc(consts_set, 1)
            g.memset(ones[:], 1.0).then_inc(consts_set, 1)
            g.memset(eps_col[:], EPS).then_inc(consts_set, 1)
            g.memset(q_stack[:].bitcast(F32), 0.0).then_inc(consts_set, 1)
            g.memset(k_first[:].bitcast(F32), 0.0).then_inc(consts_set, 1)
            g.memset(v_ones[:], 0.0).then_inc(hi_done, 1)
            pool.wait_ge(hi_done, 2)
            for r in range(NR):
                at = OFFSET[r] + DH
                ins = g.memset(v_ones[:, :, :, NG * r:NG * r + NG, at:at + 1], 1.0)
            ins.then_inc(consts_set, 1)

            def split(uses_of):
                for job, full, hi, lo_, done in (("k", k_full, k_hi, k_lo, k_cut), ("q", q_full, q_hi, q_lo, q_cut)):
                    copied_out(pool, job, uses_of)
                    passed(pool, pool_waits)
                    g.tensor_tensor(lo_[:], full, hi[:].bitcast(F32), ALU.subtract).then_inc(done, 1)

            def copy_v(batch, side):
                passed(pool, pool_waits)
                src = v_stage[:, 2 * side:2 * side + 2].rearrange("p j (h d) -> p j h d", h=HEADS)
                for r in range(NR):
                    heads = slice(NG * r, NG * r + NG)
                    g.tensor_copy(v_ones[:, side, :, heads, OFFSET[r]:OFFSET[r] + DH], src[:, :, heads]).then_inc(v_ready, 1)

            def keep_centred(batch):
                pool.wait_ge(centred, 2 * batch + 2)
                passed(pool, pool_waits)
                g.tensor_copy(xc_all[:, bass.ds(2 * batch, 2)], xc[:]).then_inc(xc_kept, 1)

            g.iota(part_i[:], pattern=[[0, 2]], base=0, channel_multiplier=1).then_inc(indices_set, 1)
            g.iota(col_i[:, 0], pattern=[[0, 16], [1, EXPERTS]], base=0, channel_multiplier=0).then_inc(indices_set, 1)
            g.iota(col_i[:, 1], pattern=[[1, 16], [0, EXPERTS]], base=0, channel_multiplier=0).then_inc(indices_set, 1)
            g.iota(iota32_i[:], pattern=[[1, 32]], base=0, channel_multiplier=0).then_inc(indices_set, 1)
            g.iota(token_i[:], pattern=[[P, TILES]], base=-ID_BASE, channel_multiplier=1).then_inc(indices_set, 1)
            g.memset(ones_b[:], 1.0).then_inc(indices_set, 1)
            pool.wait_ge(indices_set, 6)
            g.affine_select(out=upper_b[:], in_=ones_b[:], compare_op=ALU.is_gt, fill=0.0, base=0,
                            pattern=[[1, P]], channel_multiplier=-1).then_inc(indices_set, 1)

            in_prologue = numbers(PROLOGUE, [0, 0])
            split(in_prologue)
            copied_out(pool, "v", in_prologue)
            copy_v(0, 0)
            pool.wait_ge(late_in, 16 * N_LATE)
            pool.wait_ge(rows_in, 16)
            g.tensor_tensor(rows[:, :, 0:D], rows[:, :, 0:D], bo_all[:].unsqueeze(1).to_broadcast([P, TILES, D]),
                            ALU.add).then_inc(rows_biased, 1)

            def half(h):
                if h.side == 0:
                    if h.prev:
                        pool.wait_ge(pv_done, 4 * h.b)
                    copy_v(h.b + 1, 1)
                    if h.prep:
                        split(h.uses)
                elif h.ahead:
                    pool.wait_ge(pv_done, 4 * h.b)
                    copied_out(pool, "v", h.side_0)
                    copy_v(h.b + 1, 0)
                if h.prev:
                    keep_centred(h.b - 1)

            run_pairs(pool, half)
            keep_centred(BATCHES - 1)

            for part in range(HOT_PARTS[0]):
                ts = slice(part * HOT_TILES[0], (part + 1) * HOT_TILES[0])
                pool.wait_ge(hot_b_made, part + 1)
                ids = token_id[:, ts].unsqueeze(2).unsqueeze(3).to_broadcast([P, HOT_TILES[0], GROUPS[0][1], 32])
                g.tensor_tensor(hot_b[0][:, ts], hot_b[0][:, ts], ids, ALU.mult).then_inc(hot_id_made[0], 1)

            pool.wait_ge(found, 1)
            pool.wait_ge(table_out, 16)
            pool.wait_ge(sum_out, 16)

            every, halves = range(CHUNKS), (range(CHUNKS // 2), range(CHUNKS // 2, CHUNKS))

            def gather(n, side, again, chunks=every):
                e = 2 * n + side
                if again:
                    pool.wait_ge(turned, 2 * e - 2)
                    pool.wait_ge(gates_kept, e - 1)
                pool.wait_ge(from_set, e if again else 1)
                passed(pool, pool_waits)
                for c in chunks:
                    g.indirect_dma_start(taken[:, side, c], None, x1_table,
                                         bass.IndirectOffsetOnAxis(ap=from_index[:, side, c:c + 1], axis=0)
                                         ).then_inc(taken_in[2 * side + c // 4], 16)

            def scatter(n, side, first=False, chunks=every):
                e = 2 * n + side
                pool.wait_ge(to_set, e + 1)
                if not first:
                    before = 16 * CHUNKS * (n if side == 0 else n + 1)
                    pool.wait_ge(added[1 - side], before)
                for c in chunks:
                    pool.wait_ge(y_made, 8 * e + c + 1)
                    passed(pool, pool_waits)
                    g.indirect_dma_start(summed, bass.IndirectOffsetOnAxis(ap=to_index[:, side, c:c + 1], axis=0),
                                         y_out[:, side, c], None, compute_op=ALU.add).then_inc(added[side], 16)

            gather(0, 0, False)
            gather(0, 1, False)
            pool.wait_ge(found, 2)
            gather(1, 0, True)
            for half_of in halves:
                scatter(0, 0, first=True, chunks=half_of)
                gather(1, 1, True, half_of)
            scatter(0, 1)
            last = EXPERTS // 2 - 1
            with pool.Fori(2, last) as n:
                for side in range(2):
                    gather(n, side, True)
                    scatter(n - 1, side)
            gather(last, 0, True)
            scatter(last - 1, 0)
            gather(last, 1, True)
            scatter(last - 1, 1)
            for side in range(2):
                scatter(last, side)

        @block.scalar
        def _(act):
            s = nc.scalar
            act.wait_ge(weights_in, 16 * N_WEIGHTS)
            act.dma_start(rows[:, :, 0:D], x_tiled).then_inc(rows_in, 16)

            def evacuate(job, uses_of):
                if job not in ("first_xT", "xT", "latent", "k", "q", "v", "oT", "xcT"):
                    return
                made(act, job, uses_of)
                bank = ps_job[:, BANK[job]]
                if job in ("first_xT", "xT"):
                    ins = s.copy(xT[:], bank)
                elif job == "latent":
                    ins = s.activation(latT[0:LATENT], bank[0:LATENT], ACT.Identity, bias=bl_col[:, 0:1])
                elif job in ("k", "q"):
                    full, hi, col = (k_full, k_hi, bk_col) if job == "k" else (q_full, q_hi, bq_col)
                    s.activation(hi[:], bank, ACT.Identity, bias=col[:, 0:1])
                    ins = s.activation(full, bank, ACT.Identity, bias=col[:, 0:1])
                elif job == "v":
                    ins = s.copy(v_stage[:].rearrange("p a b -> p (a b)"), bank)
                elif job == "oT":
                    ins = s.copy(oT[:], bank[:, 0:SEQ])
                else:
                    ins = s.copy(xcT[:], bank[:, 0:SEQ])
                ins.then_inc(job_free[BANK[job]], 1)

            def keep_k(pair, side):
                act.wait_ge(k_first_in[side], 64 * (pair + 1))
                s.activation(k_second[:, side], k_first[:, side], ACT.Identity,
                             bias=shift_rows[:, 0:1]).then_inc(k_kept, 1)

            act.wait_ge(consts_set, 3)
            s.activation(warm[:], eps_col[:, 0:1], ACT.Exp).then_inc(warmed, 1)
            act.wait_ge(bias_out, 1)
            act.wait_ge(shift_ones, 1 + NR)
            in_prologue = numbers(PROLOGUE, [0, 0])
            for job in PROLOGUE:
                evacuate(job, in_prologue)
            keep_k(0, 0)

            def half(h):
                for k in range(HEADS):
                    r, gg = divmod(k, NG)
                    head = 16 * h.b + k
                    if k in h.jobs:
                        job = h.jobs[k]
                        if job in ("k", "q"):
                            act.wait_ge(k_cut if job == "k" else q_cut, h.n + 1)
                            act.wait_ge(k_stored if job == "k" else q_stored, 16 * TERMS * (h.n + 1))
                        if job == "v":
                            act.wait_ge(v_ready, NR * (h.b + 2))
                        evacuate(job, h.uses)
                    act.wait_ge(second_full, head + 1)
                    if gg == 0 and (h.prev or r >= 2):
                        act.wait_ge(pv_done, 4 * h.b + r - 1)
                    s.activation(probs[:, 4 * (r % 2) + gg], ps_second[:, k % 2], ACT.Exp,
                                 scale=SCALE).then_inc(exp_done, 1)
                    if k == 5 and h.nxt:
                        keep_k(h.after_pair, h.after)
                    if k == 15:
                        act.wait_ge(pv_done, 4 * h.b + 3)
                        if h.prev:
                            made(act, "norm", h.uses)
                        s.copy(oT_raw[:, 0], ps_pv[:, 0]).then_inc(o_copied, 1)

            run_pairs(act, half)
            at_end = numbers(TAIL_AT.values(), BASE_END)
            evacuate("oT", at_end)
            evacuate("xcT", at_end)

            def round_w1(e_pair, side):
                act.wait_ge(w1_in[side], 16 * (e_pair + 1))
                passed(act, act_waits)
                s.copy(w1_hi[:, side], w1_buf[:, side]).then_inc(w1_hi_made, 1)

            act.wait_ge(first_full, 16 * BATCHES)
            act.wait_ge(k_kept, BATCHES)
            round_w1(0, 0)

            act.wait_ge(var_kept, BATCHES)
            s.activation(rstd[:], var_all[:], ACT.Sqrt, bias=eps_col[:, 0:1]).then_inc(var_rooted, 1)
            act.wait_ge(rstd_made, 1)
            act.wait_ge(xc_kept, BATCHES)
            with act.Fori(0, TILES) as t:
                s.activation(rows[:, bass.ds(t, 1), 0:D].rearrange("p o d -> p (o d)"),
                             xc_all[:, bass.ds(t, 1)].rearrange("p o d -> p (o d)"),
                             ACT.Copy, scale=rstd[:, bass.ds(t, 1)]).then_inc(rows_scaled, 1)
            act.wait_ge(lg_made, 1)
            s.activation(rows[:, :, D:GATED], lg[:], ACT.Sigmoid).then_inc(gates_made, 1)

            for part in range(HOT_PARTS[1]):
                act.wait_ge(hot_b_made, HOT_PARTS[0] + part + 1)
                for t in range(part * HOT_TILES[1], (part + 1) * HOT_TILES[1]):
                    flat = hot_b[1][:, t].rearrange("p e s -> p (e s)")
                    ins = s.activation(flat, flat, ACT.Copy, scale=token_id[:, t:t + 1])
                ins.then_inc(hot_id_made[1], 1)

            act.wait_ge(b1_out, 1)

            def gelu(n, blk):
                for f in range(FBLK):
                    act.wait_ge(up_full, 16 * n + 4 * blk + f + 1)
                    if f == 0 and not (type(n) is int and blk < 2):
                        act.wait_ge(down_full, 4 * n + blk - 1)
                    passed(act, act_waits)
                    s.activation(hT[:, blk % 2, f], ps_up[:, f], ACT.Gelu,
                                 bias=b1_cols[:, bass.ds(FBLK * (2 * n + blk // 2) + f, 1)]).then_inc(gelu_done, 1)

            def gelus(n, last=False):
                for blk in range(4):
                    gelu(n, blk)
                    if blk == 0:
                        round_w1(n, 1)
                    elif blk == 2 and not last:
                        round_w1(n + 1, 0)

            gelus(0)
            with act.Fori(1, EXPERTS // 2 - 1) as n:
                gelus(n)
            gelus(EXPERTS // 2 - 1, last=True)

            def normalise(q):
                act.wait_ge(f_biased, q + 1)
                for t in range(QT * q, QT * (q + 1) - BY_DVE):
                    s.activation(xc_all[:, t], xc_all[:, t], ACT.Identity, scale=f_rstd[:, t:t + 1],
                                 bias=f_bias[:, t:t + 1]).then_inc(f_done, 1)

            for q in range(4):
                act.wait_ge(f_averaged, QT * (q + 1))
                s.activation(f_sd[:, q * QT:(q + 1) * QT].unsqueeze(2), f_mv[:, q * QT:(q + 1) * QT, 1:2], ACT.Sqrt,
                             bias=eps_col[:, 0:1]).then_inc(f_rooted, 1)
                if q:
                    normalise(q - 1)
            normalise(3)

        @block.tensor
        def _(pe):
            t_ = nc.tensor
            pe.wait_ge(weights_in, 16 * N_WEIGHTS)
            pe.wait_ge(consts_set, 2)
            pe.wait_ge(perm_done, 4)
            pe.wait_ge(latent_one, 1)
            for i in range(2):
                mm = t_.matmul(ps_pv[:, 0, i:i + 1], bias_perm[:, i], ones[0:1, 0:1], start=True, stop=True)
            mm.then_inc(bias_made, 1)

            def run_job(job, uses_of, batch, tail_batch=None):
                last_free(pe, job, uses_of)
                if job in READS:
                    copied_out(pe, READS[job], uses_of)
                bank = ps_job[:, BANK[job]]
                if job in ("first_xT", "xT"):
                    pe.wait_ge(x_pair_in, 16 * (batch + 1))
                    for c in range(4):
                        mm = t_.transpose(bank[:, c * P:(c + 1) * P], x_pair[:, c], ident[:])
                elif job == "latent":
                    mm = t_.matmul(bank[0:LATENT, :], wl[:], xT[:], start=True, stop=True)
                elif job == "k":
                    mm = t_.matmul(bank, wk[:], latT[0:LATENT], start=True, stop=True)
                elif job == "q":
                    mm = t_.matmul(bank, wq[:], xT[:], start=True, stop=True)
                elif job == "v":
                    for c in range(4):
                        o = bank[:, c * D:(c + 1) * D]
                        mm = t_.matmul(o, latT[:, c * P:(c + 1) * P], wv[:], start=True, stop=True)
                elif job.startswith("max"):
                    r = int(job[3])
                    pe.wait_ge(first_free, 16 * batch + 4 * (r + 1))
                    mm = t_.transpose(bank[0:2 * NG, 0:P], row_max[:, r], ident[:])
                elif job == "norm":
                    pe.wait_ge(o_copied, 2 * tail_batch + 2)
                    for i in range(2):
                        for slot_ in range(2):
                            mm = t_.transpose(bank[:, (2 * i + slot_) * P:(2 * i + slot_ + 1) * P],
                                              oT_raw[:, slot_, i * P:(i + 1) * P], ident[:])
                elif job == "oT":
                    for i in range(2):
                        mm = t_.transpose(bank[:, i * P:(i + 1) * P], o_nat[:, i], ident[:])
                elif job == "y":
                    for i in range(2):
                        o = bank[:, i * D:(i + 1) * D]
                        mm = t_.matmul(o, oT[:, i * P:(i + 1) * P], wo[:], start=True, stop=True)
                elif job == "xcT":
                    pe.wait_ge(centred, 2 * tail_batch + 2)
                    for i in range(2):
                        mm = t_.transpose(bank[:, i * P:(i + 1) * P], xc[:, i], ident[:])
                else:
                    for i in range(2):
                        mm = t_.matmul(bank[:, i * EXPERTS:(i + 1) * EXPERTS], xcT[:, i * P:(i + 1) * P], wg[:],
                                       start=True, stop=True)
                mm.then_inc(job_full[BANK[job]], 1)

            def first_pass(batch, side, pair, k, fresh):
                r, gg = divmod(k, NG)
                if k == 0:
                    pe.wait_ge(k_first_in[side], 64 * (pair + 1))
                if gg == 0:
                    pe.wait_ge(q_in[r], 16 * (batch + 1))
                if not (fresh and k < 3):
                    pe.wait_ge(first_free, 16 * batch + k - FIRST_AGO[k] + 1)
                for i in range(2):
                    o = ps_first[:, FIRST_BANK[k], i * SEQ:(i + 1) * SEQ]
                    mm = t_.matmul(o, q_stack[:, side, r, gg, i * P:(i + 1) * P], k_first[:, side, gg],
                                   start=True, stop=True)
                mm.then_inc(first_full, 1)

            def pv(batch, side, r):
                for j in range(2):
                    for gg in range(NG):
                        mm = t_.matmul(ps_pv[32 * gg:32 * gg + 32, SLOT[r]], v_ones[:, side, j, NR * r + gg],
                                       probs[:, 4 * (r % 2) + gg, j * SEQ:(j + 1) * SEQ],
                                       start=(j == 0 and r in (0, 3)), stop=(j == 1 and r in (2, 3)),
                                       tile_position=(0, 32 * gg), skip_group_check=True)
                mm.then_inc(pv_done, 1)

            in_prologue = numbers(PROLOGUE, [0, 0])
            for job in PROLOGUE[:6]:
                run_job(job, in_prologue, 1 if job == "xT" else 0)
            pe.wait_ge(bias_out, 1)
            for k in range(HEADS):
                if k in MAX_AT and MAX_AT[k] != "max3":
                    run_job(MAX_AT[k], in_prologue, 0)
                first_pass(0, 0, 0, k, True)

            def half(h):
                for k in range(HEADS):
                    r, gg = divmod(k, NG)
                    if k in h.jobs:
                        job = h.jobs[k]
                        if job == "latent":
                            pe.wait_ge(job_free[1], h.turned_before)
                        if job == "xT":
                            run_job(job, h.uses, h.n + 2)
                        elif job == "max3":
                            run_job(job, h.uses, h.b)
                        else:
                            run_job(job, h.uses, h.b + 1, h.b - 1)
                    if h.nxt:
                        first_pass(h.b + 1, h.after, h.after_pair, k, False)
                    if k == 0:
                        pe.wait_ge(k_kept, h.b + 1)
                    if gg == 0:
                        pe.wait_ge(shift_in[r], 16 * (h.b + 1))
                    if h.prev or k >= 2:
                        pe.wait_ge(exp_done, 16 * h.b + k - 1)
                    for j in range(2):
                        mm = t_.matmul(ps_second[:, k % 2, j * SEQ:(j + 1) * SEQ],
                                       k_second[:, h.side, gg, j * P:(j + 1) * P],
                                       q_stack[:, h.side, r, gg], start=True, stop=True)
                    mm.then_inc(second_full, 1)
                    if k == 2 and h.prev:
                        pe.wait_ge(exp_done, 16 * h.b)
                        pe.wait_ge(o_copied, 2 * h.b - 1)
                        pv(h.b - 1, 1 - h.side, 3)
                    if k in (6, 10, 14):
                        group = k // 4 - 1
                        pe.wait_ge(exp_done, 16 * h.b + 4 * (group + 1))
                        if group == 0:
                            pe.wait_ge(v_ready, NR * (h.b + 1))
                            if h.prev:
                                pe.wait_ge(o_copied, 2 * h.b)
                        pv(h.b, h.side, group)

            run_pairs(pe, half)
            pe.wait_ge(exp_done, 16 * BATCHES)
            pe.wait_ge(o_copied, 2 * BATCHES - 1)
            pv(BATCHES - 1, 1, 3)
            at_end = numbers(TAIL_AT.values(), BASE_END)
            for job in TAIL_AT.values():
                run_job(job, at_end, None, BATCHES - 1)

            stepped = Count()
            pe.wait_ge(late_in, 16 * N_LATE)
            t_.transpose(ps_second[:, 0, 0:EXPERTS * FBLK], b1_rows[:],
                         ident[0:EXPERTS * FBLK, 0:EXPERTS * FBLK]).then_inc(tensor_step, 1)
            pe.wait_ge(lg_made, 1)
            for i in range(2):
                mm = t_.transpose(ps_a[:, i * P:(i + 1) * P], lg[:, 16 * i:16 * i + 16].rearrange("p t e -> p (t e)"),
                                  ident[:])
            mm.then_inc(tensor_step, 1)
            pe.wait_ge(vector_step, stepped.next())
            t_.transpose(ps_pv[0:1, 0, 0:P], abs_col[:], ident[:]).then_inc(tensor_step, 1)
            pe.wait_ge(vector_step, stepped.next())
            t_.matmul(ps_a[:, 0:1], ones[0:1, :], bound[:], start=True, stop=True).then_inc(tensor_step, 1)
            for n in range(SEARCH_STEPS):
                pe.wait_ge(counted, 3 * n + 3)
                t_.matmul(ps_pv[:, 0, 0:3], same_eb[:], counts[:], start=True, stop=True).then_inc(totalled, 1)
            pe.wait_ge(vector_step, stepped.next())
            t_.matmul(ps_a[:, 0:2 * EXPERTS], ones[:], lo_hi[:].rearrange("p a e -> p (a e)"), start=True,
                      stop=True).then_inc(tensor_step, 1)
            pe.wait_ge(vector_step, stepped.next())
            t_.matmul(ps_pv[:, 0, 0:EXPERTS], ones_b[:], gt_sum[:], start=True, stop=True).then_inc(tensor_step, 1)

            def prefix(mask, which):
                flat = mask[:].rearrange("p t e -> p (t e)")
                for i in range(2):
                    mm = t_.matmul(ps_pv[:, 1, i:i + 1], flat[:, i * P:(i + 1) * P], ones_b[:, 0:1], start=True, stop=True)
                mm.then_inc(tensor_step, 1)
                pe.wait_ge(vector_step, stepped.next())
                t_.matmul(ps_a[:, 0:NPART], upper_b[:], flat, start=True, stop=False, skip_group_check=True)
                first = tile_sum[:, which, 0:1].to_broadcast([P, P])
                second = tile_sum[:, which, 1:2].to_broadcast([P, P])
                t_.matmul(ps_a[:, 0:P], first, before_b[:], start=False, stop=False, skip_group_check=True)
                t_.matmul(ps_a[:, P:2 * P], first, same_eb[:], start=False, stop=False, skip_group_check=True)
                t_.matmul(ps_a[:, P:2 * P], second, before_b[:], start=False, stop=True,
                          skip_group_check=True).then_inc(tensor_step, 1)

            pe.wait_ge(vector_step, stepped.next())
            prefix(tie, 0)
            pe.wait_ge(vector_step, stepped.next())
            prefix(sel, 1)
            def turn(n, blk):
                side, hb = divmod(blk, 2)
                pe.wait_ge(taken_in[blk], 64 * (n + 1))
                if not (type(n) is int and n == 0 and blk == 0):
                    pe.wait_ge(turned_copied, 4 * n + blk)
                for c in range(4):
                    mm = t_.transpose(ps_turn[:, c * P:(c + 1) * P], taken[:, side, 4 * hb + c, 0:D], ident[:])
                mm.then_inc(turned, 1)

            for group, blocks in enumerate(BLOCKS):
                for t in range(TILES):
                    if t % HOT_TILES[group] == 0:
                        part = t // HOT_TILES[group]
                        if (group, part) == EARLY_TURN:
                            turn(0, 0)
                        pe.wait_ge(hot_a_made, HOT_PARTS[0] * group + part + 1)
                        pe.wait_ge(hot_id_made[group], part + 1)
                    for first, n in blocks:
                        es = slice(first - GROUPS[group][0], first - GROUPS[group][0] + n)
                        mm = t_.matmul(product_of(first, n), hot_a[group][:, t, es].rearrange("p e s -> p (e s)"),
                                       hot_b[group][:, t, es].rearrange("p e s -> p (e s)"),
                                       start=(t == 0), stop=(t == TILES - 1), skip_group_check=True)
                mm.then_inc(tensor_step, 1)
                if group == 1:
                    turn(0, 1)
                pe.wait_ge(vector_step, stepped.next())
                for first, n in blocks:
                    for e in range(n):
                        for k in range(4):
                            mm = t_.matmul(ps_a[32 * k:32 * k + 32, CHUNKS * (first + e):CHUNKS * (first + e + 1)],
                                           ident[0:32 * n, 32 * e:32 * e + 32],
                                           picked[0:32 * n, first // 3, CHUNKS * k:CHUNKS * (k + 1)],
                                           start=True, stop=True, tile_position=(0, 32 * k), skip_group_check=True)
                mm.then_inc(tensor_step, 1)

            def up(n, blk, fs):
                side = blk // 2
                if fs[0] == 0:
                    if blk % 2 == 0:
                        pe.wait_ge(w1_cut, 2 * n + side + 1)
                    pe.wait_ge(turned_copied, 4 * n + blk + 1)
                for f in fs:
                    if not (type(n) is int and n == 0 and blk == 0):
                        pe.wait_ge(gelu_done, 16 * n + 4 * blk + f - 3)
                    cols, b = slice(f * P, (f + 1) * P), blk % 2
                    t_.matmul(ps_up[:, f], w1_hi[:, side, cols], taken_hi[b][:], start=True, stop=False)
                    t_.matmul(ps_up[:, f], w1_hi[:, side, cols], taken_lo[b][:], start=False, stop=False)
                    t_.matmul(ps_up[:, f], w1_lo[:, side, cols], taken_hi[b][:],
                              start=False, stop=True).then_inc(up_full, 1)

            def down(n, blk, early, following=None):
                side = blk // 2
                if blk % 2 == 0:
                    pe.wait_ge(w2_in[side], 16 * (n + 1))
                pe.wait_ge(gelu_done, 16 * n + 4 * blk + 4)
                if not early:
                    pe.wait_ge(y_summed, 4 * n + blk - 1)
                for c in range(4):
                    if c == TURN_CHUNK and following is not None:
                        turn(*following)
                    for f in range(FBLK):
                        mm = t_.matmul(ps_second[:, blk % 2, c * P:(c + 1) * P], hT[:, blk % 2, f, c * P:(c + 1) * P],
                                       w2_buf[:, side, f], start=(f == 0), stop=(f == FBLK - 1))
                mm.then_inc(down_full, 1)

            pe.wait_ge(found, 2)
            def four_blocks(n, begin=False, last=False):
                if not begin:
                    up(n - 1, 3, (2, 3))
                up(n, 0, (0, 1))
                if not begin:
                    down(n - 1, 3, False, (n, 1))
                for blk in range(1, 4):
                    up(n, blk - 1, (2, 3))
                    up(n, blk, (0, 1))
                    following = (n, blk + 1) if blk < 3 else None if last else (n + 1, 0)
                    down(n, blk - 1, begin and blk < 3, following)

            four_blocks(0, begin=True)
            with pe.Fori(1, EXPERTS // 2 - 1) as n:
                four_blocks(n)
            four_blocks(EXPERTS // 2 - 1, last=True)
            up(EXPERTS // 2 - 1, 3, (2, 3))
            down(EXPERTS // 2 - 1, 3, False)

        @block.vector
        def _(dve):
            v = nc.vector
            v.memset(latT[LATENT:LATENT + 1], 1.0).then_inc(latent_one, 1)
            v.memset(shift_rows[:], 0.0).then_inc(shift_ones, 1)
            v.memset(index[:, EXPERTS:], 0)
            dve.wait_ge(shift_ones, 1)
            dve.wait_ge(weights_in, 16 * N_WEIGHTS)
            for nat, perm in ((wq_nat[:], wq[:]), (wk_nat[:], wk[:]), (bias_rows[:, 0], bias_perm[:, 0]),
                              (bias_rows[:, 1], bias_perm[:, 1])):
                v.tensor_copy(perm.rearrange("p (r d g) -> p r d g", r=NR, g=NG),
                              nat.rearrange("p (r g d) -> p r d g", r=NR, g=NG)).then_inc(perm_done, 1)
            for r in range(NR):
                v.memset(shift_rows[32 * r:32 * r + 1], 1.0).then_inc(shift_ones, 1)
            dve.wait_ge(bias_made, 1)
            v.tensor_copy(bq_col[:], ps_pv[:, 0, 0:1])
            v.tensor_copy(bk_col[:], ps_pv[:, 0, 1:2]).then_inc(bias_out, 1)

            def take_maxima(batch, k):
                r, gg = divmod(k, NG)
                dve.wait_ge(first_full, 16 * batch + k + 1)
                v.tensor_reduce(row_max[:, r, 2 * gg:2 * gg + 2],
                                ps_first[:, FIRST_BANK[k]].rearrange("p (i j) -> p i j", i=2),
                                AX, ALU.max).then_inc(first_free, 1)

            def evacuate(job, uses_of, batch, tail):
                if job in ("first_xT", "xT", "latent", "k", "q", "v", "oT", "xcT"):
                    return
                made(dve, job, uses_of)
                bank = ps_job[:, BANK[job]]
                if job.startswith("max"):
                    r = int(job[3])
                    if not (type(batch) is int and batch == 0):
                        dve.wait_ge(shift_in[r], 16 * batch)
                    ins = v.tensor_scalar(shift_t[:, r], bank[0:2 * NG, 0:P], -1.0, None, ALU.mult)
                elif job == "norm":
                    raw = bank.rearrange("p (i s g c) -> p i s g c", i=2, s=2, g=NG)
                    dens = den[:].rearrange("p i (r g) -> p i g r", g=NG)
                    end = OFFSET[2] + DH + 1
                    v.reciprocal(dens[:, :, :, 0:3], raw[:, :, 0, :, DH:end:DH + 1]).then_inc(den_done, 1)
                    v.reciprocal(dens[:, :, :, 3:4], raw[:, :, 1, :, DH:DH + 1]).then_inc(den_done, 1)
                    dve.wait_ge(den_done, 2 * tail + 2)
                    for i in range(2):
                        v.tensor_tensor(o_nat[:, i].rearrange("p (r g d) -> p g r d", r=NR, g=NG)[:, :, 0:3],
                                        raw[:, i, 0, :, 0:end].rearrange("p g (r c) -> p g r c", r=3)[:, :, :, 0:DH],
                                        dens[:, i, :, 0:3].unsqueeze(3).to_broadcast([P, NG, 3, DH]),
                                        ALU.mult).then_inc(o_scaled, 1)
                    ins = v.tensor_tensor(o_nat[:, :, 3 * NG * DH:].rearrange("p i (g d) -> p i g d", g=NG),
                                          raw[:, :, 1, :, 0:DH],
                                          den[:, :, 3 * NG:].unsqueeze(3).to_broadcast([P, 2, NG, DH]), ALU.mult)
                elif job == "y":
                    if not (type(tail) is int and tail == 0):
                        dve.wait_ge(centred, 2 * tail)
                    else:
                        dve.wait_ge(rows_biased, 1)
                    ins = v.tensor_tensor(resid[:], bank[:, 0:2 * D].rearrange("p (i d) -> p i d", i=2),
                                          rows[:, bass.ds(2 * tail, 2), 0:D], ALU.add)
                else:
                    ins = v.tensor_copy(logits[:, bass.ds(2 * tail, 2)],
                                        bank[:, 0:2 * EXPERTS].rearrange("p (i e) -> p i e", i=2))
                ins.then_inc(job_free[BANK[job]], 1)

            def finish(stage, uses_of, tail):
                if stage == 0:
                    copied_out(dve, "y", uses_of)
                    for i in range(2):
                        v.bn_stats(stats[:, i], resid[:, i]).then_inc(stats_done, 1)
                elif stage == 1:
                    dve.wait_ge(stats_done, 2 * tail + 2)
                    passed(dve, dve_waits)
                    for i in range(2):
                        v.bn_aggr(mean_var[:, i], stats[:, i]).then_inc(mv_done, 1)
                else:
                    dve.wait_ge(mv_done, 2 * tail + 2)
                    if not (type(tail) is int and tail == 0):
                        dve.wait_ge(xc_kept, tail)
                    for i in range(2):
                        v.tensor_scalar(xc[:, i], resid[:, i], mean_var[:, i, 0:1], None,
                                        ALU.subtract).then_inc(centred, 1)
                    v.tensor_copy(var_all[:, bass.ds(2 * tail, 2)].unsqueeze(2), mean_var[:, :, 1:2]).then_inc(var_kept, 1)

            sent, linked = Count(), Count()

            for n in range(SEARCH_STEPS + 1):
                for j in range(4):
                    v.memset(quarters[:, n, j:j + 1], 0.5 * j * 0.25 ** n)
            dve.wait_ge(indices_set, 7)
            v.tensor_copy(iota32[:], iota32_i[:])
            v.tensor_copy(token_id[:], token_i[:])
            v.tensor_scalar(part_i[:, 0:1], part_i[:, 0:1], EXPERTS - 1, None, ALU.bitwise_and).then_inc(linked_step, 1)
            dve.wait_ge(linked_step, linked.next())
            v.tensor_scalar(part_i[:, 1:2], part_i[:, 1:2], 3, None, ALU.arith_shift_right).then_inc(linked_step, 1)
            dve.wait_ge(linked_step, linked.next())
            v.tensor_copy(part_f[:], part_i[:]).then_inc(linked_step, 1)
            dve.wait_ge(linked_step, linked.next())
            v.tensor_scalar(same_e[:], col_i[:, 0], part_f[:, 0:1], None, ALU.is_equal).then_inc(linked_step, 1)
            dve.wait_ge(linked_step, linked.next())
            v.tensor_copy(same_eb[:], same_e[:]).then_inc(linked_step, 1)
            dve.wait_ge(linked_step, linked.next())
            v.scalar_tensor_tensor(out=before_b[:], in0=col_i[:, 1], scalar=part_f[:, 1:2], in1=same_e[:],
                                   op0=ALU.is_gt, op1=ALU.mult).then_inc(linked_step, 1)
            dve.wait_ge(linked_step, linked.next())

            in_prologue = numbers(PROLOGUE, [0, 0])
            for k in range(HEADS):
                if k in MAX_AT and MAX_AT[k] != "max3":
                    evacuate(MAX_AT[k], in_prologue, 0, 0)
                take_maxima(0, k)

            def half(h):
                for k in range(HEADS):
                    if k in h.jobs:
                        job = h.jobs[k]
                        evacuate(job, h.uses, h.b if job == "max3" else h.b + 1, h.b - 1)
                    if h.nxt:
                        take_maxima(h.b + 1, k)
                    if k in (9, 10, 11) and h.prev:
                        finish(k - 9, h.uses, h.b - 1)
                    if k == 2 and h.prev:
                        dve.wait_ge(pv_done, 4 * h.b)
                        v.tensor_copy(oT_raw[:, 1], ps_pv[:, 1]).then_inc(o_copied, 1)

            run_pairs(dve, half)
            dve.wait_ge(pv_done, 4 * BATCHES)
            v.tensor_copy(oT_raw[:, 1], ps_pv[:, 1]).then_inc(o_copied, 1)
            at_end = numbers(TAIL_AT.values(), BASE_END)
            for job in TAIL_AT.values():
                evacuate(job, at_end, None, BATCHES - 1)
                if job == "y":
                    for stage in range(3):
                        finish(stage, at_end, BATCHES - 1)

            def cut_w1(n, side):
                dve.wait_ge(w1_in[side], 16 * (n + 1))
                dve.wait_ge(w1_hi_made, 2 * n + side + 1)
                v.tensor_tensor(w1_lo[:, side], w1_buf[:, side], w1_hi[:, side].bitcast(F32),
                                ALU.subtract).then_inc(w1_cut, 1)

            cut_w1(0, 0)

            read = Count()
            dve.wait_ge(var_rooted, 1)
            v.reciprocal(rstd[:], rstd[:]).then_inc(rstd_made, 1)
            dve.wait_ge(rstd_made, 1)
            v.tensor_tensor(lg[:], logits[:], rstd[:].unsqueeze(2).to_broadcast([P, TILES, EXPERTS]),
                            ALU.mult).then_inc(lg_made, 1)
            dve.wait_ge(lg_made, 1)
            dve.wait_ge(tensor_step, read.next())
            v.tensor_copy(b1_cols[:], ps_second[:, 0, 0:EXPERTS * FBLK]).then_inc(b1_out, 1)
            dve.wait_ge(tensor_step, read.next())
            v.tensor_copy(lgT[:], ps_a[:, 0:2 * P]).then_inc(linked_step, 1)
            dve.wait_ge(linked_step, linked.next())
            v.tensor_reduce(abs_col[:], lgT[:], AX, ALU.max, apply_absolute_value=True).then_inc(vector_step, 1)
            dve.wait_ge(vector_step, sent.next())
            dve.wait_ge(tensor_step, read.next())
            v.tensor_reduce(abs_row[:], ps_pv[0:1, 0, 0:P], AX, ALU.max).then_inc(linked_step, 1)
            dve.wait_ge(linked_step, linked.next())
            v.tensor_scalar(bound[:].bitcast(I32), abs_row[:].bitcast(I32), 0x7F800000, None,
                            ALU.bitwise_and).then_inc(linked_step, 1)
            dve.wait_ge(linked_step, linked.next())
            v.tensor_scalar(bound[:], bound[:], 2.0, 2.0 ** -100, ALU.mult, ALU.max).then_inc(vector_step, 1)
            dve.wait_ge(vector_step, sent.next())
            dve.wait_ge(tensor_step, read.next())
            v.tensor_copy(bound_col[:], ps_a[:, 0:1]).then_inc(linked_step, 1)
            dve.wait_ge(linked_step, linked.next())
            v.tensor_scalar(widths[:], quarters[:], bound_col[:, 0:1], None, ALU.mult).then_inc(linked_step, 1)
            dve.wait_ge(linked_step, linked.next())
            v.tensor_scalar(thr[:], widths[:, 0], bound_col[:, 0:1], None, ALU.subtract).then_inc(linked_step, 1)
            dve.wait_ge(linked_step, linked.next())
            for n in range(SEARCH_STEPS):
                for j in range(3):
                    v.tensor_scalar(hits[:, j], lgT[:], thr[:, j + 1:j + 2], None, ALU.is_ge, ALU.add,
                                    accum_out=counts[:, j:j + 1]).then_inc(counted, 1)
                v.tensor_scalar(next_thr[:], widths[:, n + 1], thr[:, 0:1], None, ALU.add)
                dve.wait_ge(totalled, n + 1)
                v.tensor_scalar(above[:], ps_pv[:, 0, 0:3], CAPACITY - 0.5, None, ALU.is_ge, ALU.add,
                                accum_out=n_above[:]).then_inc(linked_step, 1)
                dve.wait_ge(linked_step, linked.next())
                v.scalar_tensor_tensor(out=thr[:], in0=widths[:, n, 1:2].to_broadcast([P, 4]), scalar=n_above[:, 0:1],
                                       in1=next_thr[:], op0=ALU.mult, op1=ALU.add).then_inc(linked_step, 1)
                dve.wait_ge(linked_step, linked.next())

            v.scalar_tensor_tensor(out=hi_col[:], in0=widths[:, SEARCH_STEPS, 1:2], scalar=4.0, in1=thr[:, 0:1],
                                   op0=ALU.mult, op1=ALU.add).then_inc(linked_step, 1)
            dve.wait_ge(linked_step, linked.next())
            v.tensor_scalar(lo_hi[:, 0], ident[:, 0:EXPERTS], thr[:, 0:1], None, ALU.mult).then_inc(linked_step, 1)
            dve.wait_ge(linked_step, linked.next())
            v.tensor_scalar(lo_hi[:, 1], ident[:, 0:EXPERTS], hi_col[:, 0:1], None, ALU.mult).then_inc(vector_step, 1)
            dve.wait_ge(vector_step, sent.next())
            dve.wait_ge(tensor_step, read.next())
            v.tensor_copy(bounds[:].rearrange("p a e -> p (a e)"), ps_a[:, 0:2 * EXPERTS]).then_inc(linked_step, 1)
            dve.wait_ge(linked_step, linked.next())
            wide = [P, TILES, EXPERTS]
            v.tensor_tensor(gt[:], lg[:], bounds[:, 1].unsqueeze(1).to_broadcast(wide), ALU.is_ge).then_inc(linked_step, 1)
            dve.wait_ge(linked_step, linked.next())
            with nc.allow_low_precision("counts up to 32 are exact in bfloat16"):
                v.tensor_reduce(gt_sum[:], gt[:].rearrange("p t e -> p e t"), AX, ALU.add).then_inc(vector_step, 1)
                dve.wait_ge(vector_step, sent.next())
            v.tensor_tensor(ge[:], lg[:], bounds[:, 0].unsqueeze(1).to_broadcast(wide), ALU.is_ge).then_inc(linked_step, 1)
            dve.wait_ge(linked_step, linked.next())
            dve.wait_ge(tensor_step, read.next())
            v.tensor_copy(gt_all[:], ps_pv[:, 0, 0:EXPERTS]).then_inc(linked_step, 1)
            dve.wait_ge(linked_step, linked.next())
            v.tensor_tensor(tie[:], ge[:], gt[:], ALU.subtract).then_inc(vector_step, 1)
            dve.wait_ge(vector_step, sent.next())
            dve.wait_ge(tensor_step, read.next())
            v.tensor_copy(tile_sum[:, 0], ps_pv[:, 1, 0:2]).then_inc(vector_step, 1)
            dve.wait_ge(vector_step, sent.next())
            dve.wait_ge(tensor_step, read.next())
            ranks = ps_a[:, 0:NPART].rearrange("p (t e) -> p t e", e=EXPERTS)
            v.tensor_tensor(rank[:], ranks, gt_all[:].unsqueeze(1).to_broadcast(wide), ALU.add).then_inc(linked_step, 1)
            dve.wait_ge(linked_step, linked.next())
            v.scalar_tensor_tensor(out=ge[:], in0=rank[:], scalar=CAPACITY - 0.5, in1=tie[:],
                                   op0=ALU.is_lt, op1=ALU.mult).then_inc(linked_step, 1)
            dve.wait_ge(linked_step, linked.next())
            v.tensor_tensor(sel[:], gt[:], ge[:], ALU.add).then_inc(vector_step, 1)
            dve.wait_ge(vector_step, sent.next())
            v.tensor_scalar(off_slot[:], sel[:].rearrange("p t e -> p (t e)"), float(TOKENS), -float(TOKENS),
                            ALU.mult, ALU.add).then_inc(linked_step, 1)
            dve.wait_ge(linked_step, linked.next())
            dve.wait_ge(tensor_step, read.next())
            v.tensor_copy(tile_sum[:, 1], ps_pv[:, 1, 0:2]).then_inc(vector_step, 1)
            dve.wait_ge(vector_step, sent.next())
            dve.wait_ge(tensor_step, read.next())
            v.tensor_tensor(slot[:], ps_a[:, 0:NPART], off_slot[:], ALU.add).then_inc(linked_step, 1)
            dve.wait_ge(linked_step, linked.next())
            for group, (first, n) in enumerate(GROUPS):
                these = slot[:].rearrange("p (t e) -> p t e", e=EXPERTS)[:, :, first:first + n]
                v.tensor_scalar(slot_a[group][:], these, 5, None, ALU.arith_shift_right).then_inc(linked_step, 1)
                dve.wait_ge(linked_step, linked.next())
                v.tensor_scalar(slot_b[group][:], these, 31, None, ALU.bitwise_and).then_inc(linked_step, 1)
                dve.wait_ge(linked_step, linked.next())

            def one_hot(group, part):
                ts = slice(part * HOT_TILES[group], (part + 1) * HOT_TILES[group])
                shape = [P, HOT_TILES[group] * GROUPS[group][1], 32]
                for hot, bits, done in ((hot_b, slot_b, hot_b_made), (hot_a, slot_a, hot_a_made)):
                    v.tensor_tensor(hot[group][:, ts].rearrange("p t e s -> p (t e) s"),
                                    iota32[:].unsqueeze(1).to_broadcast(shape),
                                    bits[group][:, ts].rearrange("p t e -> p (t e)").unsqueeze(2).to_broadcast(shape),
                                    ALU.is_equal).then_inc(done, 1)

            def pick(group):
                dve.wait_ge(tensor_step, read.next())
                for first, n in BLOCKS[group]:
                    for e in range(n):
                        rows_e = slice(32 * e, 32 * e + 32)
                        ins = v.tensor_copy(picked[rows_e, first // 3], product_of(first, n)[rows_e, rows_e])
                ins.then_inc(vector_step, 1)
                dve.wait_ge(vector_step, sent.next())

            def number(group):
                first, n = GROUPS[group]
                dve.wait_ge(tensor_step, read.next())
                v.tensor_scalar(index[:, first:first + n].rearrange("p e c -> p (e c)"),
                                ps_a[:, CHUNKS * first:CHUNKS * (first + n)], float(ID_BASE), None,
                                ALU.add).then_inc(found, 1)

            def copy_turned(n, blk):
                dve.wait_ge(turned, 4 * n + blk + 1)
                hi, lo_ = taken_hi[blk % 2], taken_lo[blk % 2]
                v.tensor_copy(hi[:], ps_turn).then_inc(taken_hi_made, 1)
                dve.wait_ge(taken_hi_made, 4 * n + blk + 1)
                v.tensor_tensor(lo_[:], ps_turn, hi[:].bitcast(F32), ALU.subtract).then_inc(turned_copied, 1)
                if blk % 2:
                    side = blk // 2
                    e = 2 * n + side
                    if not (type(n) is int and n == 0):
                        dve.wait_ge(y_made, 8 * (e - 2) + 8)
                    v.tensor_copy(gates[:, side].unsqueeze(2), taken[:, side, :, bass.ds(D + e, 1)]).then_inc(gates_kept, 1)
                    if type(n) is int and n == 0 and blk == 1:
                        dve.wait_ge(found, 2)
                    v.tensor_copy(from_index[:, side].unsqueeze(1), index[:, bass.ds(e + 2, 1)]).then_inc(from_set, 1)

            dve.wait_ge(k_stored, 16 * TERMS * PAIRS)
            dve.wait_ge(q_stored, 16 * TERMS * PAIRS)
            for part in range(HOT_PARTS[0]):
                one_hot(0, part)
            one_hot(1, 0)
            pick(0)
            one_hot(1, 1)
            number(0)
            dve.wait_ge(found, 1)
            v.tensor_copy(from_index[:], index[:, 0:2]).then_inc(from_set, 1)
            for part in range(2, HOT_PARTS[1]):
                one_hot(1, part)
                if (1, part) == EARLY_TURN:
                    copy_turned(0, 0)
            pick(1)
            number(1)
            copy_turned(0, 1)

            def scales(q):
                part = slice(QT * q, QT * (q + 1))
                dve.wait_ge(f_rooted, q + 1)
                v.reciprocal(f_rstd[:, part], f_sd[:, part]).then_inc(f_inverted, 1)
                dve.wait_ge(f_inverted, q + 1)
                v.scalar_tensor_tensor(out=f_bias[:, part].unsqueeze(2), in0=f_mv[:, part, 0:1], scalar=-1.0,
                                       in1=f_rstd[:, part].unsqueeze(2), op0=ALU.mult, op1=ALU.mult).then_inc(f_biased, 1)
                for t in range(QT * (q + 1) - BY_DVE, QT * (q + 1)):
                    v.tensor_scalar(xc_all[:, t], xc_all[:, t], f_mv[:, t, 0:1], f_rstd[:, t:t + 1], ALU.subtract,
                                    ALU.mult).then_inc(f_done_too, 1)

            def add_bias(n, blk):
                e = 2 * n + blk // 2
                dve.wait_ge(down_full, 4 * n + blk + 1)
                b2_rows = b2_all[:, bass.ds(e, 1)].to_broadcast([P, 4, D])
                v.tensor_tensor(y_sum[:, blk % 2], ps_second[:, blk % 2].rearrange("p (c d) -> p c d", c=4), b2_rows,
                                ALU.add).then_inc(y_summed, 1)

            def gate(n, blk):
                side, hb = divmod(blk, 2)
                e = 2 * n + side
                dve.wait_ge(y_summed, 4 * n + blk + 1)
                dve.wait_ge(gates_kept, e + 1)
                if hb == 0:
                    if not (type(n) is int and n == 0):
                        dve.wait_ge(added[side], 16 * CHUNKS * n)
                    v.tensor_copy(to_index[:, side].unsqueeze(1), index[:, bass.ds(e, 1)]).then_inc(to_set, 1)
                for c in range(4):
                    ch = 4 * hb + c
                    v.tensor_scalar(y_out[:, side, ch], y_sum[:, blk % 2, c], gates[:, side, ch:ch + 1],
                                    None, ALU.mult).then_inc(y_made, 1)

            def add_up(n, blk):
                add_bias(n, blk)
                gate(n, blk)

            def two_experts(n, begin, last=False):
                for blk in range(4):
                    if not begin or blk > 1:
                        copy_turned(n, blk)
                    if blk > 1:
                        add_up(n, blk - 2)
                    elif not begin:
                        add_up(n - 1, blk + 2)
                    if blk == 1:
                        cut_w1(n, 1)
                    elif blk == 3 and not last:
                        cut_w1(n + 1, 0)

            two_experts(0, True)
            with dve.Fori(1, EXPERTS // 2 - 1) as n:
                two_experts(n, False)
            two_experts(EXPERTS // 2 - 1, False, last=True)
            add_up(EXPERTS // 2 - 1, 2)
            add_up(EXPERTS // 2 - 1, 3)

            for q in range(4):
                dve.wait_ge(f_in[q], 16)
                for t in range(QT * q, QT * (q + 1)):
                    v.bn_stats(f_stats[:, t], xc_all[:, t]).then_inc(f_statted, 1)
                dve.wait_ge(f_statted, QT * (q + 1))
                for t in range(QT * q, QT * (q + 1)):
                    v.bn_aggr(f_mv[:, t], f_stats[:, t]).then_inc(f_averaged, 1)
                if q:
                    scales(q - 1)
            scales(3)


_INS = ['L0_attn_x', 'L0_attn_Wq', 'L0_attn_bq', 'L0_attn_Wl', 'L0_attn_bl', 'L0_attn_Wk', 'L0_attn_bk',
        'L0_attn_Wv', 'L0_attn_bv', 'L0_attn_Wo', 'L0_attn_bo', 'L0_ffn_Wg', 'L0_ffn_W1', 'L0_ffn_b1',
        'L0_ffn_W2', 'L0_ffn_b2']


def kernel(**inputs):
    import numpy as _np
    import concourse.bacc as _bacc
    from concourse import mybir as _mybir
    from concourse.bass_utils import run_bass_kernel_spmd as _run

    nc = _bacc.Bacc("TRN2", target_bir_lowering=False, num_devices=1)
    arrays, args = {}, []
    for name in _INS:
        a = _np.ascontiguousarray(inputs[name])
        arrays[f"in_{name}"] = a
        args.append(nc.dram_tensor(f"in_{name}", a.shape, _mybir.dt.from_np(a.dtype), kind="ExternalInput").ap())
    out = nc.dram_tensor("out", (BATCHES, SEQ, D), F32, kind="ExternalOutput").ap()
    post_ln_layer(nc, *args, out)
    return _run(nc, [arrays], core_ids=[0]).results[0]["out"]
```
